# Optimizing a Trainium2 kernel written in Bass

```python
import numpy as np
import jax
import jax.numpy as jnp

def _softmax(x, axis=-1):
    return jax.nn.softmax(x, axis=axis)

def _gelu(x):
    return jax.nn.gelu(x, approximate=True)

def _silu(x):
    return jax.nn.silu(x)

def _sigmoid(x):
    return jax.nn.sigmoid(x)

def _layernorm(x, axis=-1, eps=1e-05):
    m = jnp.mean(x, axis=axis, keepdims=True)
    v = jnp.var(x, axis=axis, keepdims=True)
    return (x - m) / jnp.sqrt(v + eps)

def _scatter_add(tgt, idx, src, axis=0):
    return tgt.at[idx].add(src)

def _segment_sum(src, seg, n):
    return jax.ops.segment_sum(src, seg, n)
kernel_name = 'mk_xattn_ffn_d2_seqx_r8_8654d5'

def setup_inputs(seed: int=0):
    np.random.seed(seed)
    _w = jnp.asarray

    def _rec_inputs():
        import jax
        import jax.numpy as jnp
        _rk = jax.random.key(seed)
        x = 0.0001212 + 1 * jax.random.normal(jax.random.fold_in(_rk, 1), (32, 64, 256), jnp.float32)
        _lenS = 64 - jax.random.randint(jax.random.fold_in(_rk, 7), (32,), 0, max(1, 64 // 4) + 1, jnp.int32)
        _lenS2 = 64 - jax.random.randint(jax.random.fold_in(_rk, 8), (32,), 0, max(1, 64 // 4) + 1, jnp.int32)
        _ctx_2048P = jax.random.normal(jax.random.fold_in(_rk, 11), (32, 16, 256), jnp.float32)
        _ctx_2048c = jax.random.dirichlet(jax.random.fold_in(_rk, 511), 0.3 * jnp.ones((16,), jnp.float32), (32, 64))
        _ctx_2048t = jnp.einsum('bsk,bkd->bsd', _ctx_2048c, _ctx_2048P)
        _ctx_2048t = _ctx_2048t * jax.lax.rsqrt(jnp.mean(jnp.square(_ctx_2048t)) + 1e-12) * 0.953939
        ctx_2048 = 0.000173663 + 1.0001 * (_ctx_2048t + 0.3 * jax.random.normal(jax.random.fold_in(_rk, 611), (32, 64, 256), jnp.float32))
        return (x, ctx_2048)
    x, ctx_2048 = _rec_inputs()

    def _L0_xattn_setup():
        import jax, jax.numpy as jnp
        import numpy as np
        B_DIM, T_DIM, C_DIM = (16, 128, 256)

        def _wkv(w, u, k, v):
            Bn, Tn, Cn = k.shape
            NEG_INF = jnp.float32(-1e+38)

            def step(carry, kv_t):
                p, q, o = carry
                kt, vt = kv_t
                no = jnp.maximum(o, u + kt)
                A = jnp.exp(o - no)
                E = jnp.exp(u + kt - no)
                y = (A * p + E * vt) / (A * q + E)
                no2 = jnp.maximum(w + o, kt)
                A2 = jnp.exp(w + o - no2)
                E2 = jnp.exp(kt - no2)
                return ((A2 * p + E2 * vt, A2 * q + E2, no2), y)
            init = (jnp.zeros((Bn, Cn), k.dtype), jnp.zeros((Bn, Cn), k.dtype), jnp.full((Bn, Cn), NEG_INF, k.dtype))
            kT = jnp.moveaxis(k, 1, 0)
            vT = jnp.moveaxis(v, 1, 0)
            _, yT = jax.lax.scan(step, init, (kT, vT))
            return jnp.moveaxis(yT, 0, 1)
        key = jax.random.key(seed)
        k1, k2, k3, k4 = jax.random.split(key, 4)
        w = -jnp.exp(jax.random.normal(k1, (C_DIM,), jnp.float32))
        u = jax.random.normal(k2, (C_DIM,), jnp.float32)
        k = jax.random.normal(k3, (B_DIM, T_DIM, C_DIM), jnp.float32)
        v = jax.random.normal(k4, (B_DIM, T_DIM, C_DIM), jnp.float32)
        return {'B': B_DIM, 'T': T_DIM, 'C': C_DIM, 'w': w, 'u': u, 'k': k, 'v': v}
    _L0_xattn_all = _L0_xattn_setup()
    _L0_xattn_in = {k: v for k, v in _L0_xattn_all.items() if k in ('w', 'u')}
    del _L0_xattn_all

    def _L0_ffn_setup():
        import jax, jax.numpy as jnp
        import numpy as np
        EPS = 1e-05

        def act_quant(x):
            scale = 127.0 / jnp.clip(jnp.max(jnp.abs(x), axis=-1, keepdims=True), EPS)
            return jnp.clip(jnp.round(x * scale), -128.0, 127.0) / scale

        def weight_quant(w):
            scale = 1.0 / jnp.clip(jnp.mean(jnp.abs(w)), EPS)
            return jnp.clip(jnp.round(w * scale), -1.0, 1.0) / scale

        def bitlinear(x, w):
            return jnp.einsum('bsd,hd->bsh', act_quant(x), weight_quant(w))
        key = jax.random.key(seed)
        k0, k1, k2, k3 = jax.random.split(key, 4)
        d_model, hidden_dim = (256, 704)
        B, S = (4, 256)
        x = jax.random.normal(k0, (B, S, d_model), dtype=jnp.float32)
        std = 0.02
        w1 = jax.random.normal(k1, (hidden_dim, d_model), dtype=jnp.float32) * std
        w2 = jax.random.normal(k2, (d_model, hidden_dim), dtype=jnp.float32) * std
        w3 = jax.random.normal(k3, (hidden_dim, d_model), dtype=jnp.float32) * std
        return {'x': x, 'w1': w1, 'w2': w2, 'w3': w3}
    _L0_ffn_all = _L0_ffn_setup()
    _L0_ffn_in = {k: v for k, v in _L0_ffn_all.items() if k in ('w1', 'w2', 'w3')}
    del _L0_ffn_all

    def _L1_xattn_setup():
        import jax, jax.numpy as jnp
        import numpy as np
        FP8_MAX = 448.0
        EPS = 1e-05

        def _fp8_roundtrip(x):
            return x.astype(jnp.float8_e4m3fn).astype(jnp.float32)

        def _div_clamp_fp8(x, scale):
            y = jnp.clip(x.astype(jnp.float32) / scale, -FP8_MAX, FP8_MAX)
            y = y.astype(jnp.bfloat16).astype(jnp.float32)
            return _fp8_roundtrip(y)

        def _ln(x, w, b):
            mu = jnp.mean(x, axis=-1, keepdims=True)
            var = jnp.mean(jnp.square(x - mu), axis=-1, keepdims=True)
            return (x - mu) * jax.lax.rsqrt(var + EPS) * w + b

        def _fp8_linear_pertensor(x, wq, w_scale, in_scale):
            xq = _div_clamp_fp8(x, in_scale)
            return jnp.einsum('bsi,oi->bso', xq * in_scale, wq) * w_scale

        def _gqa(q, k, v):
            scale = 1.0 / np.sqrt(q.shape[-1])
            scores = jnp.einsum('bsghd,btgd->bghst', q, k) * scale
            p = jax.nn.softmax(scores, axis=-1)
            return jnp.einsum('bghst,btgd->bsghd', p, v)
        key = jax.random.key(seed)
        ks = jax.random.split(key, 8)
        B, S, SC, H, NH, G, D = (2, 256, 64, 256, 16, 8, 128)

        def qw(k, out_f, in_f):
            w = jax.random.normal(k, (out_f, in_f), jnp.float32) * 0.02
            sc = jnp.max(jnp.abs(w)) / FP8_MAX
            return (_fp8_roundtrip(w / sc), sc.astype(jnp.float32))
        wq, wq_s = qw(ks[0], NH * D, H)
        wqx, wqx_s = qw(ks[1], NH * D, H)
        wk, wk_s = qw(ks[2], G * D, H)
        wv, wv_s = qw(ks[3], G * D, H)
        wproj, wp_s = qw(ks[4], H, 2 * NH * D)
        return {'hidden_states': jax.random.normal(ks[5], (B, S, H), jnp.float32), 'cond': jax.random.normal(ks[6], (B, SC, H), jnp.float32), 'ln_w': jnp.ones((H,), jnp.float32), 'ln_b': jnp.zeros((H,), jnp.float32), 'wq': wq, 'wq_scale': wq_s, 'q_in_scale': jnp.full((H,), 0.05, jnp.float32), 'wqx': wqx, 'wqx_scale': wqx_s, 'qx_in_scale': jnp.full((H,), 0.05, jnp.float32), 'wk': wk, 'wk_scale': wk_s, 'k_in_scale': jnp.full((H,), 0.05, jnp.float32), 'wv': wv, 'wv_scale': wv_s, 'v_in_scale': jnp.full((H,), 0.05, jnp.float32), 'w_kv_x': jax.random.normal(ks[7], (2 * G * D, H), jnp.float32) * 0.02, 'qln_w': jnp.ones((D,), jnp.float32), 'qln_b': jnp.zeros((D,), jnp.float32), 'kln_w': jnp.ones((D,), jnp.float32), 'kln_b': jnp.zeros((D,), jnp.float32), 'qxln_w': jnp.ones((D,), jnp.float32), 'qxln_b': jnp.zeros((D,), jnp.float32), 'kxln_w': jnp.ones((D,), jnp.float32), 'kxln_b': jnp.zeros((D,), jnp.float32), 'wproj': wproj, 'proj_w_scale': wp_s, 'proj_in_scale': jnp.asarray(0.05, jnp.float32), 'proj_smooth': jnp.full((2 * NH * D,), 0.05, jnp.float32)}
    _L1_xattn_all = _L1_xattn_setup()
    _L1_xattn_in = {k: v for k, v in _L1_xattn_all.items() if k in ('ln_w', 'ln_b', 'wq', 'wq_scale', 'q_in_scale', 'wqx', 'wqx_scale', 'qx_in_scale', 'wk', 'wk_scale', 'k_in_scale', 'wv', 'wv_scale', 'v_in_scale', 'w_kv_x', 'qln_w', 'qln_b', 'kln_w', 'kln_b', 'qxln_w', 'qxln_b', 'kxln_w', 'kxln_b', 'wproj', 'proj_w_scale', 'proj_in_scale', 'proj_smooth')}
    del _L1_xattn_all

    def _L1_ffn_setup():
        import jax, jax.numpy as jnp
        import numpy as np
        E = 8
        K = 2
        CAP = 64
        H = 256
        F = 1024
        key = jax.random.key(seed)
        ks = jax.random.split(key, 6)
        inp = {'hidden_states': jax.random.normal(ks[0], (2, 128, H), jnp.float32), 'router_w': jax.random.normal(ks[1], (E, H), jnp.float32) * (0.01 / np.sqrt(H)), 'w1': jax.random.normal(ks[2], (F, H), jnp.float32) * (1.0 / np.sqrt(H)), 'b1': jax.random.normal(ks[3], (F,), jnp.float32) * 0.01, 'w2': jax.random.normal(ks[4], (H, F), jnp.float32) * (1.0 / np.sqrt(F)), 'b2': jax.random.normal(ks[5], (H,), jnp.float32) * 0.01}
        return inp
    _L1_ffn_all = _L1_ffn_setup()
    _L1_ffn_in = {k: v for k, v in _L1_ffn_all.items() if k in ('router_w', 'w1', 'b1', 'w2', 'b2')}
    del _L1_ffn_all
    return {'x': x, 'ctx_2048': ctx_2048, 'L0_xattn_w': _L0_xattn_in['w'], 'L0_xattn_u': _L0_xattn_in['u'], 'L0_ffn_w1': _L0_ffn_in['w1'], 'L0_ffn_w2': _L0_ffn_in['w2'], 'L0_ffn_w3': _L0_ffn_in['w3'], 'L1_xattn_ln_w': _L1_xattn_in['ln_w'], 'L1_xattn_ln_b': _L1_xattn_in['ln_b'], 'L1_xattn_wq': _L1_xattn_in['wq'], 'L1_xattn_wq_scale': _L1_xattn_in['wq_scale'], 'L1_xattn_q_in_scale': _L1_xattn_in['q_in_scale'], 'L1_xattn_wqx': _L1_xattn_in['wqx'], 'L1_xattn_wqx_scale': _L1_xattn_in['wqx_scale'], 'L1_xattn_qx_in_scale': _L1_xattn_in['qx_in_scale'], 'L1_xattn_wk': _L1_xattn_in['wk'], 'L1_xattn_wk_scale': _L1_xattn_in['wk_scale'], 'L1_xattn_k_in_scale': _L1_xattn_in['k_in_scale'], 'L1_xattn_wv': _L1_xattn_in['wv'], 'L1_xattn_wv_scale': _L1_xattn_in['wv_scale'], 'L1_xattn_v_in_scale': _L1_xattn_in['v_in_scale'], 'L1_xattn_w_kv_x': _L1_xattn_in['w_kv_x'], 'L1_xattn_qln_w': _L1_xattn_in['qln_w'], 'L1_xattn_qln_b': _L1_xattn_in['qln_b'], 'L1_xattn_kln_w': _L1_xattn_in['kln_w'], 'L1_xattn_kln_b': _L1_xattn_in['kln_b'], 'L1_xattn_qxln_w': _L1_xattn_in['qxln_w'], 'L1_xattn_qxln_b': _L1_xattn_in['qxln_b'], 'L1_xattn_kxln_w': _L1_xattn_in['kxln_w'], 'L1_xattn_kxln_b': _L1_xattn_in['kxln_b'], 'L1_xattn_wproj': _L1_xattn_in['wproj'], 'L1_xattn_proj_w_scale': _L1_xattn_in['proj_w_scale'], 'L1_xattn_proj_in_scale': _L1_xattn_in['proj_in_scale'], 'L1_xattn_proj_smooth': _L1_xattn_in['proj_smooth'], 'L1_ffn_router_w': _L1_ffn_in['router_w'], 'L1_ffn_w1': _L1_ffn_in['w1'], 'L1_ffn_b1': _L1_ffn_in['b1'], 'L1_ffn_w2': _L1_ffn_in['w2'], 'L1_ffn_b2': _L1_ffn_in['b2']}

def reference(x, ctx_2048, L0_xattn_w, L0_xattn_u, L0_ffn_w1, L0_ffn_w2, L0_ffn_w3, L1_xattn_ln_w, L1_xattn_ln_b, L1_xattn_wq, L1_xattn_wq_scale, L1_xattn_q_in_scale, L1_xattn_wqx, L1_xattn_wqx_scale, L1_xattn_qx_in_scale, L1_xattn_wk, L1_xattn_wk_scale, L1_xattn_k_in_scale, L1_xattn_wv, L1_xattn_wv_scale, L1_xattn_v_in_scale, L1_xattn_w_kv_x, L1_xattn_qln_w, L1_xattn_qln_b, L1_xattn_kln_w, L1_xattn_kln_b, L1_xattn_qxln_w, L1_xattn_qxln_b, L1_xattn_kxln_w, L1_xattn_kxln_b, L1_xattn_wproj, L1_xattn_proj_w_scale, L1_xattn_proj_in_scale, L1_xattn_proj_smooth, L1_ffn_router_w, L1_ffn_w1, L1_ffn_b1, L1_ffn_w2, L1_ffn_b2):
    import jax
    import jax.numpy as jnp

    def _L0_xattn_ref(B, T, C, w, u, k, v):
        import jax, jax.numpy as jnp
        import numpy as np
        B_DIM, T_DIM, C_DIM = (16, 128, 256)

        def _wkv(w, u, k, v):
            Bn, Tn, Cn = k.shape
            NEG_INF = jnp.float32(-1e+38)

            def step(carry, kv_t):
                p, q, o = carry
                kt, vt = kv_t
                no = jnp.maximum(o, u + kt)
                A = jnp.exp(o - no)
                E = jnp.exp(u + kt - no)
                y = (A * p + E * vt) / (A * q + E)
                no2 = jnp.maximum(w + o, kt)
                A2 = jnp.exp(w + o - no2)
                E2 = jnp.exp(kt - no2)
                return ((A2 * p + E2 * vt, A2 * q + E2, no2), y)
            init = (jnp.zeros((Bn, Cn), k.dtype), jnp.zeros((Bn, Cn), k.dtype), jnp.full((Bn, Cn), NEG_INF, k.dtype))
            kT = jnp.moveaxis(k, 1, 0)
            vT = jnp.moveaxis(v, 1, 0)
            _, yT = jax.lax.scan(step, init, (kT, vT))
            return jnp.moveaxis(yT, 0, 1)
        return _wkv(w, u, k, v)

    def _L0_ffn_ref(x, w1, w2, w3):
        import jax, jax.numpy as jnp
        import numpy as np
        EPS = 1e-05

        def act_quant(x):
            scale = 127.0 / jnp.clip(jnp.max(jnp.abs(x), axis=-1, keepdims=True), EPS)
            return jnp.clip(jnp.round(x * scale), -128.0, 127.0) / scale

        def weight_quant(w):
            scale = 1.0 / jnp.clip(jnp.mean(jnp.abs(w)), EPS)
            return jnp.clip(jnp.round(w * scale), -1.0, 1.0) / scale

        def bitlinear(x, w):
            return jnp.einsum('bsd,hd->bsh', act_quant(x), weight_quant(w))
        h = jax.nn.silu(bitlinear(x, w1)) * bitlinear(x, w3)
        return bitlinear(h, w2)

    def _L1_xattn_ref(hidden_states, cond, ln_w, ln_b, wq, wq_scale, q_in_scale, wqx, wqx_scale, qx_in_scale, wk, wk_scale, k_in_scale, wv, wv_scale, v_in_scale, w_kv_x, qln_w, qln_b, kln_w, kln_b, qxln_w, qxln_b, kxln_w, kxln_b, wproj, proj_w_scale, proj_in_scale, proj_smooth):
        import jax, jax.numpy as jnp
        import numpy as np
        FP8_MAX = 448.0
        EPS = 1e-05

        def _fp8_roundtrip(x):
            return x.astype(jnp.float8_e4m3fn).astype(jnp.float32)

        def _div_clamp_fp8(x, scale):
            y = jnp.clip(x.astype(jnp.float32) / scale, -FP8_MAX, FP8_MAX)
            y = y.astype(jnp.bfloat16).astype(jnp.float32)
            return _fp8_roundtrip(y)

        def _ln(x, w, b):
            mu = jnp.mean(x, axis=-1, keepdims=True)
            var = jnp.mean(jnp.square(x - mu), axis=-1, keepdims=True)
            return (x - mu) * jax.lax.rsqrt(var + EPS) * w + b

        def _fp8_linear_pertensor(x, wq, w_scale, in_scale):
            xq = _div_clamp_fp8(x, in_scale)
            return jnp.einsum('bsi,oi->bso', xq * in_scale, wq) * w_scale

        def _gqa(q, k, v):
            scale = 1.0 / np.sqrt(q.shape[-1])
            scores = jnp.einsum('bsghd,btgd->bghst', q, k) * scale
            p = jax.nn.softmax(scores, axis=-1)
            return jnp.einsum('bghst,btgd->bsghd', p, v)
        b, s, _ = hidden_states.shape
        sc = cond.shape[1]
        d = qln_w.shape[0]
        nh = wq.shape[0] // d
        g = wk.shape[0] // d
        hpg = nh // g
        ln_out = _ln(hidden_states, ln_w, ln_b)
        q = _fp8_linear_pertensor(ln_out, wq, wq_scale, q_in_scale).reshape(b, s, g, hpg, d)
        q = _ln(q, qln_w, qln_b)
        k = _fp8_linear_pertensor(ln_out, wk, wk_scale, k_in_scale).reshape(b, s, g, d)
        k = _ln(k, kln_w, kln_b)
        v = _fp8_linear_pertensor(ln_out, wv, wv_scale, v_in_scale).reshape(b, s, g, d)
        core = _gqa(q, k, v).reshape(b, s, nh * d)
        qx = _fp8_linear_pertensor(ln_out, wqx, wqx_scale, qx_in_scale).reshape(b, s, g, hpg, d)
        qx = _ln(qx, qxln_w, qxln_b)
        kvx = jnp.einsum('bsi,oi->bso', cond, w_kv_x)
        kx, vx = jnp.split(kvx, 2, axis=-1)
        kx = _ln(kx.reshape(b, sc, g, d), kxln_w, kxln_b)
        vx = vx.reshape(b, sc, g, d)
        xout = _gqa(qx, kx, vx).reshape(b, s, nh * d)
        cat = jnp.concatenate([core, xout], axis=-1)
        catq = _div_clamp_fp8(cat, proj_smooth)
        return jnp.einsum('bsi,oi->bso', catq, wproj) * (proj_in_scale * proj_w_scale)

    def _L1_ffn_ref(hidden_states, router_w, w1, b1, w2, b2):
        import jax, jax.numpy as jnp
        import numpy as np
        E = 8
        K = 2
        CAP = 64
        H = 256
        F = 1024
        orig_shape = hidden_states.shape
        x = hidden_states.reshape(-1, H)
        N = x.shape[0]
        logits = x @ router_w.T
        probs = jax.nn.softmax(logits, axis=-1)
        top_p, top_i = jax.lax.top_k(probs, K)
        expert_flat = top_i.T.reshape(-1)
        probs_flat = top_p.T.reshape(-1)
        token_idx = jnp.tile(jnp.arange(N), K)
        onehot = (expert_flat[:, None] == jnp.arange(E)[None, :]).astype(jnp.int32)
        pos = jnp.take_along_axis(jnp.cumsum(onehot, axis=0), expert_flat[:, None], axis=1)[:, 0] - 1
        keep = pos < CAP
        dest = expert_flat * CAP + pos
        dest_m = jnp.where(keep, dest, E * CAP)
        buf = jnp.zeros((E * CAP, H), x.dtype).at[dest_m].set(x[token_idx], mode='drop')
        h = jax.nn.gelu(buf @ w1.T + b1, approximate=False) @ w2.T + b2
        gathered = jnp.where(keep[:, None], h[jnp.where(keep, dest, 0)], 0.0) * probs_flat[:, None]
        out = jnp.zeros_like(x).at[token_idx].add(gathered)
        return out.reshape(orig_shape)
    x = x + _L0_xattn_ref(32, 64, 256, L0_xattn_w, L0_xattn_u, _layernorm(x, axis=-1), ctx_2048)
    x = x + _L0_ffn_ref(_layernorm(x, axis=-1), L0_ffn_w1, L0_ffn_w2, L0_ffn_w3)
    x = x + _L1_xattn_ref(_layernorm(x, axis=-1), ctx_2048, L1_xattn_ln_w, L1_xattn_ln_b, L1_xattn_wq, L1_xattn_wq_scale, L1_xattn_q_in_scale, L1_xattn_wqx, L1_xattn_wqx_scale, L1_xattn_qx_in_scale, L1_xattn_wk, L1_xattn_wk_scale, L1_xattn_k_in_scale, L1_xattn_wv, L1_xattn_wv_scale, L1_xattn_v_in_scale, L1_xattn_w_kv_x, L1_xattn_qln_w, L1_xattn_qln_b, L1_xattn_kln_w, L1_xattn_kln_b, L1_xattn_qxln_w, L1_xattn_qxln_b, L1_xattn_kxln_w, L1_xattn_kxln_b, L1_xattn_wproj, L1_xattn_proj_w_scale, L1_xattn_proj_in_scale, L1_xattn_proj_smooth)
    x = x + _L1_ffn_ref(_layernorm(x, axis=-1), L1_ffn_router_w, L1_ffn_w1, L1_ffn_b1, L1_ffn_w2, L1_ffn_b2)
    return x

_drawn_inputs = setup_inputs


def setup_inputs(seed=0):
    import zlib

    import numpy as np

    out = dict(_drawn_inputs(seed))
    spreads = {'L1_xattn_ln_w': (1.0, 0.6),
     'L1_xattn_ln_b': (0.0, 0.909),
     'L1_xattn_q_in_scale': (0.05000000074505806, 0.6),
     'L1_xattn_qx_in_scale': (0.05000000074505806, 0.6),
     'L1_xattn_k_in_scale': (0.05000000074505806, 0.6),
     'L1_xattn_v_in_scale': (0.05000000074505806, 0.6),
     'L1_xattn_qln_w': (1.0, 0.6),
     'L1_xattn_qln_b': (0.0, 2.0),
     'L1_xattn_kln_w': (1.0, 0.6),
     'L1_xattn_kln_b': (0.0, 2.0),
     'L1_xattn_qxln_w': (1.0, 0.6),
     'L1_xattn_qxln_b': (0.0, 2.0),
     'L1_xattn_kxln_w': (1.0, 0.6),
     'L1_xattn_kxln_b': (0.0, 2.0),
     'L1_xattn_proj_smooth': (0.05000000074505806, 0.6)}
    factors = {'L0_ffn_w1': 7.332,
     'L0_ffn_w2': 6.878,
     'L0_ffn_w3': 6.864,
     'L1_ffn_router_w': 35.36,
     'L1_ffn_b1': 64.0,
     'L1_ffn_b2': 200.0,
     'L1_ffn_w1': 5.734,
     'L1_ffn_w2': 5.129}
    for name, (base, spread) in spreads.items():
        noise = np.random.default_rng([zlib.crc32(name.encode()), seed]).standard_normal(out[name].shape)
        drawn = base * np.exp(spread * noise) if base else spread * noise
        out[name] = jnp.asarray(drawn.astype(out[name].dtype))
    for name, factor in factors.items():
        out[name] = (out[name] * factor).astype(out[name].dtype)
    return out
```

```python
from contextlib import ExitStack

import concourse.bass as bass
from concourse import mybir

F32 = mybir.dt.float32
F32R = mybir.dt.float32r
BF16 = mybir.dt.bfloat16
U16 = mybir.dt.uint16
U32 = mybir.dt.uint32
ALU = mybir.AluOpType
ACT = mybir.ActivationFunctionType
AX = mybir.AxisListType

P = 128
B, S, C = 32, 64, 256
TOK = B * S
NT = TOK // P
KC = C // P
HID = 704
NH, G, D = 16, 8, 128
HPG = NH // G
E, CAP, FF = 8, 64, 1024
LN_EPS = 1e-5
QUANT_EPS = 1e-5
FP8_MAX = 448.0
ROUND32 = 1.5 * 2.0 ** 23
NEG_BIG = -1e38
LN_EXP_SET = "natural_log_exp_and_others"

PARAM_COLS = {}
for _name, _n in (("w", KC), ("u", KC), ("ln_w", KC), ("ln_b", KC), ("sq", KC), ("sk", KC), ("sv", KC),
                  ("sqx", KC), ("qln_w", 1), ("qln_b", 1), ("kln_w", 1), ("kln_b", 1), ("qxln_w", 1),
                  ("qxln_b", 1), ("kxln_w", 1), ("kxln_b", 1), ("smooth", 2 * NH), ("b1", FF // P),
                  ("wq_s", 1), ("wk_s", 1), ("wv_s", 1), ("wqx_s", 1), ("proj_in", 1), ("proj_w", 1)):
    PARAM_COLS[_name] = (sum(n for _, n in PARAM_COLS.values()), _n)
N_PARAM = sum(n for _, n in PARAM_COLS.values())


class Chain:

    def __init__(self, eng, sem):
        self.eng, self.sem, self.base, self.n = eng, sem, 0, 0

    def at(self, base):
        self.base, self.n = base, 0

    def mark(self, ins):
        ins.then_inc(self.sem, 1)
        self.n += 1

    def settle(self):
        self.eng.wait_ge(self.sem, self.base + self.n)

    def __call__(self, ins):
        self.mark(ins)
        self.settle()


def build_program(nc, x, ctxT, params, w1T, w3T, w2T, wqT, wkT, wvT, wqxT, wkvxT, wprojT, routerT,
                  fw1T, fw2T, fb2, out):
    ctx = ExitStack()
    with ctx:
        def sb(name, shape, dt=F32, stack=ctx):
            return stack.enter_context(nc.sbuf_tensor(name, shape, dt))

        def sem(name):
            return ctx.enter_context(nc.semaphore(name))

        x_res = sb("x_res", [P, NT, C])
        par = sb("par", [P, N_PARAM])
        ident = sb("ident", [P, P])
        ones = sb("ones", [P, P])
        stat6 = sb("stat6", [P, NT, 6])
        mean = sb("mean", [P, NT])
        var = sb("var", [P, NT])
        rstd = sb("rstd", [P, NT])
        st_a = sb("st_a", [P, NT])
        st_b = sb("st_b", [P, NT])
        st_c = sb("st_c", [P, NT])
        rs0 = sb("rs0", [P, NT])

        def col(name, i=0, n=1):
            at, _ = PARAM_COLS[name]
            return par[:, at + i:at + i + n]

        tok = dict(nc=nc, ctx=ctx, sb=sb, sem=sem, x_res=x_res, par=par, col=col, ident=ident, ones=ones,
                   stat6=stat6, mean=mean, var=var, rstd=rstd, st=(st_a, st_b, st_c), rs0=rs0)
        wkv_stage(tok, x, ctxT, params)
        ternary_ffn_stage(tok, w1T, w3T, w2T)
        with ExitStack() as held:
            xq8 = sb("xq8", [P, 4 * KC, TOK], BF16, held)
            ln_quant_stage(tok, xq8)
            attention_stage(tok, "self", xq8, (wqT, wkT, wvT), wprojT, ctxT)
            attention_stage(tok, "cross", xq8, (wqxT, wkvxT), wprojT, ctxT)
        routed_ffn_stage(tok, routerT, fw1T, fw2T, fb2, out)



def rsqrt_newton(dve_chain, nc, y, y0, v, t):
    dve_chain(nc.vector.scalar_tensor_tensor(t, y0, -0.5, y0, ALU.mult, ALU.mult))
    dve_chain(nc.vector.tensor_tensor(t, t, v, ALU.mult))
    dve_chain(nc.vector.scalar_tensor_tensor(y, t, 1.5, y0, ALU.add, ALU.mult))


def dve_mean_var(k, chain, var_ready):
    nc, st6, (a, b, c) = k["nc"], k["stat6"], k["st"]
    me, m2e, mo, m2o = (st6[:, :, i] for i in (1, 2, 4, 5))
    chain.mark(nc.vector.tensor_tensor(a[:], me, mo, ALU.subtract))
    chain.mark(nc.vector.tensor_tensor(b[:], m2e, m2o, ALU.add))
    chain(nc.vector.tensor_tensor(c[:], me, mo, ALU.add))
    chain.mark(nc.vector.tensor_tensor(a[:], a[:], a[:], ALU.mult))
    chain.mark(nc.vector.tensor_scalar(b[:], b[:], 1.0 / C, LN_EPS, ALU.mult, ALU.add))
    chain(nc.vector.tensor_scalar(k["mean"][:], c[:], 0.5, None, ALU.mult))
    nc.vector.scalar_tensor_tensor(k["var"][:], a[:], 0.25, b[:], ALU.mult, ALU.add).then_inc(var_ready, 1)


def act_rsqrt(act, nc, dst, v, tmp, var_ready, count, act_chain, rs_ready):
    act.wait_ge(var_ready, count)
    act_chain(nc.scalar.activation(tmp, v, ACT.Ln))
    nc.scalar.activation(dst, tmp, ACT.Exp, scale=-0.5).then_inc(rs_ready, 1)



def wkv_stage(k, x, ctxT, params):
    nc, sem, x_res, col, ident = k["nc"], k["sem"], k["x_res"], k["col"], k["ident"]
    BQ = B // 2
    L = S + 1
    CHUNKS = [(h, q) for h in range(KC) for q in range(2)]
    with ExitStack() as own:
        def sb(name, shape, dt=F32):
            return own.enter_context(nc.sbuf_tensor(name, shape, dt))

        def psum(name, shape, dt=F32):
            return own.enter_context(nc.psum_tensor(name, shape, dt))

        z = sb("wkv_z", [P, NT, C])
        vT = sb("vT", [P, KC, B, S])
        k65 = sb("k65", [P, KC, B, L])
        w65 = sb("w65", [P, KC, BQ, L])
        yT = sb("yT", [P, KC, B, S])
        names = "o A2 E2 E2v p q"
        buf = {n: [sb(f"{n}{i}", [P, BQ, L]) for i in range(2)] for n in names.split()}
        for n in "d A E Ev Ap Aq".split():
            buf[n] = [sb(f"{n}_{i}", [P, BQ, S]) for i in range(2)]
        zT_ps = [psum(f"zT_ps{i}", [P, 512]) for i in range(4)]
        y_ps = [psum(f"y_ps{i}", [P, 512]) for i in range(2)]

        x_in = [sem(f"x_in{i}") for i in range(4)]
        par_in, v_in = sem("par_in"), [sem(f"v_in{i}") for i in range(KC)]
        consts, fills = sem("consts"), sem("wkv_fills")
        var_ready, rs_ready = sem("wkv_var_ready"), sem("wkv_rs_ready")
        dve_done, act_done, pool_done = sem("wkv_dve_done"), sem("wkv_act_done"), sem("wkv_pool_done")
        z_ready, zT_ready, k_ready = sem("wkv_z_ready"), sem("wkv_zT_ready"), sem("wkv_k_ready")
        gaps_ready, exps_ready = sem("wkv_gaps_ready"), sem("wkv_exps_ready")
        E2v_ready, Ev_ready = sem("wkv_E2v_ready"), sem("wkv_Ev_ready")
        pq_ready, Apq_ready = sem("wkv_pq_ready"), sem("wkv_Apq_ready")
        den_ready, rcp_ready = sem("wkv_den_ready"), sem("wkv_rcp_ready")
        y_ready, yt_ready, x_added = sem("wkv_y_ready"), sem("wkv_yt_ready"), sem("wkv_x_added")

        with nc.Block() as block:
            @block.sync
            def _(sp):
                sp.dma_start(k["par"][:], params).then_inc(par_in, 16)
                xr = x.rearrange("(j p) c -> p j c", p=P)
                for i in range(4):
                    sp.dma_start(x_res[:, 4 * i:4 * i + 4, :], xr[:, 4 * i:4 * i + 4, :]).then_inc(x_in[i], 16)
                for h in range(KC):
                    sp.dma_start(vT[:, h, :, :], ctxT[h * P:(h + 1) * P, :].rearrange("p (b s) -> p b s", s=S)
                                 ).then_inc(v_in[h], 16)

            @block.gpsimd
            def _(pool):
                nc.gpsimd.memset(ident[:], 0.0).then_inc(consts, 1)
                nc.gpsimd.memset(k["ones"][:], 1.0).then_inc(consts, 1)
                pool.wait_ge(consts, 2)
                nc.gpsimd.affine_select(out=ident[:], in_=ident[:], compare_op=ALU.not_equal, fill=1.0, base=0,
                                        pattern=[[-1, P]], channel_multiplier=1).then_inc(consts, 1)
                nc.gpsimd.memset(k65[:, :, :, 0], NEG_BIG).then_inc(fills, 1)
                nc.gpsimd.memset(w65[:], 0.0).then_inc(fills, 1)
                for n in ("A2", "E2", "E2v"):
                    for i in range(2):
                        nc.gpsimd.memset(buf[n][i][:, :, 0], 0.0).then_inc(fills, 1)
                for c, (h, q) in enumerate(CHUNKS):
                    i = c % 2
                    v = vT[:, h, BQ * q:BQ * (q + 1), :]
                    if c == 0:
                        pool.wait_ge(fills, 8)
                    if q == 0:
                        pool.wait_ge(v_in[h], 16)
                    pool.wait_ge(exps_ready, 4 * c + 2)
                    if c >= 2:
                        pool.wait_ge(pq_ready, 2 * (c - 1))
                    nc.gpsimd.tensor_tensor(buf["E2v"][i][:, :, 1:], buf["E2"][i][:, :, 1:], v, ALU.mult
                                            ).then_inc(E2v_ready, 1)
                    pool.wait_ge(exps_ready, 4 * c + 4)
                    nc.gpsimd.tensor_tensor(buf["Ev"][i][:], buf["E"][i][:], v, ALU.mult).then_inc(Ev_ready, 1)
                    pool.wait_ge(pq_ready, 2 * c + 1)
                    nc.gpsimd.tensor_tensor(buf["Ap"][i][:], buf["A"][i][:], buf["p"][i][:, :, 0:S], ALU.mult
                                            ).then_inc(Apq_ready, 1)
                    pool.wait_ge(pq_ready, 2 * c + 2)
                    nc.gpsimd.tensor_tensor(buf["Aq"][i][:], buf["A"][i][:], buf["q"][i][:, :, 0:S], ALU.mult
                                            ).then_inc(Apq_ready, 1)

            @block.vector
            def _(dve):
                chain = Chain(dve, dve_done)
                for j in range(NT):
                    if j % 4 == 0:
                        dve.wait_ge(x_in[j // 4], 16)
                    chain.mark(nc.vector.bn_stats(k["stat6"][:, j, :], x_res[:, j, :]))
                chain.settle()
                dve_mean_var(k, chain, var_ready)
                dve.wait_ge(rs_ready, 1)
                dve.wait_ge(var_ready, 1)
                rsqrt_newton(chain, nc, k["rstd"][:], k["rs0"][:], k["var"][:], k["st"][0][:])
                for j in range(NT):
                    nc.vector.tensor_scalar(z[:, j, :], x_res[:, j, :], k["mean"][:, j:j + 1],
                                            k["rstd"][:, j:j + 1], ALU.subtract, ALU.mult).then_inc(z_ready, 1)
                dve.wait_ge(par_in, 16)
                dve.wait_ge(fills, 8)
                for h in range(KC):
                    chain.mark(nc.vector.tensor_scalar(w65[:, h, :, 1:], w65[:, h, :, 1:], col("w", h), None, ALU.add))
                    chain.mark(nc.vector.memset(w65[:, h, :, 0], NEG_BIG))

                def flat(t):
                    return t.rearrange("p b l -> p (b l)")

                def gaps(c):
                    h, q = CHUNKS[c]
                    i = c % 2
                    kk = k65[:, h, BQ * q:BQ * (q + 1), :]
                    o = buf["o"][i]
                    if q == 0:
                        dve.wait_ge(k_ready, 4 * h + 4)
                    chain.settle()
                    chain(nc.vector.tensor_tensor_scan(flat(o[:]), flat(w65[:, h]), flat(kk), NEG_BIG,
                                                       ALU.add, ALU.max))
                    if c >= 2:
                        dve.wait_ge(E2v_ready, c - 1)
                        dve.wait_ge(Apq_ready, 2 * (c - 1))
                        dve.wait_ge(Ev_ready, c - 1)
                    nc.vector.tensor_tensor(buf["E2"][i][:, :, 1:], kk[:, :, 1:], o[:, :, 1:], ALU.subtract
                                            ).then_inc(gaps_ready, 1)
                    nc.vector.scalar_tensor_tensor(buf["A2"][i][:, :, 1:], o[:, :, 0:S], col("w", h), o[:, :, 1:],
                                                   ALU.add, ALU.subtract).then_inc(gaps_ready, 1)
                    nc.vector.scalar_tensor_tensor(buf["d"][i][:], kk[:, :, 1:], col("u", h), o[:, :, 0:S],
                                                   ALU.add, ALU.subtract).then_inc(gaps_ready, 1)

                def sums(c):
                    h, q = CHUNKS[c]
                    i = c % 2
                    t = {n: buf[n][i] for n in buf}
                    dve.wait_ge(exps_ready, 4 * c + 2)
                    dve.wait_ge(E2v_ready, c + 1)
                    if c >= 2:
                        dve.wait_ge(Apq_ready, 2 * (c - 1))
                    nc.vector.tensor_tensor_scan(flat(t["p"][:]), flat(t["A2"][:]), flat(t["E2v"][:]), 0.0,
                                                 ALU.mult, ALU.add).then_inc(pq_ready, 1)
                    nc.vector.tensor_tensor_scan(flat(t["q"][:]), flat(t["A2"][:]), flat(t["E2"][:]), 0.0,
                                                 ALU.mult, ALU.add).then_inc(pq_ready, 1)
                    dve.wait_ge(Apq_ready, 2 * c + 2)
                    dve.wait_ge(Ev_ready, c + 1)
                    nc.vector.tensor_tensor(t["Aq"][:], t["Aq"][:], t["E"][:], ALU.add).then_inc(den_ready, 1)
                    chain(nc.vector.tensor_tensor(t["Ap"][:], t["Ap"][:], t["Ev"][:], ALU.add))
                    dve.wait_ge(den_ready, c + 1)
                    dve.wait_ge(rcp_ready, c + 1)
                    chain(nc.vector.tensor_tensor(t["Aq"][:], t["Aq"][:], t["d"][:], ALU.mult))
                    chain(nc.vector.scalar_tensor_tensor(t["d"][:], t["Aq"][:], -2.0, t["d"][:], ALU.add, ALU.mult))
                    nc.vector.scalar_tensor_tensor(yT[:, h, BQ * q:BQ * (q + 1), :], t["Ap"][:], -1.0, t["d"][:],
                                                   ALU.mult, ALU.mult).then_inc(y_ready, 1)

                for c in range(len(CHUNKS) + 1):
                    if c < len(CHUNKS):
                        if c >= 2:
                            dve.wait_ge(y_ready, c - 1)
                            dve.wait_ge(pq_ready, 2 * (c - 1))
                        gaps(c)
                    if c:
                        sums(c - 1)
                for m in range(NT // 2):
                    dve.wait_ge(yt_ready, m + 1)
                    nc.vector.tensor_tensor(x_res[:, 2 * m:2 * m + 2, :], x_res[:, 2 * m:2 * m + 2, :],
                                            y_ps[m % 2][:].rearrange("p (j c) -> p j c", j=2), ALU.add
                                            ).then_inc(x_added, 1)

            @block.scalar
            def _(act):
                chain = Chain(act, act_done)
                nc.scalar.preload_act_table_set(LN_EXP_SET)
                act_rsqrt(act, nc, k["rs0"][:], k["var"][:], k["st"][2][:], var_ready, 1, chain, rs_ready)
                for n in range(2 * (NT // 4)):
                    h, g = divmod(n, NT // 4)
                    act.wait_ge(zT_ready, n + 1)
                    nc.scalar.activation(k65[:, h, 8 * g:8 * g + 8, 1:], zT_ps[n % 4][:].rearrange("p (b s) -> p b s", s=S),
                                         ACT.Copy).then_inc(k_ready, 1)

                def exps(c):
                    i = c % 2
                    t = {n: buf[n][i] for n in buf}
                    act.wait_ge(gaps_ready, 3 * c + 1)
                    nc.scalar.activation(t["E2"][:, :, 1:], t["E2"][:, :, 1:], ACT.Exp).then_inc(exps_ready, 1)
                    act.wait_ge(gaps_ready, 3 * c + 2)
                    nc.scalar.activation(t["A2"][:, :, 1:], t["A2"][:, :, 1:], ACT.Exp).then_inc(exps_ready, 1)
                    act.wait_ge(gaps_ready, 3 * c + 3)
                    chain.mark(nc.scalar.activation(t["A"][:], t["d"][:], ACT.Relu))
                    chain(nc.scalar.activation(t["E"][:], t["d"][:], ACT.Relu, scale=-1.0))
                    nc.scalar.activation(t["A"][:], t["A"][:], ACT.Exp, scale=-1.0).then_inc(exps_ready, 1)
                    nc.scalar.activation(t["E"][:], t["E"][:], ACT.Exp, scale=-1.0).then_inc(exps_ready, 1)

                def guess_rcp(c):
                    t = {n: buf[n][c % 2] for n in buf}
                    act.wait_ge(den_ready, c + 1)
                    act.wait_ge(exps_ready, 4 * c + 4)
                    chain(nc.scalar.activation(t["d"][:], t["Aq"][:], ACT.Ln))
                    nc.scalar.activation(t["d"][:], t["d"][:], ACT.Exp, scale=-1.0).then_inc(rcp_ready, 1)

                for c in range(len(CHUNKS) + 1):
                    if c < len(CHUNKS):
                        exps(c)
                    if c:
                        guess_rcp(c - 1)

            @block.tensor
            def _(pe):
                pe.wait_ge(consts, 3)
                for n in range(2 * (NT // 4)):
                    h, g = divmod(n, NT // 4)
                    pe.wait_ge(z_ready, 4 * g + 4)
                    if n >= 4:
                        pe.wait_ge(k_ready, n - 3)
                    for j in range(4):
                        last = nc.tensor.transpose(zT_ps[n % 4][:, j * P:(j + 1) * P],
                                                   z[:, 4 * g + j, h * P:(h + 1) * P], ident[:])
                    last.then_inc(zT_ready, 1)
                for m in range(NT // 2):
                    pe.wait_ge(y_ready, len(CHUNKS) - 1 + m // (NT // 4))
                    if m >= 2:
                        pe.wait_ge(x_added, m - 1)
                    for j in range(2):
                        for h in range(KC):
                            t0 = (2 * m + j) * P
                            last = nc.tensor.transpose(y_ps[m % 2][:, (2 * j + h) * P:(2 * j + h + 1) * P],
                                                       yT[:, h].rearrange("p b s -> p (b s)")[:, t0:t0 + P], ident[:])
                    last.then_inc(yt_ready, 1)



def pipeline(eng, step, rounds, width, lag, peel_last=False):
    for o in range(width):
        step(0, o)
    with eng.Fori(1, rounds - peel_last) as i:
        for o in range(width):
            step(i, o)
    if peel_last:
        for o in range(width):
            step(rounds - 1, o)
    for o in range(lag):
        step(rounds, o)


class Unit:

    def __init__(self, i, o, width, rounds, back=0):
        static = isinstance(i, int)
        self.n = width * i + o - back
        self.o = (o - back) % width
        self.live = not static or 0 <= self.n < width * rounds
        self.static = static

    def count(self, per=1, more=0):
        return self.n * per + more

    def before(self, units, per=1):
        if self.static and self.n < units:
            return None
        return (self.n - units + 1) * per


def wait_unit(eng, sem, value):
    if value is not None:
        eng.wait_ge(sem, value)



def ternary_ffn_stage(k, w1T, w3T, w2T):
    nc, sem, x_res, ident = k["nc"], k["sem"], k["x_res"], k["ident"]
    HC = -(-HID // P)
    TAIL = HID - (HC - 1) * P
    BANK = 512
    ROUNDS, WIDTH = NT // 2, 2
    with ExitStack() as own:
        def sb(name, shape, dt=F32):
            return own.enter_context(nc.sbuf_tensor(name, shape, dt))

        def psum(name, shape, dt=F32):
            return own.enter_context(nc.psum_tensor(name, shape, dt))

        raw13 = [sb(f"raw{n}", [P, KC, HID]) for n in (1, 3)]
        raw2 = sb("raw2", [P, HC, C])
        w13q = [sb(f"w{n}q", [P, KC, HID], BF16) for n in (1, 3)]
        w2q = sb("w2q", [P, HC, C], BF16)
        asum = sb("asum", [P, 4])
        ws = sb("ws", [P, 4])
        iws = sb("iws", [P, 4])
        z = sb("tf_z", [P, NT, C])
        amax = sb("tf_amax", [P, NT])
        qs = sb("tf_qs", [P, NT])
        tsc = sb("tf_tsc", [P, NT, 2])
        cur = [sb(f"tf_cur{i}", [P, 2]) for i in range(2)]
        xq = [sb(f"tf_xq{i}", [P, C], BF16) for i in range(2)]
        xqT = [sb(f"tf_xqT{i}", [P, C], BF16) for i in range(2)]
        gate = sb("tf_gate", [P, HID])
        hm = sb("tf_hm", [P, HID])
        hr = sb("tf_hr", [P, HID])
        hq = [sb(f"tf_hq{i}", [P, HID], BF16) for i in range(2)]
        hqT = [sb(f"tf_hqT{i}", [P, HC * P], BF16) for i in range(2)]
        small = sb("tf_small", [P, 4])
        gam = [sb(f"tf_gam{i}", [P, 1]) for i in range(2)]
        identb = sb("identb", [P, P], BF16)
        xT_ps = [psum(f"tf_xT_ps{i}", [P, 2 * BANK], BF16) for i in range(2)]
        h1_ps, h3_ps = psum("h1_ps", [P, 2 * BANK]), psum("h3_ps", [P, 2 * BANK])
        hT_ps = psum("hT_ps", [P, 2 * BANK], BF16)
        y_ps = psum("tf_y_ps", [P, BANK])

        w13_in, w2_in = sem("w13_in"), sem("w2_in")
        cleared, idb_ready = sem("tf_cleared"), sem("idb_ready")
        asum_ready, wsum_ready, w_ready = sem("asum_ready"), sem("wsum_ready"), sem("tf_w_ready")
        var_ready, rs_ready = sem("tf_var_ready"), sem("tf_rs_ready")
        dve_done, act_done = sem("tf_dve_done"), sem("tf_act_done")
        unit_done = sem("tf_unit_done")
        xq_ready, xT_ready, xqT_ready = sem("tf_xq_ready"), sem("tf_xT_ready"), sem("tf_xqT_ready")
        h_ready, gate_ready, hm_ready = sem("tf_h_ready"), sem("tf_gate_ready"), sem("tf_hm_ready")
        hq_ready, hT_ready, hqT_ready = sem("tf_hq_ready"), sem("tf_hT_ready"), sem("tf_hqT_ready")
        y_ready, x_added = sem("tf_y_ready"), sem("tf_x_added")

        with nc.Block() as block:
            @block.sync
            def _(sp):
                for raw, w in zip(raw13, (w1T, w3T)):
                    sp.dma_start(raw[:], w.rearrange("(h p) n -> p h n", p=P)).then_inc(w13_in, 16)
                full = (HC - 1) * P
                sp.dma_start(raw2[:, 0:HC - 1, :], w2T[0:full, :].rearrange("(a p) n -> p a n", p=P)
                             ).then_inc(w2_in, 16)
                sp.dma_start(raw2[0:TAIL, HC - 1, :], w2T[full:HID, :]).then_inc(w2_in, 16)

            @block.gpsimd
            def _(pool):
                nc.gpsimd.memset(asum[:], 0.0).then_inc(cleared, 1)
                nc.gpsimd.tensor_copy(identb[:], ident[:]).then_inc(idb_ready, 1)

            @block.vector
            def _(dve):
                chain = Chain(dve, dve_done)
                for j in range(NT):
                    chain.mark(nc.vector.bn_stats(k["stat6"][:, j, :], x_res[:, j, :]))
                chain.settle()
                dve_mean_var(k, chain, var_ready)
                dve.wait_ge(cleared, 1)
                dve.wait_ge(w13_in, 32)
                for n, raw in enumerate(raw13):
                    nc.vector.tensor_reduce(asum[:, n:n + 1], raw[:].rearrange("p h n -> p (h n)"), AX.X, ALU.add,
                                            apply_absolute_value=True).then_inc(asum_ready, 1)
                dve.wait_ge(w2_in, 32)
                nc.vector.tensor_reduce(asum[:, 2:3], raw2[:, 0:HC - 1, :].rearrange("p a n -> p (a n)"), AX.X,
                                        ALU.add, apply_absolute_value=True).then_inc(asum_ready, 1)
                nc.vector.tensor_reduce(asum[0:TAIL, 3:4], raw2[0:TAIL, HC - 1, :], AX.X, ALU.add,
                                        apply_absolute_value=True).then_inc(asum_ready, 1)
                dve.wait_ge(rs_ready, 1)
                dve.wait_ge(var_ready, 1)
                rsqrt_newton(chain, nc, k["rstd"][:], k["rs0"][:], k["var"][:], k["st"][0][:])
                for j in range(NT):
                    chain.mark(nc.vector.tensor_scalar(z[:, j, :], x_res[:, j, :], k["mean"][:, j:j + 1],
                                                       k["rstd"][:, j:j + 1], ALU.subtract, ALU.mult))
                chain.settle()
                dve.wait_ge(wsum_ready, 1)
                chain(nc.vector.tensor_scalar(ws[:, 0:3], y_ps[:, 0:3], 1.0 / (HID * C), None, ALU.mult))
                chain(nc.vector.scalar_tensor_tensor(ws[:, 2:3], y_ps[:, 3:4], 1.0 / (HID * C), ws[:, 2:3],
                                                     ALU.mult, ALU.add))
                chain(nc.vector.tensor_scalar(ws[:, 0:3], ws[:, 0:3], QUANT_EPS, None, ALU.max))
                chain(nc.vector.reciprocal(iws[:, 0:3], ws[:, 0:3]))

                def ternary(raw, n, dst):
                    chain(nc.vector.tensor_scalar(raw, raw, iws[0:raw.shape[0], n:n + 1], ROUND32, ALU.mult, ALU.add))
                    chain(nc.vector.tensor_scalar(raw, raw, -ROUND32, 1.0, ALU.add, ALU.min))
                    nc.vector.tensor_scalar(dst, raw, -1.0, None, ALU.max).then_inc(w_ready, 1)

                for n in range(2):
                    ternary(raw13[n][:], n, w13q[n][:])
                ternary(raw2[:, 0:HC - 1, :], 2, w2q[:, 0:HC - 1, :])
                ternary(raw2[0:TAIL, HC - 1, :], 2, w2q[0:TAIL, HC - 1, :])
                chain(nc.vector.tensor_reduce(amax[:], z[:], AX.X, ALU.max, apply_absolute_value=True))
                chain(nc.vector.tensor_scalar(amax[:], amax[:], QUANT_EPS, 1.0 / 127.0, ALU.max, ALU.mult))
                chain.mark(nc.vector.tensor_scalar(tsc[:, :, 0], amax[:], ws[:, 0:1], None, ALU.mult))
                chain.mark(nc.vector.tensor_scalar(tsc[:, :, 1], amax[:], ws[:, 1:2], None, ALU.mult))
                chain(nc.vector.reciprocal(qs[:], amax[:]))
                for j in range(NT):
                    chain.mark(nc.vector.tensor_scalar(z[:, j, :], z[:, j, :], qs[:, j:j + 1], ROUND32,
                                                       ALU.mult, ALU.add))
                chain.settle()
                steps = Chain(dve, unit_done)

                def step(i, o):
                    u, late = Unit(i, o, WIDTH, ROUNDS), Unit(i, o, WIDTH, ROUNDS, 1)
                    if u.live:
                        par = u.o % 2
                        steps.at(u.count(7))
                        wait_unit(dve, xT_ready, u.before(2))
                        wait_unit(dve, gate_ready, u.before(2))
                        nc.vector.tensor_scalar(xq[par][:], z[:, bass.ds(u.n, 1), :].rearrange("p a c -> p (a c)"),
                                                -ROUND32, None, ALU.add).then_inc(xq_ready, 1)
                        nc.vector.tensor_copy(cur[par][:], tsc[:, bass.ds(u.n, 1), :].rearrange("p a c -> p (a c)")
                                              ).then_inc(xq_ready, 1)
                        dve.wait_ge(gate_ready, u.count(1, 1))
                        nc.vector.tensor_tensor(hm[:], gate[:], h3_ps[:, 0:HID], ALU.mult).then_inc(hm_ready, 1)
                        dve.wait_ge(hm_ready, u.count(1, 1))
                        steps(nc.vector.tensor_reduce(small[:, 0:1], hm[:], AX.X, ALU.max, apply_absolute_value=True))
                        dve.wait_ge(xq_ready, u.count(2, 2))
                        steps(nc.vector.tensor_scalar(small[:, 0:1], small[:, 0:1], cur[par][:, 1:2], QUANT_EPS,
                                                      ALU.mult, ALU.max))
                        steps(nc.vector.reciprocal(small[:, 1:2], small[:, 0:1]))
                        wait_unit(dve, x_added, u.before(2))
                        steps.mark(nc.vector.tensor_scalar(gam[par][:], small[:, 0:1], ws[:, 2:3], 1.0 / 127.0,
                                                           ALU.mult, ALU.mult))
                        steps(nc.vector.tensor_scalar(small[:, 2:3], small[:, 1:2], cur[par][:, 1:2], 127.0,
                                                      ALU.mult, ALU.mult))
                        steps(nc.vector.tensor_scalar(hr[:], hm[:], small[:, 2:3], ROUND32, ALU.mult, ALU.add))
                        wait_unit(dve, hT_ready, u.before(2))
                        steps.mark(nc.vector.tensor_scalar(hq[par][:], hr[:], -ROUND32, None, ALU.add))
                        steps.settle()
                        nc.vector.memset(small[:, 3:4], 0.0).then_inc(hq_ready, 1)
                    if late.live:
                        dve.wait_ge(y_ready, late.count(1, 1))
                        xt = x_res[:, bass.ds(late.n, 1), :].rearrange("p a c -> p (a c)")
                        nc.vector.scalar_tensor_tensor(xt, y_ps[:, 0:C], gam[late.o % 2][:], xt, ALU.mult, ALU.add
                                                       ).then_inc(x_added, 1)

                pipeline(dve, step, ROUNDS, WIDTH, 1)

            @block.scalar
            def _(act):
                chain = Chain(act, act_done)
                nc.scalar.preload_act_table_set(LN_EXP_SET)
                act_rsqrt(act, nc, k["rs0"][:], k["var"][:], k["st"][2][:], var_ready, 1, chain, rs_ready)
                nc.scalar.preload_act_table(ACT.Silu)

                def step(i, o):
                    u, late = Unit(i, o, WIDTH, ROUNDS), Unit(i, o, WIDTH, ROUNDS, 1)
                    if u.live:
                        par = u.o % 2
                        act.wait_ge(xT_ready, u.count(1, 1))
                        wait_unit(act, h_ready, u.before(2))
                        nc.scalar.activation(xqT[par][:], xT_ps[par][:, 0:C], ACT.Copy).then_inc(xqT_ready, 1)
                    if late.live:
                        par = late.o % 2
                        act.wait_ge(hT_ready, late.count(1, 1))
                        wait_unit(act, y_ready, late.before(2))
                        full = (HC - 1) * P
                        nc.scalar.activation(hqT[par][:, 0:full], hT_ps[:, 0:full], ACT.Copy).then_inc(hqT_ready, 1)
                        nc.scalar.activation(hqT[par][0:TAIL, full:full + P], hT_ps[0:TAIL, full:full + P], ACT.Copy
                                             ).then_inc(hqT_ready, 1)
                    if u.live:
                        act.wait_ge(h_ready, u.count(1, 1))
                        act.wait_ge(xq_ready, u.count(2, 2))
                        wait_unit(act, hm_ready, u.before(1))
                        nc.scalar.activation(gate[:], h1_ps[:, 0:HID], ACT.Silu, scale=cur[u.o % 2][:, 0:1]
                                             ).then_inc(gate_ready, 1)

                pipeline(act, step, ROUNDS, WIDTH, 1)

            @block.tensor
            def _(pe):
                pe.wait_ge(asum_ready, 4)
                pe.wait_ge(cleared, 1)
                nc.tensor.matmul(y_ps[:, 0:4], k["ones"][:], asum[:], start=True, stop=True).then_inc(wsum_ready, 1)
                pe.wait_ge(idb_ready, 1)

                def step(i, o):
                    u, late = Unit(i, o, WIDTH, ROUNDS), Unit(i, o, WIDTH, ROUNDS, 1)
                    if u.live:
                        par = u.o % 2
                        pe.wait_ge(xq_ready, u.count(2, 1))
                        wait_unit(pe, xqT_ready, u.before(2))
                        for h in range(KC):
                            last = nc.tensor.transpose(xT_ps[par][:, h * P:(h + 1) * P], xq[par][:, h * P:(h + 1) * P],
                                                       identb[:])
                        last.then_inc(xT_ready, 1)
                    if late.live:
                        par = late.o % 2
                        pe.wait_ge(hq_ready, late.count(1, 1))
                        wait_unit(pe, hqT_ready, late.before(1, 2))
                        for a in range(HC):
                            m = min(P, HID - a * P)
                            last = nc.tensor.transpose(hT_ps[0:m, a * P:a * P + P], hq[par][:, a * P:a * P + m],
                                                       identb[:])
                        last.then_inc(hT_ready, 1)
                    if u.live:
                        par = u.o % 2
                        if u.static and u.n == 0:
                            pe.wait_ge(w_ready, 4)
                        pe.wait_ge(xqT_ready, u.count(1, 1))
                        wait_unit(pe, hm_ready, u.before(1))
                        for ps, w in ((h1_ps, w13q[0]), (h3_ps, w13q[1])):
                            for c0, c1 in ((0, BANK), (BANK, HID)):
                                for h in range(KC):
                                    last = nc.tensor.matmul(ps[:, c0:c1], xqT[par][:, h * P:(h + 1) * P], w[:, h, c0:c1],
                                                            start=(h == 0), stop=(h == KC - 1))
                        last.then_inc(h_ready, 1)
                    if late.live:
                        par = late.o % 2
                        pe.wait_ge(hqT_ready, late.count(2, 2))
                        wait_unit(pe, x_added, late.before(1))
                        if late.static and late.n == 0:
                            pe.wait_ge(w_ready, 4)
                        for a in range(HC):
                            m = min(P, HID - a * P)
                            last = nc.tensor.matmul(y_ps[:, 0:C], hqT[par][0:m, a * P:a * P + P], w2q[0:m, a, :],
                                                    start=(a == 0), stop=(a == HC - 1))
                        last.then_inc(y_ready, 1)

                pipeline(pe, step, ROUNDS, WIDTH, 1)



def act_like_fp8(chain, nc, y, e, m, out):
    chain(nc.vector.tensor_scalar(y, y, FP8_MAX, -FP8_MAX, ALU.min, ALU.max))
    chain(nc.vector.tensor_scalar(e.bitcast(U16), y.bitcast(U16), 0x7F80, None, ALU.bitwise_and))
    chain(nc.vector.tensor_scalar(m, e, 2.0 ** -6, 1.5 * 2.0 ** 4, ALU.max, ALU.mult))
    chain(nc.vector.tensor_tensor(y, y, m, ALU.add))
    chain.mark(nc.vector.tensor_tensor(out, y, m, ALU.subtract))


def ln_quant_stage(k, xq8):
    nc, sem, x_res, ident, col = k["nc"], k["sem"], k["x_res"], k["ident"], k["col"]
    GT = 4
    NG = NT // GT
    W = GT * P
    with ExitStack() as own:
        def sb(name, shape, dt=F32):
            return own.enter_context(nc.sbuf_tensor(name, shape, dt))

        z = sb("lq_z", [P, NT, C])
        lnT = [sb(f"lnT{i}", [P, KC, W]) for i in range(2)]
        y = [sb(f"lq_y{i}", [P, 4 * KC, W], BF16) for i in range(2)]
        e = sb("lq_e", [P, 4 * KC, W], BF16)
        m = sb("lq_m", [P, 4 * KC, W], BF16)
        inv = sb("lq_inv", [P, 4 * KC])
        zT_ps = [own.enter_context(nc.psum_tensor(f"lq_zT_ps{i}", [P, 512], F32)) for i in range(4)]
        var_ready, rs_ready = sem("lq_var_ready"), sem("lq_rs_ready")
        dve_done, act_done, inv_ready = sem("lq_dve_done"), sem("lq_act_done"), sem("lq_inv_ready")
        z_ready, zT_ready, y_ready, xq_ready = sem("lq_z_ready"), sem("lq_zT_ready"), sem("lq_y_ready"), sem("lq_xq_ready")
        lnT_ready = sem("lq_lnT_ready")

        with nc.Block() as block:
            @block.vector
            def _(dve):
                chain = Chain(dve, dve_done)
                nc.vector.reciprocal(inv[:], col("sq", 0, 4 * KC)).then_inc(inv_ready, 1)
                for r in range(2):
                    src = x_res if r == 0 else z
                    for j in range(NT):
                        chain.mark(nc.vector.bn_stats(k["stat6"][:, j, :], src[:, j, :]))
                    chain.settle()
                    dve_mean_var(k, chain, var_ready)
                    dve.wait_ge(rs_ready, r + 1)
                    dve.wait_ge(var_ready, r + 1)
                    rsqrt_newton(chain, nc, k["rstd"][:], k["rs0"][:], k["var"][:], k["st"][0][:])
                    for j in range(NT):
                        ins = nc.vector.tensor_scalar(z[:, j, :], src[:, j, :], k["mean"][:, j:j + 1],
                                                      k["rstd"][:, j:j + 1], ALU.subtract, ALU.mult)
                        if r == 0:
                            chain.mark(ins)
                        else:
                            ins.then_inc(z_ready, 1)
                    if r == 0:
                        chain.settle()
                for g in range(NG):
                    dve.wait_ge(y_ready, 8 * g + 8)
                    act_like_fp8(chain, nc, y[g % 2][:], e[:], m[:], xq8[:, :, g * W:(g + 1) * W])
                    chain.settle()
                    nc.vector.memset(k["st"][1][:, 0:1], 0.0).then_inc(xq_ready, 1)

            @block.tensor
            def _(pe):
                for n in range(NG * KC):
                    g, h = divmod(n, KC)
                    pe.wait_ge(z_ready, GT * g + GT)
                    if n >= 4:
                        pe.wait_ge(lnT_ready, n - 3)
                    for j in range(GT):
                        last = nc.tensor.transpose(zT_ps[n % 4][:, j * P:(j + 1) * P],
                                                   z[:, GT * g + j, h * P:(h + 1) * P], ident[:])
                    last.then_inc(zT_ready, 1)

            @block.scalar
            def _(act):
                chain = Chain(act, act_done)
                nc.scalar.preload_act_table_set(LN_EXP_SET)
                for r in range(2):
                    act_rsqrt(act, nc, k["rs0"][:], k["var"][:], k["st"][2][:], var_ready, r + 1, chain, rs_ready)
                act.wait_ge(inv_ready, 1)
                for g in range(NG):
                    for h in range(KC):
                        n = g * KC + h
                        act.wait_ge(zT_ready, n + 1)
                        nc.scalar.activation(lnT[g % 2][:, h, :], zT_ps[n % 4][:], ACT.Identity, scale=col("ln_w", h),
                                             bias=col("ln_b", h)).then_inc(lnT_ready, 1)
                    act.wait_ge(lnT_ready, KC * (g + 1))
                    if g >= 2:
                        act.wait_ge(xq_ready, g - 1)
                    for q in range(4):
                        for h in range(KC):
                            a = q * KC + h
                            nc.scalar.activation(y[g % 2][:, a, :], lnT[g % 2][:, h, :], ACT.Copy,
                                                 scale=inv[:, a:a + 1]).then_inc(y_ready, 1)



def attention_stage(k, kind, xq8, weights, wprojT, ctxT):
    nc, sem, x_res, ident, col = k["nc"], k["sem"], k["x_res"], k["ident"], k["col"]
    own_kv = kind == "self"
    name = kind[0]
    GU = 2
    HU = GU * HPG
    UT = G // GU
    WIDTH = 2 * UT
    ROUNDS = NT // 2
    QW, KW = HU * D, GU * D
    NQ = 3 if own_kv else 1
    Q0 = 0 if own_kv else 3
    CHUNK = 2048
    scale = float(D) ** -0.5
    pre = "" if own_kv else "x"
    with ExitStack() as own:
        def sb(nm, shape, dt=F32):
            return own.enter_context(nc.sbuf_tensor(f"{name}_{nm}", shape, dt))

        def psum(nm, shape, dt=F32):
            return own.enter_context(nc.psum_tensor(f"{name}_{nm}", shape, dt))

        def sg(nm):
            return sem(f"{name}_{nm}")

        wq = [sb(f"wq{p}", [P, KC, NH * D], F32R) for p in range(2)]
        wp = [sb(f"wp{p}", [P, NH, C], F32R) for p in range(2)]
        if own_kv:
            wk = [sb(f"wk{p}", [P, KC, G * D], F32R) for p in range(2)]
            wv = [sb(f"wv{p}", [P, KC, G * D], F32R) for p in range(2)]
        else:
            wkx, wvx = sb("wkx", [P, KC, G * D]), sb("wvx", [P, KC, G * D])
            ctx_t = [sb(f"ctx{i}", [P, KC, P]) for i in range(2)]
        raw = [sb(f"raw{i}", [P, CHUNK]) for i in range(2)]
        hsum = sb("hsum", [P, NH])
        xqf = [sb(f"xqf{i}", [P, NQ * KC, P], F32R) for i in range(2)]
        lnp = sb("lnp", [P, 2])
        ism = sb("ism", [P, NH])
        pscale = sb("pscale", [P, 1])
        sq = sb("sq", [P, QW + KW])
        v6, r6, t6, l6 = (sb(nm, [P, HU + GU]) for nm in ("v6", "r6", "t6", "l6"))
        g6 = sb("g6", [P, HU + GU])
        qn, kn = sb("qn", [P, QW]), sb("kn", [P, KW])
        v_s = [sb(f"v{i}", [P, KW]) for i in range(4)]
        qT, kT = sb("qT", [P, QW]), sb("kT", [P, KW])
        nmax, psum_s, rsum = sb("nmax", [P, 4]), sb("psums", [P, 4]), sb("rsum", [P, 4])
        pe_s, pn = sb("p", [P, 4 * S]), sb("pn", [P, 4 * S])
        pT = sb("pT", [P, GU, HPG, 2, S])
        yb, eb, mb = (sb(nm, [P, QW], BF16) for nm in ("yb", "eb", "mb"))
        cat = [sb(f"cat{i}", [P, QW], F32R) for i in range(2)]
        q_ps = [psum(f"q_ps{i}", [P, QW]) for i in range(2)]
        kv_ps = [psum(f"kv_ps{i}", [P, 2 * KW]) for i in range(2)]
        qT_ps = psum("qT_ps", [P, QW])
        ks_ps = psum("ks_ps", [P, 512])
        po_ps = psum("po_ps", [P, 512])
        pj_ps = psum("pj_ps", [P, 512])

        raw_in = [sg(f"raw_in{i}") for i in range(2)]
        hi_ready, lo_ready, prep_done, w_direct = sg("hi_ready"), sg("lo_ready"), sg("prep_done"), sg("w_direct")
        pT_cleared = sg("pT_cleared")
        xqf_ready, ctx_in = sg("xqf_ready"), [sg(f"ctx_in{i}") for i in range(2)]
        q_done, kv_done, t_done = sg("q_done"), sg("kv_done"), sg("t_done")
        sqq_ready, sqk_ready, v_ready = sg("sqq_ready"), sg("sqk_ready"), sg("v_ready")
        var_ready, rs_ready = sg("var_ready"), sg("rs_ready")
        qn_ready, kn_ready = sg("qn_ready"), sg("kn_ready")
        qT_ready, kT_ready = sg("qT_ready"), sg("kT_ready")
        sc_done, max_ready, exp_ready = sg("sc_done"), sg("max_ready"), sg("exp_ready")
        rsum_ready, pn_ready = sg("rsum_ready"), sg("pn_ready")
        pt_done, pT_ready, pv_done = sg("pt_done"), sg("pT_ready"), sg("pv_done")
        y_ready, cat_ready, pj_done, x_added = sg("y_ready"), sg("cat_ready"), sg("pj_done"), sg("x_added")
        norm_steps, cat_steps, act_steps = sg("norm_steps"), sg("cat_steps"), sg("act_steps")

        steps = []
        if own_kv:
            wqT, wkT, wvT = weights
            for h in range(KC):
                steps.append((wqT[h * P:(h + 1) * P, :], col("sq", h), col("wq_s"), True, wq[0][:, h, :], wq[1][:, h, :], None))
            for h in range(KC):
                steps.append((wkT[h * P:(h + 1) * P, :], col("sk", h), col("wk_s"), True, wk[0][:, h, :], wk[1][:, h, :], None))
                steps.append((wvT[h * P:(h + 1) * P, :], col("sv", h), col("wv_s"), False, wv[0][:, h, :], wv[1][:, h, :], None))
        else:
            wqxT, wkvxT = weights
            for h in range(KC):
                steps.append((wqxT[h * P:(h + 1) * P, :], col("sqx", h), col("wqx_s"), True, wq[0][:, h, :], wq[1][:, h, :], None))
            for h in range(KC):
                steps.append((wkvxT[h * P:(h + 1) * P, 0:G * D], None, None, True, None, None, wkx[:, h, :]))
        half = NH // 2
        row0 = 0 if own_kv else NH * D
        for a in range(2):
            src = wprojT[row0 + a * half * D:row0 + (a + 1) * half * D, :].rearrange("(c p) n -> p c n", p=P)
            steps.append((src, None, None, False, wp[0][:, a * half:(a + 1) * half, :],
                          wp[1][:, a * half:(a + 1) * half, :], None))
        n_hi = [sum(1 for s in steps[:i + 1] if s[4] is not None) for i in range(len(steps))]
        n_plain = [sum(1 for s in steps[:i + 1] if s[6] is not None) for i in range(len(steps))]

        def raw_view(i, shape):
            n = 1
            for s in shape[1:]:
                n *= s
            v = raw[i % 2][:, 0:n]
            return v if len(shape) == 2 else v.rearrange("p (c n) -> p c n", c=shape[1])

        def units(i, o, *backs):
            return [Unit(i, o, WIDTH, ROUNDS, b) for b in backs]

        def tile_of(i, o):
            return 2 * i + o // UT

        with nc.Block() as block:
            @block.sync
            def _(sp):
                if not own_kv:
                    for h in range(KC):
                        sp.dma_start(wvx[:, h, :], wkvxT[h * P:(h + 1) * P, G * D:2 * G * D]).then_inc(w_direct, 16)
                for i, s in enumerate(steps):
                    if i >= 2:
                        sp.wait_ge(lo_ready, i - 1)
                    sp.dma_start(raw_view(i, s[0].shape), s[0]).then_inc(raw_in[i % 2], 16)
                if not own_kv:
                    cv = ctxT.rearrange("(h p) t -> p h t", p=P)
                    for t in range(2):
                        sp.dma_start(ctx_t[t][:], cv[:, :, t * P:(t + 1) * P]).then_inc(ctx_in[t], 16)
                    with sp.Fori(1, ROUNDS) as i:
                        for t in range(2):
                            sp.wait_ge(kv_done, WIDTH * i + UT * (t + 1) - WIDTH)
                            sp.dma_start(ctx_t[t][:], cv[:, :, bass.ds((2 * i + t) * P, P)]).then_inc(ctx_in[t], 16)

            @block.gpsimd
            def _(pool):
                nc.gpsimd.memset(pT[:], 0.0).then_inc(pT_cleared, 1)

                def convert(t, par):
                    nc.gpsimd.tensor_copy(xqf[par][:], xq8[:, Q0 * KC:(Q0 + NQ) * KC, bass.ds(t * P, P)]
                                          ).then_inc(xqf_ready, 1)

                convert(0, 0)

                def step(i, o):
                    u, soft = units(i, o, 0, 1)
                    if u.live and o % UT == 0:
                        nxt = tile_of(i, o) + 1
                        if not isinstance(nxt, int) or nxt < NT:
                            wait_unit(pool, kv_done, u.before(1))
                            convert(nxt, (o // UT + 1) % 2)
                    if soft.live:
                        pool.wait_ge(rsum_ready, soft.count(1, 1))
                        pool.wait_ge(exp_ready, soft.count(4, 4))
                        wait_unit(pool, pt_done, soft.before(1))
                        nc.gpsimd.tensor_tensor(
                            pn[:].rearrange("p (a t) -> p a t", a=4), pe_s[:].rearrange("p (a t) -> p a t", a=4),
                            rsum[:].unsqueeze(2).broadcast_to([P, 4, S]), ALU.mult).then_inc(pn_ready, 1)

                pipeline(pool, step, ROUNDS, WIDTH, 1, peel_last=True)

            @block.vector
            def _(dve):
                prep = Chain(dve, prep_done)
                prep.mark(nc.vector.tensor_scalar(lnp[:], col(f"q{pre}ln_w", 0, 2), scale, None, ALU.mult))
                prep.mark(nc.vector.reciprocal(ism[:], col("smooth", 0 if own_kv else NH, NH)))
                prep.mark(nc.vector.tensor_tensor(pscale[:], col("proj_in"), col("proj_w"), ALU.mult))
                for i, (src, sc, wsc, centred, hi, lo, plain) in enumerate(steps):
                    dve.wait_ge(raw_in[i % 2], 16 * (i // 2 + 1))
                    if i:
                        dve.wait_ge(lo_ready, i)
                    w = raw_view(i, src.shape)
                    if sc is not None:
                        prep(nc.vector.tensor_scalar(w, w, sc, wsc, ALU.mult, ALU.mult))
                    if centred:
                        n = src.shape[1] // D
                        wh = w.rearrange("p (h d) -> p h d", d=D)
                        prep(nc.vector.tensor_reduce(hsum[:, 0:n], wh, AX.X, ALU.add))
                        dst = wh if plain is None else plain.rearrange("p (h d) -> p h d", d=D)
                        ins = nc.vector.scalar_tensor_tensor(dst, hsum[:, 0:n].unsqueeze(2).broadcast_to([P, n, D]),
                                                             -1.0 / D, wh, ALU.mult, ALU.add)
                        if plain is None:
                            prep(ins)
                        else:
                            ins.then_inc(lo_ready, 1)
                    if hi is not None:
                        prep(nc.vector.tensor_copy(hi, w))
                        nc.vector.tensor_tensor(lo, w, hi.bitcast(F32), ALU.subtract).then_inc(lo_ready, 1)

                norm, catc = Chain(dve, norm_steps), Chain(dve, cat_steps)

                def step(i, o):
                    u, sm, pv, pj = units(i, o, 0, 1, 2, 3)
                    if u.live:
                        par = u.o % 2
                        norm.at(u.count(4))
                        dve.wait_ge(sqq_ready, u.count(1, 1))
                        dve.wait_ge(sqk_ready, u.count(1, 1))
                        norm(nc.vector.tensor_reduce(v6[:], sq[:].rearrange("p (h d) -> p h d", d=D), AX.X, ALU.add))
                        nc.vector.tensor_scalar(v6[:], v6[:], 1.0 / D, LN_EPS, ALU.mult, ALU.add
                                                ).then_inc(var_ready, 1)
                        dve.wait_ge(rs_ready, u.count(1, 1))
                        dve.wait_ge(var_ready, u.count(1, 1))
                        rsqrt_newton(norm, nc, r6[:], g6[:], v6[:], t6[:])
                        wait_unit(dve, t_done, u.before(1))
                        nc.vector.tensor_tensor(qn[:].rearrange("p (h d) -> p h d", d=D),
                                                q_ps[par][:].rearrange("p (h d) -> p h d", d=D),
                                                r6[:, 0:HU].unsqueeze(2).broadcast_to([P, HU, D]), ALU.mult
                                                ).then_inc(qn_ready, 1)
                        dve.wait_ge(v_ready, u.count(1, 1))
                        nc.vector.tensor_tensor(kn[:].rearrange("p (h d) -> p h d", d=D),
                                                kv_ps[par][:, 0:KW].rearrange("p (h d) -> p h d", d=D),
                                                r6[:, HU:HU + GU].unsqueeze(2).broadcast_to([P, GU, D]), ALU.mult
                                                ).then_inc(kn_ready, 1)
                    if sm.live:
                        dve.wait_ge(sc_done, sm.count(1, 1))
                        wait_unit(dve, exp_ready, sm.before(1, 4))
                        nc.vector.tensor_reduce(nmax[:], ks_ps[:, 0:4 * S].rearrange("p (a t) -> p a t", a=4), AX.X,
                                                ALU.max, negate=True).then_inc(max_ready, 1)
                    if pv.live:
                        catc.at(pv.count(4))
                        dve.wait_ge(pv_done, pv.count(1, 1))
                        wait_unit(dve, cat_ready, pv.before(1))
                        first_head = (pv.o % UT) * HU
                        nc.vector.tensor_tensor(yb[:].rearrange("p (h t) -> p h t", h=HU),
                                                po_ps[:].rearrange("p (h t) -> p h t", h=HU),
                                                ism[:, first_head:first_head + HU].unsqueeze(2).broadcast_to([P, HU, P]),
                                                ALU.mult).then_inc(y_ready, 1)
                    if sm.live:
                        dve.wait_ge(exp_ready, sm.count(4, 4))
                        wait_unit(dve, pn_ready, sm.before(1))
                        nc.vector.reciprocal(rsum[:], psum_s[:]).then_inc(rsum_ready, 1)
                    if pv.live:
                        dve.wait_ge(y_ready, pv.count(1, 1))
                        wait_unit(dve, pj_done, pv.before(2))
                        chain = catc
                        chain(nc.vector.tensor_scalar(yb[:], yb[:], FP8_MAX, -FP8_MAX, ALU.min, ALU.max))
                        chain(nc.vector.tensor_scalar(eb[:].bitcast(U16), yb[:].bitcast(U16), 0x7F80, None,
                                                      ALU.bitwise_and))
                        chain(nc.vector.tensor_scalar(mb[:], eb[:], 2.0 ** -6, 1.5 * 2.0 ** 4, ALU.max, ALU.mult))
                        chain(nc.vector.tensor_tensor(yb[:], yb[:], mb[:], ALU.add))
                        nc.vector.tensor_tensor(cat[pv.o % 2][:], yb[:], mb[:], ALU.subtract).then_inc(cat_ready, 1)
                    if pj.live and pj.o % UT == UT - 1:
                        t = tile_of(i, o) - (1 if pj.o > o or o // UT != pj.o // UT else 0)
                        dve.wait_ge(pj_done, pj.count(1, 1))
                        xt = x_res[:, bass.ds(t, 1), :].rearrange("p a c -> p (a c)")
                        nc.vector.scalar_tensor_tensor(xt, pj_ps[:, 0:C], pscale[:], xt, ALU.mult, ALU.add
                                                       ).then_inc(x_added, 1)

                pipeline(dve, step, ROUNDS, WIDTH, 3)

            @block.scalar
            def _(act):
                nc.scalar.preload_act_table_set(LN_EXP_SET)
                act.wait_ge(prep_done, 3)
                act.wait_ge(pT_cleared, 1)
                chain = Chain(act, act_steps)

                def step(i, o):
                    u, sm, pv = units(i, o, 0, 1, 2)
                    if u.live:
                        par = u.o % 2
                        act.wait_ge(q_done, u.count(1, 1))
                        wait_unit(act, var_ready, u.before(1))
                        nc.scalar.activation(sq[:, 0:QW], q_ps[par][:], ACT.Square).then_inc(sqq_ready, 1)
                    if sm.live:
                        act.wait_ge(t_done, sm.count(1, 1))
                        nc.scalar.activation(kT[:], ks_ps[:, 0:KW], ACT.Identity, scale=col(f"k{pre}ln_w"),
                                             bias=col(f"k{pre}ln_b")).then_inc(kT_ready, 1)
                        nc.scalar.activation(qT[:], qT_ps[:], ACT.Identity, scale=lnp[:, 0:1], bias=lnp[:, 1:2]
                                             ).then_inc(qT_ready, 1)
                    if u.live:
                        par = u.o % 2
                        act.wait_ge(kv_done, u.count(1, 1))
                        nc.scalar.activation(sq[:, QW:QW + KW], kv_ps[par][:, 0:KW], ACT.Square).then_inc(sqk_ready, 1)
                        wait_unit(act, pv_done, u.before(4))
                        nc.scalar.activation(v_s[u.o % 4][:], kv_ps[par][:, KW:2 * KW], ACT.Copy).then_inc(v_ready, 1)
                        chain.at(u.count(1))
                        act.wait_ge(var_ready, u.count(1, 1))
                        chain(nc.scalar.activation(l6[:], v6[:], ACT.Ln))
                        wait_unit(act, qn_ready, u.before(1))
                        nc.scalar.activation(g6[:], l6[:], ACT.Exp, scale=-0.5).then_inc(rs_ready, 1)
                    if pv.live:
                        act.wait_ge(pt_done, pv.count(1, 1))
                        for b in range(2):
                            rows = slice(b * S, (b + 1) * S)
                            nc.scalar.activation(pT[rows, :, :, b, :], po_ps[rows, 0:GU * P].rearrange(
                                "p (g h s) -> p g h s", g=GU, h=HPG), ACT.Copy).then_inc(pT_ready, 1)
                    if sm.live:
                        act.wait_ge(max_ready, sm.count(1, 1))
                        wait_unit(act, pn_ready, sm.before(1))
                        wait_unit(act, rsum_ready, sm.before(1))
                        for a in range(4):
                            nc.scalar.activation(pe_s[:, a * S:(a + 1) * S], ks_ps[:, a * S:(a + 1) * S], ACT.Exp,
                                                 bias=nmax[:, a:a + 1], accum_out=psum_s[:, a:a + 1]
                                                 ).then_inc(exp_ready, 1)

                pipeline(act, step, ROUNDS, WIDTH, 2)

            @block.tensor
            def _(pe):
                pe.wait_ge(lo_ready, len(steps))
                if not own_kv:
                    pe.wait_ge(w_direct, 16 * KC)

                def split_product(out_ap, x_col, w_pair, c0, c1):
                    n = 0
                    for h in range(KC):
                        for part in range(2):
                            last = nc.tensor.matmul(out_ap, x_col(h), w_pair[part][:, h, c0:c1], start=(n == 0),
                                                    stop=(n == 2 * KC - 1))
                            n += 1
                    return last

                def step(i, o):
                    u, t, pv, pj = units(i, o, 0, 1, 2, 3)
                    if u.live:
                        par, gp, tp = u.o % 2, u.o % UT, (u.o // UT) % 2
                        if gp == 0:
                            pe.wait_ge(xqf_ready, tile_of(i, o) + 1)
                        wait_unit(pe, qn_ready, u.before(2))
                        split_product(q_ps[par][:], lambda h: xqf[tp][:, h, :], wq, gp * QW, (gp + 1) * QW
                                      ).then_inc(q_done, 1)
                    if t.live:
                        pe.wait_ge(qn_ready, t.count(1, 1))
                        pe.wait_ge(kn_ready, t.count(1, 1))
                        wait_unit(pe, qT_ready, t.before(1))
                        wait_unit(pe, exp_ready, t.before(1, 4))
                        for a in range(HU):
                            g, h = divmod(a, HPG)
                            qcols = qT_ps[:].rearrange("p (g b h s) -> p g b h s", g=GU, b=2, h=HPG)[:, g, :, h, :]
                            nc.tensor.transpose(qcols, qn[:, a * P:(a + 1) * P], ident[:])
                        for a in range(GU):
                            last = nc.tensor.transpose(ks_ps[:, a * P:(a + 1) * P], kn[:, a * P:(a + 1) * P], ident[:])
                        last.then_inc(t_done, 1)
                    if u.live:
                        wait_unit(pe, kn_ready, u.before(2))
                        if own_kv:
                            split_product(kv_ps[par][:, 0:KW], lambda h: xqf[tp][:, KC + h, :], wk, gp * KW, (gp + 1) * KW)
                            last = split_product(kv_ps[par][:, KW:2 * KW], lambda h: xqf[tp][:, 2 * KC + h, :], wv,
                                                 gp * KW, (gp + 1) * KW)
                        else:
                            if gp == 0:
                                pe.wait_ge(ctx_in[tp], 16 * (i + 1))
                            for c, w in ((0, wkx), (KW, wvx)):
                                for h in range(KC):
                                    last = nc.tensor.matmul(kv_ps[par][:, c:c + KW], ctx_t[tp][:, h, :],
                                                            w[:, h, gp * KW:(gp + 1) * KW], start=(h == 0),
                                                            stop=(h == KC - 1))
                        last.then_inc(kv_done, 1)
                    if pv.live:
                        pe.wait_ge(pn_ready, pv.count(1, 1))
                        wait_unit(pe, y_ready, pv.before(1))
                        for g in range(GU):
                            last = nc.tensor.transpose(po_ps[:, g * P:(g + 1) * P], pn[:, g * P:(g + 1) * P], ident[:])
                        last.then_inc(pt_done, 1)
                    if pj.live:
                        gpj = pj.o % UT
                        pe.wait_ge(cat_ready, pj.count(1, 1))
                        if gpj == 0 and not (pj.static and pj.n < UT):
                            pe.wait_ge(x_added, tile_of(i, o) - (1 if pj.o > o or o // UT != pj.o // UT else 0))
                        for a in range(HU):
                            for part in range(2):
                                last = nc.tensor.matmul(pj_ps[:, 0:C], cat[pj.o % 2][:, a * P:(a + 1) * P],
                                                        wp[part][:, gpj * HU + a, :],
                                                        start=(gpj == 0 and a == 0 and part == 0),
                                                        stop=(gpj == UT - 1 and a == HU - 1 and part == 1))
                        last.then_inc(pj_done, 1)
                    if t.live:
                        pe.wait_ge(qT_ready, t.count(1, 1))
                        pe.wait_ge(kT_ready, t.count(1, 1))
                        for g in range(GU):
                            for b in range(2):
                                a = g * 2 + b
                                last = nc.tensor.matmul(ks_ps[:, a * S:(a + 1) * S], qT[:, a * P:(a + 1) * P],
                                                        kT[:, g * P + b * S:g * P + (b + 1) * S], start=True, stop=True)
                        last.then_inc(sc_done, 1)
                    if pv.live:
                        pe.wait_ge(pT_ready, pv.count(2, 2))
                        for g in range(GU):
                            last = nc.tensor.matmul(po_ps[:, g * HPG * P:(g + 1) * HPG * P],
                                                    v_s[pv.o % 4][:, g * D:(g + 1) * D],
                                                    pT[:, g].rearrange("p h b s -> p (h b s)"), start=True, stop=True)
                        last.then_inc(pv_done, 1)

                pipeline(pe, step, ROUNDS, WIDTH, 3)



def routed_ffn_stage(k, routerT, fw1T, fw2T, fb2, out):
    nc, sem, x_res, ident, col = k["nc"], k["sem"], k["x_res"], k["ident"], k["col"]
    GT = 4
    NG = NT // GT
    W = GT * P
    FC = FF // P
    N2 = 2 * NT
    with ExitStack() as own:
        def sb(name, shape, dt=F32):
            return own.enter_context(nc.sbuf_tensor(name, shape, dt))

        def psum(name, shape, dt=F32):
            return own.enter_context(nc.psum_tensor(name, shape, dt))

        z = sb("rf_z", [P, NT, C])
        zT = sb("rf_zT", [P, KC, TOK])
        rw = sb("rf_rw", [P, KC, E])
        w1, w2 = sb("rf_w1", [P, KC, FF]), sb("rf_w2", [P, FC, C])
        b2 = sb("rf_b2", [P, C])
        tri = sb("rf_tri", [P, P])
        iota8 = sb("rf_iota8", [P, NT, E])
        first = sb("rf_first", [P, E, N2])
        pr, tmp = sb("rf_pr", [P, NT, E]), sb("rf_tmp", [P, NT, E])
        oh = sb("rf_oh", [P, N2, E])
        top = sb("rf_top", [P, N2])
        low = sb("rf_low", [P, NT])
        tot, acc = sb("rf_tot", [P, E, N2]), sb("rf_acc", [P, E, N2])
        cnt = sb("rf_cnt", [P, N2, E])
        pos = sb("rf_pos", [P, N2])
        gate = sb("rf_gate", [P, NT])
        hT = [sb(f"rf_hT{i}", [P, FC, W]) for i in range(2)]
        t_s = sb("rf_t", [P, C])
        zT_ps = [psum(f"rf_zT_ps{i}", [P, 512]) for i in range(2)]
        h_ps = [psum(f"rf_h_ps{i}", [P, 512]) for i in range(3)]
        y_ps = [psum(f"rf_y_ps{i}", [P, 512]) for i in range(2)]
        lg_ps = psum("rf_lg_ps", [P, 512])

        w_in, b2_in, rw_in = sem("rf_w_in"), sem("rf_b2_in"), sem("rf_rw_in")
        consts = sem("rf_consts")
        var_ready, rs_ready = sem("rf_var_ready"), sem("rf_rs_ready")
        dve_done, act_done = sem("rf_dve_done"), sem("rf_act_done")
        z_ready, zTp_ready, zT_ready = sem("rf_z_ready"), sem("rf_zTp_ready"), sem("rf_zT_ready")
        lg_ready, sub_ready, exp_ready = sem("rf_lg_ready"), sem("rf_sub_ready"), sem("rf_exp_ready")
        oh_ready, cnt_ready = sem("rf_oh_ready"), sem("rf_cnt_ready")
        h_ready, hT_ready, y_ready, x_added = sem("rf_h_ready"), sem("rf_hT_ready"), sem("rf_y_ready"), sem("rf_x_added")
        counts_read, out_done = sem("rf_counts_read"), sem("out_done")

        with nc.Block() as block:
            @block.sync
            def _(sp):
                sp.dma_start(rw[:], routerT.rearrange("(h p) n -> p h n", p=P)).then_inc(rw_in, 16)
                sp.dma_start(w1[:], fw1T.rearrange("(h p) n -> p h n", p=P)).then_inc(w_in, 16)
                sp.dma_start(w2[:], fw2T.rearrange("(h p) n -> p h n", p=P)).then_inc(w_in, 16)
                sp.dma_start(b2[:], fb2.broadcast_to([P, C])).then_inc(b2_in, 16)
                outr = out.rearrange("(j p) c -> p j c", p=P)
                for j in range(0, NT, 2):
                    sp.wait_ge(x_added, j + 2)
                    sp.dma_start(outr[:, j:j + 2, :], x_res[:, j:j + 2, :]).then_inc(out_done, 16)
                sp.wait_ge(out_done, 16 * (NT // 2))

            @block.gpsimd
            def _(pool):
                nc.gpsimd.memset(tri[:], 1.0).then_inc(consts, 1)
                nc.gpsimd.memset(first[:], 1.0).then_inc(consts, 1)
                for e in range(E):
                    nc.gpsimd.memset(iota8[:, :, e], float(e - E)).then_inc(consts, 1)
                pool.wait_ge(consts, 2 + E)
                nc.gpsimd.affine_select(out=tri[:], in_=tri[:], compare_op=ALU.is_ge, fill=0.0, base=0,
                                        pattern=[[1, P]], channel_multiplier=-1).then_inc(consts, 1)
                nc.gpsimd.memset(first[:, :, 0], 0.0).then_inc(consts, 1)

            @block.vector
            def _(dve):
                chain = Chain(dve, dve_done)
                for j in range(NT):
                    chain.mark(nc.vector.bn_stats(k["stat6"][:, j, :], x_res[:, j, :]))
                chain.settle()
                dve_mean_var(k, chain, var_ready)
                dve.wait_ge(rs_ready, 1)
                dve.wait_ge(var_ready, 1)
                rsqrt_newton(chain, nc, k["rstd"][:], k["rs0"][:], k["var"][:], k["st"][0][:])
                for j in range(NT):
                    nc.vector.tensor_scalar(z[:, j, :], x_res[:, j, :], k["mean"][:, j:j + 1],
                                            k["rstd"][:, j:j + 1], ALU.subtract, ALU.mult).then_inc(z_ready, 1)

                def wide(v):
                    return v.unsqueeze(2).broadcast_to([P, NT, E])

                dve.wait_ge(lg_ready, 1)
                lg = lg_ps[:, 0:NT * E].rearrange("p (j e) -> p j e", e=E)
                chain(nc.vector.tensor_reduce(low[:], lg, AX.X, ALU.max))
                nc.vector.tensor_tensor(tmp[:], lg, wide(low[:]), ALU.subtract).then_inc(sub_ready, 1)
                dve.wait_ge(exp_ready, 1)
                chain(nc.vector.tensor_reduce(low[:], pr[:], AX.X, ALU.add))
                chain(nc.vector.reciprocal(low[:], low[:]))
                chain(nc.vector.tensor_tensor(pr[:], pr[:], wide(low[:]), ALU.mult))
                dve.wait_ge(consts, 4 + E)
                for c in range(2):
                    best = top[:, c * NT:(c + 1) * NT]
                    one = oh[:, c * NT:(c + 1) * NT, :]
                    chain(nc.vector.tensor_reduce(best, pr[:], AX.X, ALU.max))
                    chain(nc.vector.tensor_tensor(tmp[:], pr[:], wide(best), ALU.is_equal))
                    chain(nc.vector.tensor_tensor(tmp[:], tmp[:], iota8[:], ALU.mult))
                    chain(nc.vector.tensor_reduce(low[:], tmp[:], AX.X, ALU.min))
                    nc.vector.tensor_tensor(one, iota8[:], wide(low[:]), ALU.is_equal).then_inc(oh_ready, 1)
                    dve.wait_ge(oh_ready, c + 1)
                    if c == 0:
                        chain(nc.vector.scalar_tensor_tensor(pr[:], one, -2.0, pr[:], ALU.mult, ALU.add))
                dve.wait_ge(cnt_ready, 2)
                inside = h_ps[0][:, 0:N2 * E].rearrange("p (n e) -> p n e", e=E)
                totals = h_ps[1][:, 0:N2 * E].rearrange("p (n e) -> p e n", e=E)
                chain(nc.vector.tensor_copy(tot[:], totals))
                chain(nc.vector.tensor_tensor_scan(acc[:].rearrange("p e n -> p (e n)"),
                                                   first[:].rearrange("p e n -> p (e n)"),
                                                   tot[:].rearrange("p e n -> p (e n)"), 0.0, ALU.mult, ALU.add))
                chain(nc.vector.tensor_tensor(acc[:], acc[:], tot[:], ALU.subtract))
                nc.vector.tensor_tensor(cnt[:], inside, acc[:].rearrange("p e n -> p n e"), ALU.add
                                        ).then_inc(counts_read, 1)
                dve.wait_ge(counts_read, 1)
                chain(nc.vector.tensor_tensor(cnt[:], cnt[:], oh[:], ALU.mult))
                chain(nc.vector.tensor_reduce(pos[:], cnt[:], AX.X, ALU.add))
                chain(nc.vector.tensor_scalar(pos[:], pos[:], float(CAP), None, ALU.is_le))
                chain(nc.vector.tensor_tensor(pos[:], pos[:], top[:], ALU.mult))
                chain(nc.vector.tensor_tensor(gate[:], pos[:, 0:NT], pos[:, NT:N2], ALU.add))
                dve.wait_ge(b2_in, 16)
                for j in range(NT):
                    dve.wait_ge(y_ready, j + 1)
                    if j:
                        dve.wait_ge(x_added, j)
                    chain(nc.vector.tensor_tensor(t_s[:], y_ps[j % 2][:, 0:C], b2[:], ALU.add))
                    nc.vector.scalar_tensor_tensor(x_res[:, j, :], t_s[:], gate[:, j:j + 1], x_res[:, j, :],
                                                   ALU.mult, ALU.add).then_inc(x_added, 1)

            @block.scalar
            def _(act):
                chain = Chain(act, act_done)
                nc.scalar.preload_act_table_set(LN_EXP_SET)
                act_rsqrt(act, nc, k["rs0"][:], k["var"][:], k["st"][2][:], var_ready, 1, chain, rs_ready)
                for n in range(NG * KC):
                    g, h = divmod(n, KC)
                    act.wait_ge(zTp_ready, n + 1)
                    nc.scalar.activation(zT[:, h, g * W:(g + 1) * W], zT_ps[n % 2][:], ACT.Copy).then_inc(zT_ready, 1)
                act.wait_ge(sub_ready, 1)
                nc.scalar.activation(pr[:], tmp[:], ACT.Exp).then_inc(exp_ready, 1)
                for n in range(NG * FC):
                    g, f = divmod(n, FC)
                    act.wait_ge(h_ready, n + 1)
                    if g >= 2:
                        act.wait_ge(y_ready, GT * (g - 1))
                    nc.scalar.activation(hT[g % 2][:, f, :], h_ps[n % 3][:], ACT.Gelu, bias=col("b1", f)
                                         ).then_inc(hT_ready, 1)

            @block.tensor
            def _(pe):
                for n in range(NG * KC):
                    g, h = divmod(n, KC)
                    pe.wait_ge(z_ready, GT * (g + 1))
                    if n >= 2:
                        pe.wait_ge(zT_ready, n - 1)
                    for j in range(GT):
                        last = nc.tensor.transpose(zT_ps[n % 2][:, j * P:(j + 1) * P],
                                                   z[:, GT * g + j, h * P:(h + 1) * P], ident[:])
                    last.then_inc(zTp_ready, 1)
                pe.wait_ge(zT_ready, NG * KC)
                pe.wait_ge(rw_in, 16)
                for j in range(NT):
                    for h in range(KC):
                        last = nc.tensor.matmul(lg_ps[:, j * E:(j + 1) * E], zT[:, h, j * P:(j + 1) * P], rw[:, h, :],
                                                start=(h == 0), stop=(h == KC - 1))
                last.then_inc(lg_ready, 1)
                pe.wait_ge(consts, 4 + E)
                pe.wait_ge(oh_ready, 2)
                ohf = oh[:].rearrange("p n e -> p (n e)")
                nc.tensor.matmul(h_ps[0][:, 0:N2 * E], tri[:], ohf, start=True, stop=True).then_inc(cnt_ready, 1)
                nc.tensor.matmul(h_ps[1][:, 0:N2 * E], k["ones"][:], ohf, start=True, stop=True).then_inc(cnt_ready, 1)
                pe.wait_ge(w_in, 32)
                pe.wait_ge(counts_read, 1)

                def second(g):
                    for j in range(GT):
                        n = GT * g + j
                        if n >= 2:
                            pe.wait_ge(x_added, n - 1)
                        for f in range(FC):
                            last = nc.tensor.matmul(y_ps[n % 2][:, 0:C], hT[g % 2][:, f, j * P:(j + 1) * P], w2[:, f, :],
                                                    start=(f == 0), stop=(f == FC - 1))
                        last.then_inc(y_ready, 1)

                for g in range(NG):
                    for f in range(FC):
                        n = g * FC + f
                        if n >= 3:
                            pe.wait_ge(hT_ready, n - 2)
                        for h in range(KC):
                            last = nc.tensor.matmul(h_ps[n % 3][:], w1[:, h, f * P:(f + 1) * P],
                                                    zT[:, h, g * W:(g + 1) * W], start=(h == 0), stop=(h == KC - 1))
                        last.then_inc(h_ready, 1)
                    if g:
                        pe.wait_ge(hT_ready, FC * g)
                        second(g - 1)
                pe.wait_ge(hT_ready, FC * NG)
                second(NG - 1)



def kernel(**inputs):
    import numpy as np
    import concourse.bacc as bacc
    from concourse.bass_utils import run_bass_kernel_spmd

    def get(name):
        return np.asarray(inputs[name])

    def columns(v, n):
        return v.reshape(n, P).T

    def everywhere(v):
        return np.broadcast_to(v.reshape(1, 1), (P, 1))

    packed = {
        "w": columns(get("L0_xattn_w"), KC), "u": columns(get("L0_xattn_u"), KC),
        "ln_w": columns(get("L1_xattn_ln_w"), KC), "ln_b": columns(get("L1_xattn_ln_b"), KC),
        "sq": columns(get("L1_xattn_q_in_scale"), KC), "sk": columns(get("L1_xattn_k_in_scale"), KC),
        "sv": columns(get("L1_xattn_v_in_scale"), KC), "sqx": columns(get("L1_xattn_qx_in_scale"), KC),
        "smooth": columns(get("L1_xattn_proj_smooth"), 2 * NH), "b1": columns(get("L1_ffn_b1"), FF // P),
        "wq_s": everywhere(get("L1_xattn_wq_scale")), "wk_s": everywhere(get("L1_xattn_wk_scale")),
        "wv_s": everywhere(get("L1_xattn_wv_scale")), "wqx_s": everywhere(get("L1_xattn_wqx_scale")),
        "proj_in": everywhere(get("L1_xattn_proj_in_scale")), "proj_w": everywhere(get("L1_xattn_proj_w_scale")),
    }
    for name in ("qln_w", "qln_b", "kln_w", "kln_b", "qxln_w", "qxln_b", "kxln_w", "kxln_b"):
        packed[name] = columns(get(f"L1_xattn_{name}"), 1)
    arrays = {
        "x": get("x").reshape(TOK, C),
        "ctxT": get("ctx_2048").reshape(TOK, C).T,
        "params": np.concatenate([packed[name] for name in PARAM_COLS], axis=1),
        "w1T": get("L0_ffn_w1").T, "w3T": get("L0_ffn_w3").T, "w2T": get("L0_ffn_w2").T,
        "wqT": get("L1_xattn_wq").T, "wkT": get("L1_xattn_wk").T, "wvT": get("L1_xattn_wv").T,
        "wqxT": get("L1_xattn_wqx").T, "wkvxT": get("L1_xattn_w_kv_x").T, "wprojT": get("L1_xattn_wproj").T,
        "routerT": get("L1_ffn_router_w").T, "fw1T": get("L1_ffn_w1").T, "fw2T": get("L1_ffn_w2").T,
        "fb2": get("L1_ffn_b2").reshape(1, C),
    }
    nc = bacc.Bacc("TRN2", target_bir_lowering=False, num_devices=1)
    args, feed = [], {}
    for name, a in arrays.items():
        a = np.ascontiguousarray(a)
        feed[f"in_{name}"] = a
        args.append(nc.dram_tensor(f"in_{name}", a.shape, mybir.dt.from_np(a.dtype), kind="ExternalInput").ap())
    args.append(nc.dram_tensor("out_x", (TOK, C), F32, kind="ExternalOutput").ap())
    build_program(nc, *args)
    r = run_bass_kernel_spmd(nc, [feed], core_ids=[0])
    return r.results[0]["out_x"].reshape(B, S, C)
```

```python
from contextlib import ExitStack

import concourse.bass as bass
from concourse import mybir

F32 = mybir.dt.float32
F32R = mybir.dt.float32r
BF16 = mybir.dt.bfloat16
U16 = mybir.dt.uint16
U32 = mybir.dt.uint32
ALU = mybir.AluOpType
ACT = mybir.ActivationFunctionType
AX = mybir.AxisListType

P = 128
B, S, C = 32, 64, 256
TOK = B * S
NT = TOK // P
KC = C // P
HID = 704
NH, G, D = 16, 8, 128
HPG = NH // G
E, CAP, FF = 8, 64, 1024
LN_EPS = 1e-5
QUANT_EPS = 1e-5
FP8_MAX = 448.0
ROUND32 = 1.5 * 2.0 ** 23
NEG_BIG = -1e38
LN_EXP_SET = "natural_log_exp_and_others"

PARAM_COLS = {}
for _name, _n in (("w", KC), ("u", KC), ("ln_w", KC), ("ln_b", KC), ("sq", KC), ("sk", KC), ("sv", KC),
                  ("sqx", KC), ("qln_w", 1), ("qln_b", 1), ("kln_w", 1), ("kln_b", 1), ("qxln_w", 1),
                  ("qxln_b", 1), ("kxln_w", 1), ("kxln_b", 1), ("smooth", 2 * NH), ("b1", FF // P),
                  ("wq_s", 1), ("wk_s", 1), ("wv_s", 1), ("wqx_s", 1), ("proj_in", 1), ("proj_w", 1)):
    PARAM_COLS[_name] = (sum(n for _, n in PARAM_COLS.values()), _n)
N_PARAM = sum(n for _, n in PARAM_COLS.values())


class Chain:

    def __init__(self, eng, sem):
        self.eng, self.sem, self.base, self.n = eng, sem, 0, 0

    def at(self, base):
        self.base, self.n = base, 0

    def mark(self, ins):
        ins.then_inc(self.sem, 1)
        self.n += 1

    def settle(self):
        self.eng.wait_ge(self.sem, self.base + self.n)

    def __call__(self, ins):
        self.mark(ins)
        self.settle()


def build_program(nc, x, ctxT, params, w1T, w3T, w2T, wqT, wkT, wvT, wqxT, wkvxT, wprojT, routerT,
                  fw1T, fw2T, fb2, out):
    ctx = ExitStack()
    with ctx:
        def sb(name, shape, dt=F32, stack=ctx):
            return stack.enter_context(nc.sbuf_tensor(name, shape, dt))

        def sem(name):
            return ctx.enter_context(nc.semaphore(name))

        x_res = sb("x_res", [P, NT, C])
        par = sb("par", [P, N_PARAM])
        ident = sb("ident", [P, P])
        ones = sb("ones", [P, P])
        stat6 = sb("stat6", [P, NT, 6])
        mean = sb("mean", [P, NT])
        var = sb("var", [P, NT])
        rstd = sb("rstd", [P, NT])
        st_a = sb("st_a", [P, NT])
        st_b = sb("st_b", [P, NT])
        st_c = sb("st_c", [P, NT])
        rs0 = sb("rs0", [P, NT])

        def col(name, i=0, n=1):
            at, _ = PARAM_COLS[name]
            return par[:, at + i:at + i + n]

        tok = dict(nc=nc, ctx=ctx, sb=sb, sem=sem, x_res=x_res, par=par, col=col, ident=ident, ones=ones,
                   ln_var_ready=sem("ln_var_ready"), ln_rs_ready=sem("ln_rs_ready"), stat6=stat6, mean=mean, var=var, rstd=rstd, st=(st_a, st_b, st_c), rs0=rs0)
        wkv_stage(tok, x, ctxT, params)
        ternary_ffn_stage(tok, w1T, w3T, w2T)
        with ExitStack() as held:
            xq8 = sb("xq8", [P, 4 * KC, TOK], BF16, held)
            ln_quant_stage(tok, xq8)
            attention_stage(tok, "self", xq8, (wqT, wkT, wvT), wprojT, ctxT)
            attention_stage(tok, "cross", xq8, (wqxT, wkvxT), wprojT, ctxT)
        routed_ffn_stage(tok, routerT, fw1T, fw2T, fb2, out)


LN_BEFORE = {"wkv": 0, "ternary": 1, "quant": 2, "routed": 4}



def rsqrt_newton(dve_chain, nc, y, y0, v, t):
    dve_chain(nc.vector.scalar_tensor_tensor(t, y0, -0.5, y0, ALU.mult, ALU.mult))
    dve_chain(nc.vector.tensor_tensor(t, t, v, ALU.mult))
    dve_chain(nc.vector.scalar_tensor_tensor(y, t, 1.5, y0, ALU.add, ALU.mult))


def dve_mean_var(k, chain, var_ready):
    nc, st6, (a, b, c) = k["nc"], k["stat6"], k["st"]
    me, m2e, mo, m2o = (st6[:, :, i] for i in (1, 2, 4, 5))
    chain.mark(nc.vector.tensor_tensor(a[:], me, mo, ALU.subtract))
    chain.mark(nc.vector.tensor_tensor(b[:], m2e, m2o, ALU.add))
    chain(nc.vector.tensor_tensor(c[:], me, mo, ALU.add))
    chain.mark(nc.vector.tensor_tensor(a[:], a[:], a[:], ALU.mult))
    chain.mark(nc.vector.tensor_scalar(b[:], b[:], 1.0 / C, LN_EPS, ALU.mult, ALU.add))
    chain(nc.vector.tensor_scalar(k["mean"][:], c[:], 0.5, None, ALU.mult))
    nc.vector.scalar_tensor_tensor(k["var"][:], a[:], 0.25, b[:], ALU.mult, ALU.add).then_inc(var_ready, 1)


def act_rsqrt(act, nc, dst, v, tmp, var_ready, count, act_chain, rs_ready):
    act.wait_ge(var_ready, count)
    act_chain(nc.scalar.activation(tmp, v, ACT.Ln))
    nc.scalar.activation(dst, tmp, ACT.Exp, scale=-0.5).then_inc(rs_ready, 1)



def wkv_stage(k, x, ctxT, params):
    nc, sem, x_res, col, ident = k["nc"], k["sem"], k["x_res"], k["col"], k["ident"]
    BQ = B // 2
    L = S + 1
    CHUNKS = [(h, q) for h in range(KC) for q in range(2)]
    with ExitStack() as own:
        def sb(name, shape, dt=F32):
            return own.enter_context(nc.sbuf_tensor(name, shape, dt))

        def psum(name, shape, dt=F32):
            return own.enter_context(nc.psum_tensor(name, shape, dt))

        z = sb("wkv_z", [P, NT, C])
        vT = sb("vT", [P, KC, B, S])
        k65 = sb("k65", [P, KC, B, L])
        w65 = sb("w65", [P, KC, BQ, L])
        yT = sb("yT", [P, KC, B, S])
        names = "o A2 E2 E2v p q"
        buf = {n: [sb(f"{n}{i}", [P, BQ, L]) for i in range(2)] for n in names.split()}
        for n in "d A E Ev Ap Aq".split():
            buf[n] = [sb(f"{n}_{i}", [P, BQ, S]) for i in range(2)]
        zT_ps = [psum(f"zT_ps{i}", [P, 512]) for i in range(4)]
        y_ps = [psum(f"y_ps{i}", [P, 512]) for i in range(2)]

        x_in = [sem(f"x_in{i}") for i in range(4)]
        par_in, v_in = sem("par_in"), [sem(f"v_in{i}") for i in range(KC)]
        consts, fills = sem("consts"), sem("wkv_fills")
        var_ready, rs_ready = k["ln_var_ready"], k["ln_rs_ready"]
        dve_done, act_done, pool_done = sem("wkv_dve_done"), sem("wkv_act_done"), sem("wkv_pool_done")
        z_ready, zT_ready, k_ready = sem("wkv_z_ready"), sem("wkv_zT_ready"), sem("wkv_k_ready")
        gaps_ready, exps_ready = sem("wkv_gaps_ready"), sem("wkv_exps_ready")
        E2v_ready, Ev_ready = sem("wkv_E2v_ready"), sem("wkv_Ev_ready")
        pq_ready, Apq_ready = sem("wkv_pq_ready"), sem("wkv_Apq_ready")
        den_ready, rcp_ready = sem("wkv_den_ready"), sem("wkv_rcp_ready")
        y_ready, yt_ready, x_added = sem("wkv_y_ready"), sem("wkv_yt_ready"), sem("wkv_x_added")

        with nc.Block() as block:
            @block.sync
            def _(sp):
                sp.dma_start(k["par"][:], params).then_inc(par_in, 16)
                xr = x.rearrange("(j p) c -> p j c", p=P)
                for i in range(4):
                    sp.dma_start(x_res[:, 4 * i:4 * i + 4, :], xr[:, 4 * i:4 * i + 4, :]).then_inc(x_in[i], 16)
                for h in range(KC):
                    sp.dma_start(vT[:, h, :, :], ctxT[h * P:(h + 1) * P, :].rearrange("p (b s) -> p b s", s=S)
                                 ).then_inc(v_in[h], 16)

            @block.gpsimd
            def _(pool):
                nc.gpsimd.memset(ident[:], 0.0).then_inc(consts, 1)
                nc.gpsimd.memset(k["ones"][:], 1.0).then_inc(consts, 1)
                pool.wait_ge(consts, 2)
                nc.gpsimd.affine_select(out=ident[:], in_=ident[:], compare_op=ALU.not_equal, fill=1.0, base=0,
                                        pattern=[[-1, P]], channel_multiplier=1).then_inc(consts, 1)
                nc.gpsimd.memset(k65[:, :, :, 0], NEG_BIG).then_inc(fills, 1)
                nc.gpsimd.memset(w65[:], 0.0).then_inc(fills, 1)
                for n in ("A2", "E2", "E2v"):
                    for i in range(2):
                        nc.gpsimd.memset(buf[n][i][:, :, 0], 0.0).then_inc(fills, 1)
                for c, (h, q) in enumerate(CHUNKS):
                    i = c % 2
                    v = vT[:, h, BQ * q:BQ * (q + 1), :]
                    if c == 0:
                        pool.wait_ge(fills, 8)
                    if q == 0:
                        pool.wait_ge(v_in[h], 16)
                    pool.wait_ge(exps_ready, 4 * c + 2)
                    if c >= 2:
                        pool.wait_ge(pq_ready, 2 * (c - 1))
                    nc.gpsimd.tensor_tensor(buf["E2v"][i][:, :, 1:], buf["E2"][i][:, :, 1:], v, ALU.mult
                                            ).then_inc(E2v_ready, 1)
                    pool.wait_ge(exps_ready, 4 * c + 4)
                    nc.gpsimd.tensor_tensor(buf["Ev"][i][:], buf["E"][i][:], v, ALU.mult).then_inc(Ev_ready, 1)
                    pool.wait_ge(pq_ready, 2 * c + 1)
                    nc.gpsimd.tensor_tensor(buf["Ap"][i][:], buf["A"][i][:], buf["p"][i][:, :, 0:S], ALU.mult
                                            ).then_inc(Apq_ready, 1)
                    pool.wait_ge(pq_ready, 2 * c + 2)
                    nc.gpsimd.tensor_tensor(buf["Aq"][i][:], buf["A"][i][:], buf["q"][i][:, :, 0:S], ALU.mult
                                            ).then_inc(Apq_ready, 1)

            @block.vector
            def _(dve):
                chain = Chain(dve, dve_done)
                for j in range(NT):
                    if j % 4 == 0:
                        dve.wait_ge(x_in[j // 4], 16)
                    chain.mark(nc.vector.bn_stats(k["stat6"][:, j, :], x_res[:, j, :]))
                chain.settle()
                dve_mean_var(k, chain, var_ready)
                dve.wait_ge(rs_ready, LN_BEFORE["wkv"] + 1)
                dve.wait_ge(var_ready, LN_BEFORE["wkv"] + 1)
                rsqrt_newton(chain, nc, k["rstd"][:], k["rs0"][:], k["var"][:], k["st"][0][:])
                for j in range(NT):
                    nc.vector.tensor_scalar(z[:, j, :], x_res[:, j, :], k["mean"][:, j:j + 1],
                                            k["rstd"][:, j:j + 1], ALU.subtract, ALU.mult).then_inc(z_ready, 1)
                dve.wait_ge(par_in, 16)
                dve.wait_ge(fills, 8)
                for h in range(KC):
                    chain.mark(nc.vector.tensor_scalar(w65[:, h, :, 1:], w65[:, h, :, 1:], col("w", h), None, ALU.add))
                    chain.mark(nc.vector.memset(w65[:, h, :, 0], NEG_BIG))

                def flat(t):
                    return t.rearrange("p b l -> p (b l)")

                def gaps(c):
                    h, q = CHUNKS[c]
                    i = c % 2
                    kk = k65[:, h, BQ * q:BQ * (q + 1), :]
                    o = buf["o"][i]
                    if q == 0:
                        dve.wait_ge(k_ready, 4 * h + 4)
                    chain.settle()
                    chain(nc.vector.tensor_tensor_scan(flat(o[:]), flat(w65[:, h]), flat(kk), NEG_BIG,
                                                       ALU.add, ALU.max))
                    if c >= 2:
                        dve.wait_ge(E2v_ready, c - 1)
                        dve.wait_ge(Apq_ready, 2 * (c - 1))
                        dve.wait_ge(Ev_ready, c - 1)
                    nc.vector.tensor_tensor(buf["E2"][i][:, :, 1:], kk[:, :, 1:], o[:, :, 1:], ALU.subtract
                                            ).then_inc(gaps_ready, 1)
                    nc.vector.scalar_tensor_tensor(buf["A2"][i][:, :, 1:], o[:, :, 0:S], col("w", h), o[:, :, 1:],
                                                   ALU.add, ALU.subtract).then_inc(gaps_ready, 1)
                    nc.vector.scalar_tensor_tensor(buf["d"][i][:], kk[:, :, 1:], col("u", h), o[:, :, 0:S],
                                                   ALU.add, ALU.subtract).then_inc(gaps_ready, 1)

                def sums(c):
                    h, q = CHUNKS[c]
                    i = c % 2
                    t = {n: buf[n][i] for n in buf}
                    dve.wait_ge(exps_ready, 4 * c + 2)
                    dve.wait_ge(E2v_ready, c + 1)
                    if c >= 2:
                        dve.wait_ge(Apq_ready, 2 * (c - 1))
                    nc.vector.tensor_tensor_scan(flat(t["p"][:]), flat(t["A2"][:]), flat(t["E2v"][:]), 0.0,
                                                 ALU.mult, ALU.add).then_inc(pq_ready, 1)
                    nc.vector.tensor_tensor_scan(flat(t["q"][:]), flat(t["A2"][:]), flat(t["E2"][:]), 0.0,
                                                 ALU.mult, ALU.add).then_inc(pq_ready, 1)
                    dve.wait_ge(Apq_ready, 2 * c + 2)
                    dve.wait_ge(Ev_ready, c + 1)
                    nc.vector.tensor_tensor(t["Aq"][:], t["Aq"][:], t["E"][:], ALU.add).then_inc(den_ready, 1)
                    chain(nc.vector.tensor_tensor(t["Ap"][:], t["Ap"][:], t["Ev"][:], ALU.add))
                    dve.wait_ge(den_ready, c + 1)
                    dve.wait_ge(rcp_ready, c + 1)
                    chain(nc.vector.tensor_tensor(t["Aq"][:], t["Aq"][:], t["d"][:], ALU.mult))
                    chain(nc.vector.scalar_tensor_tensor(t["d"][:], t["Aq"][:], -2.0, t["d"][:], ALU.add, ALU.mult))
                    nc.vector.scalar_tensor_tensor(yT[:, h, BQ * q:BQ * (q + 1), :], t["Ap"][:], -1.0, t["d"][:],
                                                   ALU.mult, ALU.mult).then_inc(y_ready, 1)

                for c in range(len(CHUNKS) + 1):
                    if c < len(CHUNKS):
                        if c >= 2:
                            dve.wait_ge(y_ready, c - 1)
                            dve.wait_ge(pq_ready, 2 * (c - 1))
                        gaps(c)
                    if c:
                        sums(c - 1)
                for m in range(NT // 2):
                    dve.wait_ge(yt_ready, m + 1)
                    nc.vector.tensor_tensor(x_res[:, 2 * m:2 * m + 2, :], x_res[:, 2 * m:2 * m + 2, :],
                                            y_ps[m % 2][:].rearrange("p (j c) -> p j c", j=2), ALU.add
                                            ).then_inc(x_added, 1)

            @block.scalar
            def _(act):
                chain = Chain(act, act_done)
                nc.scalar.preload_act_table_set(LN_EXP_SET)
                act_rsqrt(act, nc, k["rs0"][:], k["var"][:], k["st"][2][:], var_ready, LN_BEFORE["wkv"] + 1,
                          chain, rs_ready)
                for n in range(2 * (NT // 4)):
                    h, g = divmod(n, NT // 4)
                    act.wait_ge(zT_ready, n + 1)
                    nc.scalar.activation(k65[:, h, 8 * g:8 * g + 8, 1:], zT_ps[n % 4][:].rearrange("p (b s) -> p b s", s=S),
                                         ACT.Copy).then_inc(k_ready, 1)

                def exps(c):
                    i = c % 2
                    t = {n: buf[n][i] for n in buf}
                    act.wait_ge(gaps_ready, 3 * c + 1)
                    nc.scalar.activation(t["E2"][:, :, 1:], t["E2"][:, :, 1:], ACT.Exp).then_inc(exps_ready, 1)
                    act.wait_ge(gaps_ready, 3 * c + 2)
                    nc.scalar.activation(t["A2"][:, :, 1:], t["A2"][:, :, 1:], ACT.Exp).then_inc(exps_ready, 1)
                    act.wait_ge(gaps_ready, 3 * c + 3)
                    chain.mark(nc.scalar.activation(t["A"][:], t["d"][:], ACT.Relu))
                    chain(nc.scalar.activation(t["E"][:], t["d"][:], ACT.Relu, scale=-1.0))
                    nc.scalar.activation(t["A"][:], t["A"][:], ACT.Exp, scale=-1.0).then_inc(exps_ready, 1)
                    nc.scalar.activation(t["E"][:], t["E"][:], ACT.Exp, scale=-1.0).then_inc(exps_ready, 1)

                def guess_rcp(c):
                    t = {n: buf[n][c % 2] for n in buf}
                    act.wait_ge(den_ready, c + 1)
                    act.wait_ge(exps_ready, 4 * c + 4)
                    chain(nc.scalar.activation(t["d"][:], t["Aq"][:], ACT.Ln))
                    nc.scalar.activation(t["d"][:], t["d"][:], ACT.Exp, scale=-1.0).then_inc(rcp_ready, 1)

                for c in range(len(CHUNKS) + 1):
                    if c < len(CHUNKS):
                        exps(c)
                    if c:
                        guess_rcp(c - 1)

            @block.tensor
            def _(pe):
                pe.wait_ge(consts, 3)
                for n in range(2 * (NT // 4)):
                    h, g = divmod(n, NT // 4)
                    pe.wait_ge(z_ready, 4 * g + 4)
                    if n >= 4:
                        pe.wait_ge(k_ready, n - 3)
                    for j in range(4):
                        last = nc.tensor.transpose(zT_ps[n % 4][:, j * P:(j + 1) * P],
                                                   z[:, 4 * g + j, h * P:(h + 1) * P], ident[:])
                    last.then_inc(zT_ready, 1)
                for m in range(NT // 2):
                    pe.wait_ge(y_ready, len(CHUNKS) - 1 + m // (NT // 4))
                    if m >= 2:
                        pe.wait_ge(x_added, m - 1)
                    for j in range(2):
                        for h in range(KC):
                            t0 = (2 * m + j) * P
                            last = nc.tensor.transpose(y_ps[m % 2][:, (2 * j + h) * P:(2 * j + h + 1) * P],
                                                       yT[:, h].rearrange("p b s -> p (b s)")[:, t0:t0 + P], ident[:])
                    last.then_inc(yt_ready, 1)



def pipeline(eng, step, rounds, width, lag, peel_last=False, peel=1):
    for i in range(peel):
        for o in range(width):
            step(i, o)
    with eng.Fori(peel, rounds - peel_last) as i:
        for o in range(width):
            step(i, o)
    if peel_last:
        for o in range(width):
            step(rounds - 1, o)
    for o in range(lag):
        step(rounds, o)


class Unit:

    def __init__(self, i, o, width, rounds, back=0):
        static = isinstance(i, int)
        self.n = width * i + o - back
        self.o = (o - back) % width
        self.live = not static or 0 <= self.n < width * rounds
        self.static = static

    def count(self, per=1, more=0):
        return self.n * per + more

    def before(self, units, per=1):
        if self.static and self.n < units:
            return None
        return (self.n - units + 1) * per


def wait_unit(eng, sem, value):
    if value is not None:
        eng.wait_ge(sem, value)



def ternary_ffn_stage(k, w1T, w3T, w2T):
    nc, sem, x_res, ident = k["nc"], k["sem"], k["x_res"], k["ident"]
    HC = -(-HID // P)
    TAIL = HID - (HC - 1) * P
    BANK = 512
    HH = HID // 2
    WIDTH = 4
    ROUNDS = NT // WIDTH
    with ExitStack() as own:
        def sb(name, shape, dt=F32):
            return own.enter_context(nc.sbuf_tensor(name, shape, dt))

        def psum(name, shape, dt=F32):
            return own.enter_context(nc.psum_tensor(name, shape, dt))

        raw13 = [sb(f"raw{n}", [P, KC, HID]) for n in (1, 3)]
        raw2 = sb("raw2", [P, HC, C])
        w13q = [sb(f"w{n}q", [P, KC, HID], BF16) for n in (1, 3)]
        w2q = sb("w2q", [P, HC, C], BF16)
        asum = sb("asum", [P, 4])
        ws = sb("ws", [P, 4])
        iws = sb("iws", [P, 4])
        z = sb("tf_z", [P, NT, C])
        amax = sb("tf_amax", [P, NT])
        qs = sb("tf_qs", [P, NT])
        tsc = sb("tf_tsc", [P, NT, 2])
        cur = [sb(f"tf_cur{i}", [P, 2]) for i in range(4)]
        xq = [sb(f"tf_xq{i}", [P, C], BF16) for i in range(2)]
        xqT = [sb(f"tf_xqT{i}", [P, C], BF16) for i in range(2)]
        gate = sb("tf_gate", [P, HID])
        hm = sb("tf_hm", [P, HID])
        hr = sb("tf_hr", [P, HID])
        hq = [sb(f"tf_hq{i}", [P, HID], BF16) for i in range(2)]
        hqT = [sb(f"tf_hqT{i}", [P, HC * P], BF16) for i in range(2)]
        small = sb("tf_small", [P, 4])
        gam = [sb(f"tf_gam{i}", [P, 1]) for i in range(4)]
        identb = sb("identb", [P, P], BF16)
        xT_ps = psum("tf_xT_ps", [P, 2 * BANK], BF16)
        h1_ps = [psum(f"h1_ps{i}", [P, BANK]) for i in range(2)]
        h3_ps = [psum(f"h3_ps{i}", [P, BANK]) for i in range(2)]
        hT_ps = psum("hT_ps", [P, 2 * BANK], BF16)
        y_ps = psum("tf_y_ps", [P, BANK])

        w13_in, w2_in = sem("w13_in"), sem("w2_in")
        cleared, idb_ready = sem("tf_cleared"), sem("idb_ready")
        asum_ready, wsum_ready, w_ready = sem("asum_ready"), sem("wsum_ready"), sem("tf_w_ready")
        var_ready, rs_ready = k["ln_var_ready"], k["ln_rs_ready"]
        dve_done, act_done = sem("tf_dve_done"), sem("tf_act_done")
        unit_done = sem("tf_unit_done")
        xq_ready, xT_ready, xqT_ready = sem("tf_xq_ready"), sem("tf_xT_ready"), sem("tf_xqT_ready")
        h_ready, gate_ready, hm_ready = sem("tf_h_ready"), sem("tf_gate_ready"), sem("tf_hm_ready")
        hq_ready, hT_ready, hqT_ready = sem("tf_hq_ready"), sem("tf_hT_ready"), sem("tf_hqT_ready")
        y_ready, x_added = sem("tf_y_ready"), sem("tf_x_added")

        with nc.Block() as block:
            @block.sync
            def _(sp):
                for raw, w in zip(raw13, (w1T, w3T)):
                    sp.dma_start(raw[:], w.rearrange("(h p) n -> p h n", p=P)).then_inc(w13_in, 16)
                full = (HC - 1) * P
                sp.dma_start(raw2[:, 0:HC - 1, :], w2T[0:full, :].rearrange("(a p) n -> p a n", p=P)
                             ).then_inc(w2_in, 16)
                sp.dma_start(raw2[0:TAIL, HC - 1, :], w2T[full:HID, :]).then_inc(w2_in, 16)

            @block.gpsimd
            def _(pool):
                nc.gpsimd.memset(asum[:], 0.0).then_inc(cleared, 1)
                nc.gpsimd.tensor_copy(identb[:], ident[:]).then_inc(idb_ready, 1)

            @block.vector
            def _(dve):
                chain = Chain(dve, dve_done)
                for j in range(NT):
                    chain.mark(nc.vector.bn_stats(k["stat6"][:, j, :], x_res[:, j, :]))
                chain.settle()
                dve_mean_var(k, chain, var_ready)
                dve.wait_ge(cleared, 1)
                dve.wait_ge(w13_in, 32)
                for n, raw in enumerate(raw13):
                    nc.vector.tensor_reduce(asum[:, n:n + 1], raw[:].rearrange("p h n -> p (h n)"), AX.X, ALU.add,
                                            apply_absolute_value=True).then_inc(asum_ready, 1)
                dve.wait_ge(w2_in, 32)
                nc.vector.tensor_reduce(asum[:, 2:3], raw2[:, 0:HC - 1, :].rearrange("p a n -> p (a n)"), AX.X,
                                        ALU.add, apply_absolute_value=True).then_inc(asum_ready, 1)
                nc.vector.tensor_reduce(asum[0:TAIL, 3:4], raw2[0:TAIL, HC - 1, :], AX.X, ALU.add,
                                        apply_absolute_value=True).then_inc(asum_ready, 1)
                dve.wait_ge(rs_ready, LN_BEFORE["ternary"] + 1)
                dve.wait_ge(var_ready, LN_BEFORE["ternary"] + 1)
                rsqrt_newton(chain, nc, k["rstd"][:], k["rs0"][:], k["var"][:], k["st"][0][:])
                for j in range(NT):
                    chain.mark(nc.vector.tensor_scalar(z[:, j, :], x_res[:, j, :], k["mean"][:, j:j + 1],
                                                       k["rstd"][:, j:j + 1], ALU.subtract, ALU.mult))
                chain.settle()
                dve.wait_ge(wsum_ready, 1)
                chain(nc.vector.tensor_scalar(ws[:, 0:3], y_ps[:, 0:3], 1.0 / (HID * C), None, ALU.mult))
                chain(nc.vector.scalar_tensor_tensor(ws[:, 2:3], y_ps[:, 3:4], 1.0 / (HID * C), ws[:, 2:3],
                                                     ALU.mult, ALU.add))
                chain(nc.vector.tensor_scalar(ws[:, 0:3], ws[:, 0:3], QUANT_EPS, None, ALU.max))
                chain(nc.vector.reciprocal(iws[:, 0:3], ws[:, 0:3]))

                def ternary(raw, n, dst):
                    chain(nc.vector.tensor_scalar(raw, raw, iws[0:raw.shape[0], n:n + 1], ROUND32, ALU.mult, ALU.add))
                    chain(nc.vector.tensor_scalar(raw, raw, -ROUND32, 1.0, ALU.add, ALU.min))
                    nc.vector.tensor_scalar(dst, raw, -1.0, None, ALU.max).then_inc(w_ready, 1)

                for n in range(2):
                    ternary(raw13[n][:], n, w13q[n][:])
                ternary(raw2[:, 0:HC - 1, :], 2, w2q[:, 0:HC - 1, :])
                ternary(raw2[0:TAIL, HC - 1, :], 2, w2q[0:TAIL, HC - 1, :])
                chain(nc.vector.tensor_reduce(amax[:], z[:], AX.X, ALU.max, apply_absolute_value=True))
                chain(nc.vector.tensor_scalar(amax[:], amax[:], QUANT_EPS, 1.0 / 127.0, ALU.max, ALU.mult))
                chain.mark(nc.vector.tensor_scalar(tsc[:, :, 0], amax[:], ws[:, 0:1], None, ALU.mult))
                chain.mark(nc.vector.tensor_scalar(tsc[:, :, 1], amax[:], ws[:, 1:2], None, ALU.mult))
                chain(nc.vector.reciprocal(qs[:], amax[:]))
                for j in range(NT):
                    chain.mark(nc.vector.tensor_scalar(z[:, j, :], z[:, j, :], qs[:, j:j + 1], ROUND32,
                                                       ALU.mult, ALU.add))
                chain.settle()
                steps = Chain(dve, unit_done)

                def step(i, o):
                    u, mid, late = (Unit(i, o, WIDTH, ROUNDS, b) for b in (0, 2, 4))
                    if mid.live:
                        steps.at(mid.count(6))
                        for c in range(2):
                            dve.wait_ge(gate_ready, mid.count(2, c + 1))
                            nc.vector.tensor_tensor(hm[:, c * HH:(c + 1) * HH], gate[:, c * HH:(c + 1) * HH],
                                                    h3_ps[c][:, 0:HH], ALU.mult).then_inc(hm_ready, 1)
                        dve.wait_ge(hm_ready, mid.count(2, 2))
                        steps.mark(nc.vector.tensor_reduce(small[:, 0:1], hm[:], AX.X, ALU.max,
                                                           apply_absolute_value=True))
                    if u.live:
                        wait_unit(dve, xT_ready, u.before(2))
                        wait_unit(dve, gate_ready, u.before(4, 2))
                        nc.vector.tensor_scalar(xq[u.o % 2][:], z[:, bass.ds(u.n, 1), :].rearrange("p a c -> p (a c)"),
                                                -ROUND32, None, ALU.add).then_inc(xq_ready, 1)
                        nc.vector.tensor_copy(cur[u.o][:], tsc[:, bass.ds(u.n, 1), :].rearrange("p a c -> p (a c)")
                                              ).then_inc(xq_ready, 1)
                    if mid.live:
                        steps.settle()
                        dve.wait_ge(xq_ready, mid.count(2, 2))
                        steps(nc.vector.tensor_scalar(small[:, 0:1], small[:, 0:1], cur[mid.o][:, 1:2], QUANT_EPS,
                                                      ALU.mult, ALU.max))
                        steps.mark(nc.vector.reciprocal(small[:, 1:2], small[:, 0:1]))
                        wait_unit(dve, x_added, mid.before(4))
                        steps(nc.vector.tensor_scalar(gam[mid.o][:], small[:, 0:1], ws[:, 2:3], 1.0 / 127.0,
                                                      ALU.mult, ALU.mult))
                        steps.mark(nc.vector.tensor_scalar(small[:, 2:3], small[:, 1:2], cur[mid.o][:, 1:2], 127.0,
                                                           ALU.mult, ALU.mult))
                    if late.live:
                        dve.wait_ge(y_ready, late.count(1, 1))
                        xt = x_res[:, bass.ds(late.n, 1), :].rearrange("p a c -> p (a c)")
                        nc.vector.scalar_tensor_tensor(xt, y_ps[:, 0:C], gam[late.o][:], xt, ALU.mult, ALU.add
                                                       ).then_inc(x_added, 1)
                    if mid.live:
                        steps.settle()
                        steps(nc.vector.tensor_scalar(hr[:], hm[:], small[:, 2:3], ROUND32, ALU.mult, ALU.add))
                        wait_unit(dve, hT_ready, mid.before(2))
                        nc.vector.tensor_scalar(hq[mid.o % 2][:], hr[:], -ROUND32, None, ALU.add).then_inc(hq_ready, 1)
                        dve.wait_ge(hq_ready, mid.count(1, 1))

                pipeline(dve, step, ROUNDS, WIDTH, 4, peel=2)

            @block.scalar
            def _(act):
                chain = Chain(act, act_done)
                nc.scalar.preload_act_table_set(LN_EXP_SET)
                act_rsqrt(act, nc, k["rs0"][:], k["var"][:], k["st"][2][:], var_ready, LN_BEFORE["ternary"] + 1,
                          chain, rs_ready)
                nc.scalar.preload_act_table(ACT.Silu)

                def step(i, o):
                    u, mid, late = (Unit(i, o, WIDTH, ROUNDS, b) for b in (0, 1, 3))
                    if mid.live:
                        for c in range(2):
                            act.wait_ge(h_ready, mid.count(2, c + 1))
                            act.wait_ge(xq_ready, mid.count(2, 2))
                            wait_unit(act, hm_ready, mid.before(1, 2))
                            nc.scalar.activation(gate[:, c * HH:(c + 1) * HH], h1_ps[c][:, 0:HH], ACT.Silu,
                                                 scale=cur[mid.o][:, 0:1]).then_inc(gate_ready, 1)
                    if late.live:
                        par = late.o % 2
                        act.wait_ge(hT_ready, late.count(1, 1))
                        wait_unit(act, y_ready, late.before(2))
                        full = (HC - 1) * P
                        nc.scalar.activation(hqT[par][:, 0:full], hT_ps[:, 0:full], ACT.Copy).then_inc(hqT_ready, 1)
                        nc.scalar.activation(hqT[par][0:TAIL, full:full + P], hT_ps[0:TAIL, full:full + P], ACT.Copy
                                             ).then_inc(hqT_ready, 1)
                    if u.live:
                        act.wait_ge(xT_ready, u.count(1, 1))
                        wait_unit(act, h_ready, u.before(2, 2))
                        nc.scalar.activation(xqT[u.o % 2][:], xT_ps[:, 0:C], ACT.Copy).then_inc(xqT_ready, 1)

                pipeline(act, step, ROUNDS, WIDTH, 3, peel=2)

            @block.tensor
            def _(pe):
                pe.wait_ge(asum_ready, 4)
                pe.wait_ge(cleared, 1)
                nc.tensor.matmul(y_ps[:, 0:4], k["ones"][:], asum[:], start=True, stop=True).then_inc(wsum_ready, 1)
                pe.wait_ge(idb_ready, 1)

                def step(i, o):
                    u, mid, late = (Unit(i, o, WIDTH, ROUNDS, b) for b in (0, 1, 3))
                    if mid.live:
                        if mid.static and mid.n == 0:
                            pe.wait_ge(w_ready, 4)
                        pe.wait_ge(xqT_ready, mid.count(1, 1))
                        for c in range(2):
                            if not (mid.static and mid.n == 0):
                                pe.wait_ge(hm_ready, mid.count(2, c - 1))
                            for ps, w in ((h1_ps, w13q[0]), (h3_ps, w13q[1])):
                                for h in range(KC):
                                    last = nc.tensor.matmul(ps[c][:, 0:HH], xqT[mid.o % 2][:, h * P:(h + 1) * P],
                                                            w[:, h, c * HH:(c + 1) * HH], start=(h == 0),
                                                            stop=(h == KC - 1))
                            last.then_inc(h_ready, 1)
                    if late.live:
                        par = late.o % 2
                        pe.wait_ge(hq_ready, late.count(1, 1))
                        wait_unit(pe, hqT_ready, late.before(1, 2))
                        for a in range(HC):
                            m = min(P, HID - a * P)
                            last = nc.tensor.transpose(hT_ps[0:m, a * P:a * P + P], hq[par][:, a * P:a * P + m],
                                                       identb[:])
                        last.then_inc(hT_ready, 1)
                    if u.live:
                        par = u.o % 2
                        pe.wait_ge(xq_ready, u.count(2, 1))
                        wait_unit(pe, xqT_ready, u.before(1))
                        for h in range(KC):
                            last = nc.tensor.transpose(xT_ps[:, h * P:(h + 1) * P], xq[par][:, h * P:(h + 1) * P],
                                                       identb[:])
                        last.then_inc(xT_ready, 1)
                    if late.live:
                        par = late.o % 2
                        pe.wait_ge(hqT_ready, late.count(2, 2))
                        wait_unit(pe, x_added, late.before(1))
                        for a in range(HC):
                            m = min(P, HID - a * P)
                            last = nc.tensor.matmul(y_ps[:, 0:C], hqT[par][0:m, a * P:a * P + P], w2q[0:m, a, :],
                                                    start=(a == 0), stop=(a == HC - 1))
                        last.then_inc(y_ready, 1)

                pipeline(pe, step, ROUNDS, WIDTH, 3)



def fp8_rounding(chain, nc, y, e, m, out):
    chain(nc.vector.tensor_scalar(y, y, FP8_MAX, -FP8_MAX, ALU.min, ALU.max))
    chain(nc.vector.tensor_scalar(e.bitcast(U16), y.bitcast(U16), 0x7F80, None, ALU.bitwise_and))
    chain(nc.vector.tensor_scalar(m, e, 2.0 ** -6, 1.5 * 2.0 ** 4, ALU.max, ALU.mult))
    chain(nc.vector.tensor_tensor(y, y, m, ALU.add))
    chain.mark(nc.vector.tensor_tensor(out, y, m, ALU.subtract))


def ln_quant_stage(k, xq8):
    nc, sem, x_res, ident, col = k["nc"], k["sem"], k["x_res"], k["ident"], k["col"]
    GT = 4
    NG = NT // GT
    W = GT * P
    with ExitStack() as own:
        def sb(name, shape, dt=F32):
            return own.enter_context(nc.sbuf_tensor(name, shape, dt))

        z = sb("lq_z", [P, NT, C])
        lnT = [sb(f"lnT{i}", [P, KC, W]) for i in range(2)]
        y = [sb(f"lq_y{i}", [P, 4 * KC, W], BF16) for i in range(2)]
        e = sb("lq_e", [P, 4 * KC, W], BF16)
        m = sb("lq_m", [P, 4 * KC, W], BF16)
        inv = sb("lq_inv", [P, 4 * KC])
        zT_ps = [own.enter_context(nc.psum_tensor(f"lq_zT_ps{i}", [P, 512], F32)) for i in range(4)]
        var_ready, rs_ready = k["ln_var_ready"], k["ln_rs_ready"]
        dve_done, act_done, inv_ready = sem("lq_dve_done"), sem("lq_act_done"), sem("lq_inv_ready")
        z_ready, zT_ready, y_ready, xq_ready = sem("lq_z_ready"), sem("lq_zT_ready"), sem("lq_y_ready"), sem("lq_xq_ready")
        lnT_ready = sem("lq_lnT_ready")

        with nc.Block() as block:
            @block.vector
            def _(dve):
                chain = Chain(dve, dve_done)
                nc.vector.reciprocal(inv[:], col("sq", 0, 4 * KC)).then_inc(inv_ready, 1)
                for r in range(2):
                    src = x_res if r == 0 else z
                    for j in range(NT):
                        chain.mark(nc.vector.bn_stats(k["stat6"][:, j, :], src[:, j, :]))
                    chain.settle()
                    dve_mean_var(k, chain, var_ready)
                    dve.wait_ge(rs_ready, LN_BEFORE["quant"] + r + 1)
                    dve.wait_ge(var_ready, LN_BEFORE["quant"] + r + 1)
                    rsqrt_newton(chain, nc, k["rstd"][:], k["rs0"][:], k["var"][:], k["st"][0][:])
                    for j in range(NT):
                        ins = nc.vector.tensor_scalar(z[:, j, :], src[:, j, :], k["mean"][:, j:j + 1],
                                                      k["rstd"][:, j:j + 1], ALU.subtract, ALU.mult)
                        if r == 0:
                            chain.mark(ins)
                        else:
                            ins.then_inc(z_ready, 1)
                    if r == 0:
                        chain.settle()
                for g in range(NG):
                    dve.wait_ge(y_ready, 8 * g + 8)
                    fp8_rounding(chain, nc, y[g % 2][:], e[:], m[:], xq8[:, :, g * W:(g + 1) * W])
                    chain.settle()
                    nc.vector.memset(k["st"][1][:, 0:1], 0.0).then_inc(xq_ready, 1)

            @block.tensor
            def _(pe):
                for n in range(NG * KC):
                    g, h = divmod(n, KC)
                    pe.wait_ge(z_ready, GT * g + GT)
                    if n >= 4:
                        pe.wait_ge(lnT_ready, n - 3)
                    for j in range(GT):
                        last = nc.tensor.transpose(zT_ps[n % 4][:, j * P:(j + 1) * P],
                                                   z[:, GT * g + j, h * P:(h + 1) * P], ident[:])
                    last.then_inc(zT_ready, 1)

            @block.scalar
            def _(act):
                chain = Chain(act, act_done)
                nc.scalar.preload_act_table_set(LN_EXP_SET)
                for r in range(2):
                    act_rsqrt(act, nc, k["rs0"][:], k["var"][:], k["st"][2][:], var_ready,
                              LN_BEFORE["quant"] + r + 1, chain, rs_ready)
                act.wait_ge(inv_ready, 1)
                for g in range(NG):
                    for h in range(KC):
                        n = g * KC + h
                        act.wait_ge(zT_ready, n + 1)
                        nc.scalar.activation(lnT[g % 2][:, h, :], zT_ps[n % 4][:], ACT.Identity, scale=col("ln_w", h),
                                             bias=col("ln_b", h)).then_inc(lnT_ready, 1)
                    act.wait_ge(lnT_ready, KC * (g + 1))
                    if g >= 2:
                        act.wait_ge(xq_ready, g - 1)
                    for q in range(4):
                        for h in range(KC):
                            a = q * KC + h
                            nc.scalar.activation(y[g % 2][:, a, :], lnT[g % 2][:, h, :], ACT.Copy,
                                                 scale=inv[:, a:a + 1]).then_inc(y_ready, 1)



def attention_stage(k, kind, xq8, weights, wprojT, ctxT):
    nc, sem, x_res, ident, col = k["nc"], k["sem"], k["x_res"], k["ident"], k["col"]
    own_kv = kind == "self"
    name = kind[0]
    GU = 2
    HU = GU * HPG
    UT = G // GU
    WIDTH = 2 * UT
    ROUNDS = NT // 2
    QW, KW = HU * D, GU * D
    NQ = 3 if own_kv else 1
    Q0 = 0 if own_kv else 3
    CHUNK = 2048
    scale = float(D) ** -0.5
    pre = "" if own_kv else "x"
    with ExitStack() as own:
        def sb(nm, shape, dt=F32):
            return own.enter_context(nc.sbuf_tensor(f"{name}_{nm}", shape, dt))

        def psum(nm, shape, dt=F32):
            return own.enter_context(nc.psum_tensor(f"{name}_{nm}", shape, dt))

        def sg(nm):
            return sem(f"{name}_{nm}")

        wq = [sb(f"wq{p}", [P, KC, NH * D], F32R) for p in range(2)]
        wp = [sb(f"wp{p}", [P, NH, C], F32R) for p in range(2)]
        if own_kv:
            wk = [sb(f"wk{p}", [P, KC, G * D], F32R) for p in range(2)]
            wv = [sb(f"wv{p}", [P, KC, G * D], F32R) for p in range(2)]
        else:
            wkx, wvx = sb("wkx", [P, KC, G * D]), sb("wvx", [P, KC, G * D])
            ctx_t = [sb(f"ctx{i}", [P, KC, P]) for i in range(2)]
        raw = [sb(f"raw{i}", [P, CHUNK]) for i in range(2)]
        hsum = sb("hsum", [P, NH])
        xqf = [sb(f"xqf{i}", [P, NQ * KC, P], F32R) for i in range(2)]
        lnp = sb("lnp", [P, 2])
        ism = sb("ism", [P, NH])
        pscale = sb("pscale", [P, 1])
        sq = sb("sq", [P, QW + KW])
        v6, r6, t6, l6 = (sb(nm, [P, HU + GU]) for nm in ("v6", "r6", "t6", "l6"))
        g6 = sb("g6", [P, HU + GU])
        qn, kn = sb("qn", [P, QW]), sb("kn", [P, KW])
        v_s = [sb(f"v{i}", [P, KW]) for i in range(4)]
        qT, kT = sb("qT", [P, QW]), sb("kT", [P, KW])
        nmax, psum_s, rsum = sb("nmax", [P, 4]), sb("psums", [P, 4]), sb("rsum", [P, 4])
        pe_s, pn = sb("p", [P, 4 * S]), sb("pn", [P, 4 * S])
        pT = sb("pT", [P, GU, HPG, 2, S])
        yb, eb, mb, tb = (sb(nm, [P, QW], BF16) for nm in ("yb", "eb", "mb", "tb"))
        cat = [sb(f"cat{i}", [P, QW], F32R) for i in range(2)]
        qkv_ps = [psum(f"qkv_ps{i}", [P, 512]) for i in range(3)]
        bank_of = [j % 3 for j in range(2 * WIDTH - 1)] + [1]
        qT_ps = psum("qT_ps", [P, QW])
        kT_ps = psum("kT_ps", [P, KW])
        sc_ps = psum("sc_ps", [P, 4 * S])
        po_ps = psum("po_ps", [P, 512])
        pj_ps = psum("pj_ps", [P, 512])

        raw_in = [sg(f"raw_in{i}") for i in range(2)]
        lo_ready, prep_done, w_direct = sg("lo_ready"), sg("prep_done"), sg("w_direct")
        pT_cleared = sg("pT_cleared")
        xqf_ready, ctx_in = sg("xqf_ready"), [sg(f"ctx_in{i}") for i in range(2)]
        q_done, kv_done, t_done = sg("q_done"), sg("kv_done"), sg("t_done")
        sqq_ready, sqk_ready, v_ready = sg("sqq_ready"), sg("sqk_ready"), sg("v_ready")
        var_ready, rs_ready = sg("var_ready"), sg("rs_ready")
        qn_ready, kn_ready = sg("qn_ready"), sg("kn_ready")
        qT_ready, kT_ready = sg("qT_ready"), sg("kT_ready")
        sc_done, max_ready, exp_ready = sg("sc_done"), sg("max_ready"), sg("exp_ready")
        rsum_ready, pn_ready = sg("rsum_ready"), sg("pn_ready")
        pt_done, pT_ready, pv_done = sg("pt_done"), sg("pT_ready"), sg("pv_done")
        r_ready, cadd_ready = sg("r_ready"), sg("cadd_ready")
        y_ready, cat_ready, pj_done, x_added = sg("y_ready"), sg("cat_ready"), sg("pj_done"), sg("x_added")
        norm_steps, cat_steps, act_steps = sg("norm_steps"), sg("cat_steps"), sg("act_steps")

        steps = []
        if own_kv:
            wqT, wkT, wvT = weights
            for h in range(KC):
                steps.append((wqT[h * P:(h + 1) * P, :], col("sq", h), col("wq_s"), True, wq[0][:, h, :], wq[1][:, h, :], None))
            for h in range(KC):
                steps.append((wkT[h * P:(h + 1) * P, :], col("sk", h), col("wk_s"), True, wk[0][:, h, :], wk[1][:, h, :], None))
                steps.append((wvT[h * P:(h + 1) * P, :], col("sv", h), col("wv_s"), False, wv[0][:, h, :], wv[1][:, h, :], None))
        else:
            wqxT, wkvxT = weights
            for h in range(KC):
                steps.append((wqxT[h * P:(h + 1) * P, :], col("sqx", h), col("wqx_s"), True, wq[0][:, h, :], wq[1][:, h, :], None))
            for h in range(KC):
                steps.append((wkvxT[h * P:(h + 1) * P, 0:G * D], None, None, True, None, None, wkx[:, h, :]))
        half = NH // 2
        row0 = 0 if own_kv else NH * D
        for a in range(2):
            src = wprojT[row0 + a * half * D:row0 + (a + 1) * half * D, :].rearrange("(c p) n -> p c n", p=P)
            steps.append((src, None, None, False, wp[0][:, a * half:(a + 1) * half, :],
                          wp[1][:, a * half:(a + 1) * half, :], None))
        n_hi = [sum(1 for s in steps[:i + 1] if s[4] is not None) for i in range(len(steps))]
        n_plain = [sum(1 for s in steps[:i + 1] if s[6] is not None) for i in range(len(steps))]

        def raw_view(i, shape):
            n = 1
            for s in shape[1:]:
                n *= s
            v = raw[i % 2][:, 0:n]
            return v if len(shape) == 2 else v.rearrange("p (c n) -> p c n", c=shape[1])

        def units(i, o, *backs):
            return [Unit(i, o, WIDTH, ROUNDS, b) for b in backs]

        def tile_of(i, o, back=0):
            return 2 * i + (o - back) // UT

        def q_bank(u):
            return qkv_ps[bank_of[2 * u.o]]

        def kv_bank(u):
            return qkv_ps[bank_of[2 * u.o + 1]]

        def wait_bank(pe, u, use):
            j = 2 * u.o + use
            back = next(b for b in range(1, 2 * WIDTH + 1) if bank_of[(j - b) % (2 * WIDTH)] == bank_of[j])
            units_back = u.o - (j - back) // 2
            wait_unit(pe, (qn_ready, kn_ready)[(j - back) % 2], u.before(units_back))

        with nc.Block() as block:
            @block.sync
            def _(sp):
                if not own_kv:
                    for h in range(KC):
                        sp.dma_start(wvx[:, h, :], wkvxT[h * P:(h + 1) * P, G * D:2 * G * D]).then_inc(w_direct, 16)
                for i, s in enumerate(steps):
                    if i >= 2:
                        sp.wait_ge(lo_ready, i - 1)
                    sp.dma_start(raw_view(i, s[0].shape), s[0]).then_inc(raw_in[i % 2], 16)
                if not own_kv:
                    cv = ctxT.rearrange("(h p) t -> p h t", p=P)
                    for t in range(2):
                        sp.dma_start(ctx_t[t][:], cv[:, :, t * P:(t + 1) * P]).then_inc(ctx_in[t], 16)
                    with sp.Fori(1, ROUNDS) as i:
                        for t in range(2):
                            sp.wait_ge(kv_done, WIDTH * i + UT * (t + 1) - WIDTH)
                            sp.dma_start(ctx_t[t][:], cv[:, :, bass.ds((2 * i + t) * P, P)]).then_inc(ctx_in[t], 16)

            @block.gpsimd
            def _(pool):
                nc.gpsimd.memset(pT[:], 0.0).then_inc(pT_cleared, 1)

                def convert(t, par):
                    nc.gpsimd.tensor_copy(xqf[par][:], xq8[:, Q0 * KC:(Q0 + NQ) * KC, bass.ds(t * P, P)]
                                          ).then_inc(xqf_ready, 1)

                convert(0, 0)

                def step(i, o):
                    u, soft, out8 = units(i, o, 0, 1, 3)
                    if u.live and o % UT == 0:
                        nxt = tile_of(i, o) + 1
                        if not isinstance(nxt, int) or nxt < NT:
                            wait_unit(pool, kv_done, u.before(1))
                            convert(nxt, (o // UT + 1) % 2)
                    if out8.live:
                        pool.wait_ge(cadd_ready, out8.count(1, 1))
                        wait_unit(pool, pj_done, out8.before(2))
                        nc.gpsimd.tensor_tensor(cat[out8.o % 2][:], tb[:], mb[:], ALU.subtract).then_inc(cat_ready, 1)
                    if soft.live:
                        pool.wait_ge(rsum_ready, soft.count(1, 1))
                        pool.wait_ge(exp_ready, soft.count(4, 4))
                        wait_unit(pool, pt_done, soft.before(1))
                        nc.gpsimd.tensor_tensor(
                            pn[:].rearrange("p (a t) -> p a t", a=4), pe_s[:].rearrange("p (a t) -> p a t", a=4),
                            rsum[:].unsqueeze(2).broadcast_to([P, 4, S]), ALU.mult).then_inc(pn_ready, 1)

                pipeline(pool, step, ROUNDS, WIDTH, 3, peel_last=True)

            @block.vector
            def _(dve):
                prep = Chain(dve, prep_done)
                prep.mark(nc.vector.tensor_scalar(lnp[:], col(f"q{pre}ln_w", 0, 2), scale, None, ALU.mult))
                prep.mark(nc.vector.reciprocal(ism[:], col("smooth", 0 if own_kv else NH, NH)))
                prep.mark(nc.vector.tensor_tensor(pscale[:], col("proj_in"), col("proj_w"), ALU.mult))
                for i, (src, sc, wsc, centred, hi, lo, plain) in enumerate(steps):
                    dve.wait_ge(raw_in[i % 2], 16 * (i // 2 + 1))
                    if i:
                        dve.wait_ge(lo_ready, i)
                    w = raw_view(i, src.shape)
                    if sc is not None:
                        prep(nc.vector.tensor_scalar(w, w, sc, wsc, ALU.mult, ALU.mult))
                    if centred:
                        n = src.shape[1] // D
                        wh = w.rearrange("p (h d) -> p h d", d=D)
                        prep(nc.vector.tensor_reduce(hsum[:, 0:n], wh, AX.X, ALU.add))
                        dst = wh if plain is None else plain.rearrange("p (h d) -> p h d", d=D)
                        ins = nc.vector.scalar_tensor_tensor(dst, hsum[:, 0:n].unsqueeze(2).broadcast_to([P, n, D]),
                                                             -1.0 / D, wh, ALU.mult, ALU.add)
                        if plain is None:
                            prep(ins)
                        else:
                            ins.then_inc(lo_ready, 1)
                    if hi is not None:
                        prep(nc.vector.tensor_copy(hi, w))
                        nc.vector.tensor_tensor(lo, w, hi.bitcast(F32), ALU.subtract).then_inc(lo_ready, 1)

                norm, catc = Chain(dve, norm_steps), Chain(dve, cat_steps)

                def step(i, o):
                    u, sm, pv, f8, pj = units(i, o, 0, 1, 2, 3, 4)

                    def norm_guess():
                        norm.at(u.count(3))
                        dve.wait_ge(sqq_ready, u.count(1, 1))
                        dve.wait_ge(sqk_ready, u.count(1, 1))
                        norm(nc.vector.tensor_reduce(v6[:], sq[:].rearrange("p (h d) -> p h d", d=D), AX.X, ALU.add))
                        nc.vector.tensor_scalar(v6[:], v6[:], 1.0 / D, LN_EPS, ALU.mult, ALU.add
                                                ).then_inc(var_ready, 1)

                    def maxima():
                        dve.wait_ge(sc_done, sm.count(1, 1))
                        wait_unit(dve, exp_ready, sm.before(1, 4))
                        nc.vector.tensor_reduce(nmax[:], sc_ps[:].rearrange("p (a t) -> p a t", a=4), AX.X,
                                                ALU.max, negate=True).then_inc(max_ready, 1)

                    def newton(part):
                        if part == 0:
                            dve.wait_ge(rs_ready, u.count(1, 1))
                            dve.wait_ge(var_ready, u.count(1, 1))
                            norm.mark(nc.vector.scalar_tensor_tensor(t6[:], g6[:], -0.5, g6[:], ALU.mult, ALU.mult))
                        elif part == 1:
                            norm.settle()
                            norm.mark(nc.vector.tensor_tensor(t6[:], t6[:], v6[:], ALU.mult))
                        else:
                            norm.settle()
                            nc.vector.scalar_tensor_tensor(r6[:], t6[:], 1.5, g6[:], ALU.add, ALU.mult
                                                           ).then_inc(r_ready, 1)

                    def round8(part):
                        if part == 0:
                            catc.at(f8.count(3))
                            dve.wait_ge(y_ready, f8.count(1, 1))
                            catc.mark(nc.vector.tensor_scalar(yb[:], yb[:], FP8_MAX, -FP8_MAX, ALU.min, ALU.max))
                        elif part == 1:
                            catc.settle()
                            catc.mark(nc.vector.tensor_scalar(eb[:].bitcast(U16), yb[:].bitcast(U16), 0x7F80, None,
                                                              ALU.bitwise_and))
                        elif part == 2:
                            catc.settle()
                            wait_unit(dve, cat_ready, f8.before(1))
                            catc.mark(nc.vector.tensor_scalar(mb[:], eb[:], 2.0 ** -6, 1.5 * 2.0 ** 4, ALU.max,
                                                              ALU.mult))
                        elif part == 3:
                            catc.settle()
                            nc.vector.tensor_tensor(tb[:], yb[:], mb[:], ALU.add).then_inc(cadd_ready, 1)

                    def normalised():
                        dve.wait_ge(r_ready, u.count(1, 1))
                        wait_unit(dve, t_done, u.before(1))
                        nc.vector.tensor_tensor(qn[:].rearrange("p (h d) -> p h d", d=D),
                                                q_bank(u)[:].rearrange("p (h d) -> p h d", d=D),
                                                r6[:, 0:HU].unsqueeze(2).broadcast_to([P, HU, D]), ALU.mult
                                                ).then_inc(qn_ready, 1)
                        dve.wait_ge(v_ready, u.count(1, 1))
                        nc.vector.tensor_tensor(kn[:].rearrange("p (h d) -> p h d", d=D),
                                                kv_bank(u)[:, 0:KW].rearrange("p (h d) -> p h d", d=D),
                                                r6[:, HU:HU + GU].unsqueeze(2).broadcast_to([P, GU, D]), ALU.mult
                                                ).then_inc(kn_ready, 1)

                    if u.live:
                        norm_guess()
                    for part in range(3):
                        if f8.live:
                            round8(part)
                        if u.live:
                            newton(part)
                    if sm.live:
                        maxima()
                    if f8.live:
                        round8(3)
                    if u.live:
                        normalised()
                    if pv.live:
                        dve.wait_ge(pv_done, pv.count(1, 1))
                        wait_unit(dve, cadd_ready, pv.before(1))
                        first_head = (pv.o % UT) * HU
                        nc.vector.tensor_tensor(yb[:].rearrange("p (h t) -> p h t", h=HU),
                                                po_ps[:].rearrange("p (h t) -> p h t", h=HU),
                                                ism[:, first_head:first_head + HU].unsqueeze(2).broadcast_to([P, HU, P]),
                                                ALU.mult).then_inc(y_ready, 1)
                    if sm.live:
                        dve.wait_ge(exp_ready, sm.count(4, 4))
                        wait_unit(dve, pn_ready, sm.before(1))
                        nc.vector.reciprocal(rsum[:], psum_s[:]).then_inc(rsum_ready, 1)
                    if pj.live and pj.o % UT == UT - 1:
                        dve.wait_ge(pj_done, pj.count(1, 1))
                        xt = x_res[:, bass.ds(tile_of(i, o, 4), 1), :].rearrange("p a c -> p (a c)")
                        nc.vector.scalar_tensor_tensor(xt, pj_ps[:, 0:C], pscale[:], xt, ALU.mult, ALU.add
                                                       ).then_inc(x_added, 1)

                pipeline(dve, step, ROUNDS, WIDTH, 4)

            @block.scalar
            def _(act):
                nc.scalar.preload_act_table_set(LN_EXP_SET)
                act.wait_ge(prep_done, 3)
                act.wait_ge(pT_cleared, 1)
                chain = Chain(act, act_steps)

                def step(i, o):
                    u, sm, pv = units(i, o, 0, 1, 2)
                    if u.live:
                        act.wait_ge(q_done, u.count(1, 1))
                        wait_unit(act, var_ready, u.before(1))
                        nc.scalar.activation(sq[:, 0:QW], q_bank(u)[:], ACT.Square).then_inc(sqq_ready, 1)
                        act.wait_ge(kv_done, u.count(1, 1))
                        nc.scalar.activation(sq[:, QW:QW + KW], kv_bank(u)[:, 0:KW], ACT.Square).then_inc(sqk_ready, 1)
                        wait_unit(act, pv_done, u.before(4))
                        nc.scalar.activation(v_s[u.o % 4][:], kv_bank(u)[:, KW:2 * KW], ACT.Copy).then_inc(v_ready, 1)
                    if sm.live:
                        act.wait_ge(t_done, sm.count(1, 1))
                        nc.scalar.activation(kT[:], kT_ps[:], ACT.Identity, scale=col(f"k{pre}ln_w"),
                                             bias=col(f"k{pre}ln_b")).then_inc(kT_ready, 1)
                        nc.scalar.activation(qT[:], qT_ps[:], ACT.Identity, scale=lnp[:, 0:1], bias=lnp[:, 1:2]
                                             ).then_inc(qT_ready, 1)
                    if u.live:
                        chain.at(u.count(1))
                        act.wait_ge(var_ready, u.count(1, 1))
                        chain(nc.scalar.activation(l6[:], v6[:], ACT.Ln))
                        wait_unit(act, r_ready, u.before(1))
                        nc.scalar.activation(g6[:], l6[:], ACT.Exp, scale=-0.5).then_inc(rs_ready, 1)
                    if pv.live:
                        act.wait_ge(pt_done, pv.count(1, 1))
                        for b in range(2):
                            rows = slice(b * S, (b + 1) * S)
                            nc.scalar.activation(pT[rows, :, :, b, :], po_ps[rows, 0:GU * P].rearrange(
                                "p (g h s) -> p g h s", g=GU, h=HPG), ACT.Copy).then_inc(pT_ready, 1)
                    if sm.live:
                        act.wait_ge(max_ready, sm.count(1, 1))
                        wait_unit(act, pn_ready, sm.before(1))
                        wait_unit(act, rsum_ready, sm.before(1))
                        for a in range(4):
                            nc.scalar.activation(pe_s[:, a * S:(a + 1) * S], sc_ps[:, a * S:(a + 1) * S], ACT.Exp,
                                                 bias=nmax[:, a:a + 1], accum_out=psum_s[:, a:a + 1]
                                                 ).then_inc(exp_ready, 1)

                pipeline(act, step, ROUNDS, WIDTH, 2)

            @block.tensor
            def _(pe):
                pe.wait_ge(lo_ready, len(steps))
                if not own_kv:
                    pe.wait_ge(w_direct, 16 * KC)

                def split_product(out_ap, x_col, w_pair, c0, c1):
                    n = 0
                    for h in range(KC):
                        for part in range(2):
                            last = nc.tensor.matmul(out_ap, x_col(h), w_pair[part][:, h, c0:c1], start=(n == 0),
                                                    stop=(n == 2 * KC - 1))
                            n += 1
                    return last

                def step(i, o):
                    u, t, pv, pj = units(i, o, 0, 1, 2, 4)
                    if u.live:
                        gp, tp = u.o % UT, (u.o // UT) % 2
                        if gp == 0:
                            pe.wait_ge(xqf_ready, tile_of(i, o) + 1)
                        wait_bank(pe, u, 0)
                        split_product(q_bank(u)[:], lambda h: xqf[tp][:, h, :], wq, gp * QW, (gp + 1) * QW
                                      ).then_inc(q_done, 1)
                        wait_bank(pe, u, 1)
                        kv = kv_bank(u)
                        if own_kv:
                            split_product(kv[:, 0:KW], lambda h: xqf[tp][:, KC + h, :], wk, gp * KW, (gp + 1) * KW)
                            last = split_product(kv[:, KW:2 * KW], lambda h: xqf[tp][:, 2 * KC + h, :], wv,
                                                 gp * KW, (gp + 1) * KW)
                        else:
                            if gp == 0:
                                pe.wait_ge(ctx_in[tp], 16 * (i + 1))
                            for c, w in ((0, wkx), (KW, wvx)):
                                for h in range(KC):
                                    last = nc.tensor.matmul(kv[:, c:c + KW], ctx_t[tp][:, h, :],
                                                            w[:, h, gp * KW:(gp + 1) * KW], start=(h == 0),
                                                            stop=(h == KC - 1))
                        last.then_inc(kv_done, 1)
                    if t.live:
                        pe.wait_ge(qn_ready, t.count(1, 1))
                        pe.wait_ge(kn_ready, t.count(1, 1))
                        wait_unit(pe, qT_ready, t.before(1))
                        for a in range(HU):
                            g, h = divmod(a, HPG)
                            qcols = qT_ps[:].rearrange("p (g b h s) -> p g b h s", g=GU, b=2, h=HPG)[:, g, :, h, :]
                            nc.tensor.transpose(qcols, qn[:, a * P:(a + 1) * P], ident[:])
                        for a in range(GU):
                            last = nc.tensor.transpose(kT_ps[:, a * P:(a + 1) * P], kn[:, a * P:(a + 1) * P], ident[:])
                        last.then_inc(t_done, 1)
                    if pv.live:
                        pe.wait_ge(pn_ready, pv.count(1, 1))
                        wait_unit(pe, y_ready, pv.before(1))
                        for g in range(GU):
                            last = nc.tensor.transpose(po_ps[:, g * P:(g + 1) * P], pn[:, g * P:(g + 1) * P], ident[:])
                        last.then_inc(pt_done, 1)
                    if pj.live:
                        gpj = pj.o % UT
                        pe.wait_ge(cat_ready, pj.count(1, 1))
                        if gpj == 0 and not (pj.static and pj.n < UT):
                            pe.wait_ge(x_added, tile_of(i, o, 4))
                        for a in range(HU):
                            for part in range(2):
                                last = nc.tensor.matmul(pj_ps[:, 0:C], cat[pj.o % 2][:, a * P:(a + 1) * P],
                                                        wp[part][:, gpj * HU + a, :],
                                                        start=(gpj == 0 and a == 0 and part == 0),
                                                        stop=(gpj == UT - 1 and a == HU - 1 and part == 1))
                        last.then_inc(pj_done, 1)
                    if t.live:
                        pe.wait_ge(qT_ready, t.count(1, 1))
                        pe.wait_ge(kT_ready, t.count(1, 1))
                        wait_unit(pe, exp_ready, t.before(1, 4))
                        for g in range(GU):
                            for b in range(2):
                                a = g * 2 + b
                                last = nc.tensor.matmul(sc_ps[:, a * S:(a + 1) * S], qT[:, a * P:(a + 1) * P],
                                                        kT[:, g * P + b * S:g * P + (b + 1) * S], start=True, stop=True)
                        last.then_inc(sc_done, 1)
                    if pv.live:
                        pe.wait_ge(pT_ready, pv.count(2, 2))
                        for g in range(GU):
                            last = nc.tensor.matmul(po_ps[:, g * HPG * P:(g + 1) * HPG * P],
                                                    v_s[pv.o % 4][:, g * D:(g + 1) * D],
                                                    pT[:, g].rearrange("p h b s -> p (h b s)"), start=True, stop=True)
                        last.then_inc(pv_done, 1)

                pipeline(pe, step, ROUNDS, WIDTH, 4)



def routed_ffn_stage(k, routerT, fw1T, fw2T, fb2, out):
    nc, sem, x_res, ident, col = k["nc"], k["sem"], k["x_res"], k["ident"], k["col"]
    GT = 4
    NG = NT // GT
    W = GT * P
    FC = FF // P
    N2 = 2 * NT
    with ExitStack() as own:
        def sb(name, shape, dt=F32):
            return own.enter_context(nc.sbuf_tensor(name, shape, dt))

        def psum(name, shape, dt=F32):
            return own.enter_context(nc.psum_tensor(name, shape, dt))

        z = sb("rf_z", [P, NT, C])
        zT = sb("rf_zT", [P, KC, TOK])
        rw = sb("rf_rw", [P, KC, E])
        w1, w2 = sb("rf_w1", [P, KC, FF]), sb("rf_w2", [P, FC, C])
        b2 = sb("rf_b2", [P, C])
        tri = sb("rf_tri", [P, P])
        iota8 = sb("rf_iota8", [P, NT, E])
        first = sb("rf_first", [P, E, N2])
        pr, tmp = sb("rf_pr", [P, NT, E]), sb("rf_tmp", [P, NT, E])
        oh = sb("rf_oh", [P, N2, E])
        top = sb("rf_top", [P, N2])
        low = sb("rf_low", [P, NT])
        tot, acc = sb("rf_tot", [P, E, N2]), sb("rf_acc", [P, E, N2])
        cnt = sb("rf_cnt", [P, N2, E])
        pos = sb("rf_pos", [P, N2])
        gate = sb("rf_gate", [P, NT])
        hT = [sb(f"rf_hT{i}", [P, FC, W]) for i in range(2)]
        t_s = sb("rf_t", [P, C])
        zT_ps = [psum(f"rf_zT_ps{i}", [P, 512]) for i in range(2)]
        h_ps = [psum(f"rf_h_ps{i}", [P, 512]) for i in range(3)]
        y_ps = [psum(f"rf_y_ps{i}", [P, 512]) for i in range(2)]
        lg_ps = psum("rf_lg_ps", [P, 512])

        w_in, b2_in, rw_in = sem("rf_w_in"), sem("rf_b2_in"), sem("rf_rw_in")
        consts = sem("rf_consts")
        var_ready, rs_ready = k["ln_var_ready"], k["ln_rs_ready"]
        dve_done, act_done = sem("rf_dve_done"), sem("rf_act_done")
        z_ready, zTp_ready, zT_ready = sem("rf_z_ready"), sem("rf_zTp_ready"), sem("rf_zT_ready")
        lg_ready, sub_ready, exp_ready = sem("rf_lg_ready"), sem("rf_sub_ready"), sem("rf_exp_ready")
        oh_ready, cnt_ready = sem("rf_oh_ready"), sem("rf_cnt_ready")
        h_ready, hT_ready, y_ready, x_added = sem("rf_h_ready"), sem("rf_hT_ready"), sem("rf_y_ready"), sem("rf_x_added")
        counts_read, out_done = sem("rf_counts_read"), sem("out_done")

        with nc.Block() as block:
            @block.sync
            def _(sp):
                sp.dma_start(rw[:], routerT.rearrange("(h p) n -> p h n", p=P)).then_inc(rw_in, 16)
                sp.dma_start(w1[:], fw1T.rearrange("(h p) n -> p h n", p=P)).then_inc(w_in, 16)
                sp.dma_start(w2[:], fw2T.rearrange("(h p) n -> p h n", p=P)).then_inc(w_in, 16)
                sp.dma_start(b2[:], fb2.broadcast_to([P, C])).then_inc(b2_in, 16)
                outr = out.rearrange("(j p) c -> p j c", p=P)
                for j in range(0, NT, 2):
                    sp.wait_ge(x_added, j + 2)
                    sp.dma_start(outr[:, j:j + 2, :], x_res[:, j:j + 2, :]).then_inc(out_done, 16)
                sp.wait_ge(out_done, 16 * (NT // 2))

            @block.gpsimd
            def _(pool):
                nc.gpsimd.memset(tri[:], 1.0).then_inc(consts, 1)
                nc.gpsimd.memset(first[:], 1.0).then_inc(consts, 1)
                for e in range(E):
                    nc.gpsimd.memset(iota8[:, :, e], float(e - E)).then_inc(consts, 1)
                pool.wait_ge(consts, 2 + E)
                nc.gpsimd.affine_select(out=tri[:], in_=tri[:], compare_op=ALU.is_ge, fill=0.0, base=0,
                                        pattern=[[1, P]], channel_multiplier=-1).then_inc(consts, 1)
                nc.gpsimd.memset(first[:, :, 0], 0.0).then_inc(consts, 1)

            @block.vector
            def _(dve):
                chain = Chain(dve, dve_done)
                for j in range(NT):
                    chain.mark(nc.vector.bn_stats(k["stat6"][:, j, :], x_res[:, j, :]))
                chain.settle()
                dve_mean_var(k, chain, var_ready)
                dve.wait_ge(rs_ready, LN_BEFORE["routed"] + 1)
                dve.wait_ge(var_ready, LN_BEFORE["routed"] + 1)
                rsqrt_newton(chain, nc, k["rstd"][:], k["rs0"][:], k["var"][:], k["st"][0][:])
                for j in range(NT):
                    nc.vector.tensor_scalar(z[:, j, :], x_res[:, j, :], k["mean"][:, j:j + 1],
                                            k["rstd"][:, j:j + 1], ALU.subtract, ALU.mult).then_inc(z_ready, 1)

                def wide(v):
                    return v.unsqueeze(2).broadcast_to([P, NT, E])

                dve.wait_ge(lg_ready, 1)
                lg = lg_ps[:, 0:NT * E].rearrange("p (j e) -> p j e", e=E)
                chain(nc.vector.tensor_reduce(low[:], lg, AX.X, ALU.max))
                nc.vector.tensor_tensor(tmp[:], lg, wide(low[:]), ALU.subtract).then_inc(sub_ready, 1)
                dve.wait_ge(exp_ready, 1)
                chain(nc.vector.tensor_reduce(low[:], pr[:], AX.X, ALU.add))
                chain(nc.vector.reciprocal(low[:], low[:]))
                chain(nc.vector.tensor_tensor(pr[:], pr[:], wide(low[:]), ALU.mult))
                dve.wait_ge(consts, 4 + E)
                for c in range(2):
                    best = top[:, c * NT:(c + 1) * NT]
                    one = oh[:, c * NT:(c + 1) * NT, :]
                    chain(nc.vector.tensor_reduce(best, pr[:], AX.X, ALU.max))
                    chain(nc.vector.tensor_tensor(tmp[:], pr[:], wide(best), ALU.is_equal))
                    chain(nc.vector.tensor_tensor(tmp[:], tmp[:], iota8[:], ALU.mult))
                    chain(nc.vector.tensor_reduce(low[:], tmp[:], AX.X, ALU.min))
                    nc.vector.tensor_tensor(one, iota8[:], wide(low[:]), ALU.is_equal).then_inc(oh_ready, 1)
                    dve.wait_ge(oh_ready, c + 1)
                    if c == 0:
                        chain(nc.vector.scalar_tensor_tensor(pr[:], one, -2.0, pr[:], ALU.mult, ALU.add))
                dve.wait_ge(cnt_ready, 2)
                inside = h_ps[0][:, 0:N2 * E].rearrange("p (n e) -> p n e", e=E)
                totals = h_ps[1][:, 0:N2 * E].rearrange("p (n e) -> p e n", e=E)
                chain(nc.vector.tensor_copy(tot[:], totals))
                chain(nc.vector.tensor_tensor_scan(acc[:].rearrange("p e n -> p (e n)"),
                                                   first[:].rearrange("p e n -> p (e n)"),
                                                   tot[:].rearrange("p e n -> p (e n)"), 0.0, ALU.mult, ALU.add))
                chain(nc.vector.tensor_tensor(acc[:], acc[:], tot[:], ALU.subtract))
                nc.vector.tensor_tensor(cnt[:], inside, acc[:].rearrange("p e n -> p n e"), ALU.add
                                        ).then_inc(counts_read, 1)
                dve.wait_ge(counts_read, 1)
                chain(nc.vector.tensor_tensor(cnt[:], cnt[:], oh[:], ALU.mult))
                chain(nc.vector.tensor_reduce(pos[:], cnt[:], AX.X, ALU.add))
                chain(nc.vector.tensor_scalar(pos[:], pos[:], float(CAP), None, ALU.is_le))
                chain(nc.vector.tensor_tensor(pos[:], pos[:], top[:], ALU.mult))
                chain(nc.vector.tensor_tensor(gate[:], pos[:, 0:NT], pos[:, NT:N2], ALU.add))
                dve.wait_ge(b2_in, 16)
                for j in range(NT):
                    dve.wait_ge(y_ready, j + 1)
                    if j:
                        dve.wait_ge(x_added, j)
                    chain(nc.vector.tensor_tensor(t_s[:], y_ps[j % 2][:, 0:C], b2[:], ALU.add))
                    nc.vector.scalar_tensor_tensor(x_res[:, j, :], t_s[:], gate[:, j:j + 1], x_res[:, j, :],
                                                   ALU.mult, ALU.add).then_inc(x_added, 1)

            @block.scalar
            def _(act):
                chain = Chain(act, act_done)
                nc.scalar.preload_act_table_set(LN_EXP_SET)
                act_rsqrt(act, nc, k["rs0"][:], k["var"][:], k["st"][2][:], var_ready, LN_BEFORE["routed"] + 1,
                          chain, rs_ready)
                for n in range(NG * KC):
                    g, h = divmod(n, KC)
                    act.wait_ge(zTp_ready, n + 1)
                    nc.scalar.activation(zT[:, h, g * W:(g + 1) * W], zT_ps[n % 2][:], ACT.Copy).then_inc(zT_ready, 1)
                act.wait_ge(sub_ready, 1)
                nc.scalar.activation(pr[:], tmp[:], ACT.Exp).then_inc(exp_ready, 1)
                for n in range(NG * FC):
                    g, f = divmod(n, FC)
                    act.wait_ge(h_ready, n + 1)
                    if g >= 2:
                        act.wait_ge(y_ready, GT * (g - 1))
                    nc.scalar.activation(hT[g % 2][:, f, :], h_ps[n % 3][:], ACT.Gelu, bias=col("b1", f)
                                         ).then_inc(hT_ready, 1)

            @block.tensor
            def _(pe):
                for n in range(NG * KC):
                    g, h = divmod(n, KC)
                    pe.wait_ge(z_ready, GT * (g + 1))
                    if n >= 2:
                        pe.wait_ge(zT_ready, n - 1)
                    for j in range(GT):
                        last = nc.tensor.transpose(zT_ps[n % 2][:, j * P:(j + 1) * P],
                                                   z[:, GT * g + j, h * P:(h + 1) * P], ident[:])
                    last.then_inc(zTp_ready, 1)
                pe.wait_ge(zT_ready, NG * KC)
                pe.wait_ge(rw_in, 16)
                for j in range(NT):
                    for h in range(KC):
                        last = nc.tensor.matmul(lg_ps[:, j * E:(j + 1) * E], zT[:, h, j * P:(j + 1) * P], rw[:, h, :],
                                                start=(h == 0), stop=(h == KC - 1))
                last.then_inc(lg_ready, 1)
                pe.wait_ge(consts, 4 + E)
                pe.wait_ge(oh_ready, 2)
                ohf = oh[:].rearrange("p n e -> p (n e)")
                nc.tensor.matmul(h_ps[0][:, 0:N2 * E], tri[:], ohf, start=True, stop=True).then_inc(cnt_ready, 1)
                nc.tensor.matmul(h_ps[1][:, 0:N2 * E], k["ones"][:], ohf, start=True, stop=True).then_inc(cnt_ready, 1)
                pe.wait_ge(w_in, 32)
                pe.wait_ge(counts_read, 1)

                def second(g):
                    for j in range(GT):
                        n = GT * g + j
                        if n >= 2:
                            pe.wait_ge(x_added, n - 1)
                        for f in range(FC):
                            last = nc.tensor.matmul(y_ps[n % 2][:, 0:C], hT[g % 2][:, f, j * P:(j + 1) * P], w2[:, f, :],
                                                    start=(f == 0), stop=(f == FC - 1))
                        last.then_inc(y_ready, 1)

                for g in range(NG):
                    for f in range(FC):
                        n = g * FC + f
                        if n >= 3:
                            pe.wait_ge(hT_ready, n - 2)
                        for h in range(KC):
                            last = nc.tensor.matmul(h_ps[n % 3][:], w1[:, h, f * P:(f + 1) * P],
                                                    zT[:, h, g * W:(g + 1) * W], start=(h == 0), stop=(h == KC - 1))
                        last.then_inc(h_ready, 1)
                    if g:
                        pe.wait_ge(hT_ready, FC * g)
                        second(g - 1)
                pe.wait_ge(hT_ready, FC * NG)
                second(NG - 1)



def kernel(**inputs):
    import numpy as np
    import concourse.bacc as bacc
    from concourse.bass_utils import run_bass_kernel_spmd

    def get(name):
        return np.asarray(inputs[name])

    def columns(v, n):
        return v.reshape(n, P).T

    def everywhere(v):
        return np.broadcast_to(v.reshape(1, 1), (P, 1))

    packed = {
        "w": columns(get("L0_xattn_w"), KC), "u": columns(get("L0_xattn_u"), KC),
        "ln_w": columns(get("L1_xattn_ln_w"), KC), "ln_b": columns(get("L1_xattn_ln_b"), KC),
        "sq": columns(get("L1_xattn_q_in_scale"), KC), "sk": columns(get("L1_xattn_k_in_scale"), KC),
        "sv": columns(get("L1_xattn_v_in_scale"), KC), "sqx": columns(get("L1_xattn_qx_in_scale"), KC),
        "smooth": columns(get("L1_xattn_proj_smooth"), 2 * NH), "b1": columns(get("L1_ffn_b1"), FF // P),
        "wq_s": everywhere(get("L1_xattn_wq_scale")), "wk_s": everywhere(get("L1_xattn_wk_scale")),
        "wv_s": everywhere(get("L1_xattn_wv_scale")), "wqx_s": everywhere(get("L1_xattn_wqx_scale")),
        "proj_in": everywhere(get("L1_xattn_proj_in_scale")), "proj_w": everywhere(get("L1_xattn_proj_w_scale")),
    }
    for name in ("qln_w", "qln_b", "kln_w", "kln_b", "qxln_w", "qxln_b", "kxln_w", "kxln_b"):
        packed[name] = columns(get(f"L1_xattn_{name}"), 1)
    arrays = {
        "x": get("x").reshape(TOK, C),
        "ctxT": get("ctx_2048").reshape(TOK, C).T,
        "params": np.concatenate([packed[name] for name in PARAM_COLS], axis=1),
        "w1T": get("L0_ffn_w1").T, "w3T": get("L0_ffn_w3").T, "w2T": get("L0_ffn_w2").T,
        "wqT": get("L1_xattn_wq").T, "wkT": get("L1_xattn_wk").T, "wvT": get("L1_xattn_wv").T,
        "wqxT": get("L1_xattn_wqx").T, "wkvxT": get("L1_xattn_w_kv_x").T, "wprojT": get("L1_xattn_wproj").T,
        "routerT": get("L1_ffn_router_w").T, "fw1T": get("L1_ffn_w1").T, "fw2T": get("L1_ffn_w2").T,
        "fb2": get("L1_ffn_b2").reshape(1, C),
    }
    nc = bacc.Bacc("TRN2", target_bir_lowering=False, num_devices=1)
    args, feed = [], {}
    for name, a in arrays.items():
        a = np.ascontiguousarray(a)
        feed[f"in_{name}"] = a
        args.append(nc.dram_tensor(f"in_{name}", a.shape, mybir.dt.from_np(a.dtype), kind="ExternalInput").ap())
    args.append(nc.dram_tensor("out_x", (TOK, C), F32, kind="ExternalOutput").ap())
    build_program(nc, *args)
    r = run_bass_kernel_spmd(nc, [feed], core_ids=[0])
    return r.results[0]["out_x"].reshape(B, S, C)
```

```python
from contextlib import ExitStack

import concourse.bass as bass
from concourse import mybir

F32 = mybir.dt.float32
F32R = mybir.dt.float32r
BF16 = mybir.dt.bfloat16
U16 = mybir.dt.uint16
U32 = mybir.dt.uint32
ALU = mybir.AluOpType
ACT = mybir.ActivationFunctionType
AX = mybir.AxisListType

P = 128
B, S, C = 32, 64, 256
TOK = B * S
NT = TOK // P
KC = C // P
HID = 704
NH, G, D = 16, 8, 128
HPG = NH // G
E, CAP, FF = 8, 64, 1024
LN_EPS = 1e-5
QUANT_EPS = 1e-5
FP8_MAX = 448.0
ROUND32 = 1.5 * 2.0 ** 23
NEG_BIG = -1e38
LN_EXP_SET = "natural_log_exp_and_others"

PARAM_COLS = {}
for _name, _n in (("w", KC), ("u", KC), ("ln_w", KC), ("ln_b", KC), ("sq", KC), ("sk", KC), ("sv", KC),
                  ("sqx", KC), ("qln_w", 1), ("qln_b", 1), ("kln_w", 1), ("kln_b", 1), ("qxln_w", 1),
                  ("qxln_b", 1), ("kxln_w", 1), ("kxln_b", 1), ("smooth", 2 * NH), ("b1", FF // P),
                  ("wq_s", 1), ("wk_s", 1), ("wv_s", 1), ("wqx_s", 1), ("proj_in", 1), ("proj_w", 1)):
    PARAM_COLS[_name] = (sum(n for _, n in PARAM_COLS.values()), _n)
N_PARAM = sum(n for _, n in PARAM_COLS.values())


class Chain:

    def __init__(self, eng, sem):
        self.eng, self.sem, self.base, self.n = eng, sem, 0, 0

    def on(self, eng):
        self.eng = eng
        return self

    def at(self, base):
        self.base, self.n = base, 0

    def mark(self, ins):
        ins.then_inc(self.sem, 1)
        self.n += 1

    def settle(self):
        self.eng.wait_ge(self.sem, self.base + self.n)

    def __call__(self, ins):
        self.mark(ins)
        self.settle()


def build_program(nc, x, ctxT, params, w1T, w3T, w2T, wqT, wkT, wvT, wqxT, wkvxT, wprojT, routerT,
                  fw1T, fw2T, fb2, out):
    ctx = ExitStack()
    with ctx:
        def sb(name, shape, dt=F32, stack=ctx):
            return stack.enter_context(nc.sbuf_tensor(name, shape, dt))

        def sem(name):
            return ctx.enter_context(nc.semaphore(name))

        x_res = sb("x_res", [P, NT, C])
        par = sb("par", [P, N_PARAM])
        ident = sb("ident", [P, P])
        ones = sb("ones", [P, P])
        stat6 = sb("stat6", [P, NT, 6])
        mean = sb("mean", [P, NT])
        var, var0 = sb("var", [P, NT]), sb("var0", [P, NT])
        rstd = sb("rstd", [P, NT])
        st_a = sb("st_a", [P, NT])
        st_b = sb("st_b", [P, NT])
        st_c = sb("st_c", [P, NT])
        rs0 = sb("rs0", [P, NT])

        def col(name, i=0, n=1):
            at, _ = PARAM_COLS[name]
            return par[:, at + i:at + i + n]

        tok = dict(nc=nc, ctx=ctx, sb=sb, sem=sem, x_res=x_res, par=par, col=col, ident=ident, ones=ones,
                   ln_var_ready=sem("ln_var_ready"), ln_rs_ready=sem("ln_rs_ready"),
                   dve_chain=Chain(None, sem("dve_done")), act_chain=Chain(None, sem("act_done")), stat6=stat6, mean=mean, var=var, var0=var0, rstd=rstd, st=(st_a, st_b, st_c), rs0=rs0)
        with ExitStack() as held:
            work = [sb(f"w_work{i}", [P, KC * G * D], F32, held) for i in range(3)]
            tok["tw"] = ternary_weights(tok, work, held)
            wkv_stage(tok, x, ctxT, params, (w1T, w3T, w2T))
            aw = attention_weights(tok, held)
            ternary_ffn_stage(tok, aw, self_chunks(tok, aw, wqT, wkT, wvT, wprojT))
            xq8 = sb("xq8", [P, 4 * KC, TOK], BF16, held)
            ln_quant_stage(tok, xq8, work)
            cross_w = cross_chunks(tok, aw, wqxT, wkvxT, wprojT)
            attention_stage(tok, "self", xq8, aw, work, cross_w, ctxT)
            attention_stage(tok, "cross", xq8, aw, work, cross_w, ctxT)
        routed_ffn_stage(tok, routerT, fw1T, fw2T, fb2, out)


LN_BEFORE = {"wkv": 0, "ternary": 1, "quant": 2, "routed": 4}



def rsqrt_newton(dve_chain, nc, y, y0, v, t):
    dve_chain(nc.vector.scalar_tensor_tensor(t, y0, -0.5, y0, ALU.mult, ALU.mult))
    dve_chain(nc.vector.tensor_tensor(t, t, v, ALU.mult))
    dve_chain(nc.vector.scalar_tensor_tensor(y, t, 1.5, y0, ALU.add, ALU.mult))


def dve_mean_var(k, chain, var_ready):
    nc, st6, (a, b, c) = k["nc"], k["stat6"], k["st"]
    me, m2e, mo, m2o = (st6[:, :, i] for i in (1, 2, 4, 5))
    chain.mark(nc.vector.tensor_tensor(a[:], me, mo, ALU.subtract))
    chain.mark(nc.vector.tensor_tensor(b[:], m2e, m2o, ALU.add))
    chain(nc.vector.tensor_tensor(c[:], me, mo, ALU.add))
    chain.mark(nc.vector.tensor_tensor(a[:], a[:], a[:], ALU.mult))
    chain.mark(nc.vector.tensor_scalar(b[:], b[:], 1.0 / C, None, ALU.mult))
    chain(nc.vector.tensor_scalar(k["mean"][:], c[:], 0.5, None, ALU.mult))
    chain(nc.vector.scalar_tensor_tensor(k["var0"][:], a[:], 0.25, b[:], ALU.mult, ALU.add))
    nc.vector.tensor_scalar(k["var"][:], k["var0"][:], LN_EPS, None, ALU.add).then_inc(var_ready, 1)


def act_rsqrt(act, nc, dst, v, tmp, var_ready, count, act_chain, rs_ready):
    act.wait_ge(var_ready, count)
    act_chain(nc.scalar.activation(tmp, v, ACT.Ln))
    nc.scalar.activation(dst, tmp, ACT.Exp, scale=-0.5).then_inc(rs_ready, 1)



HC = -(-HID // P)
TAIL = HID - (HC - 1) * P


def ternary_weights(k, work, stack):
    return dict(raw13=[work[n][:, 0:KC * HID].rearrange("p (h n) -> p h n", h=KC) for n in range(2)],
                raw2=work[2][:, 0:HC * C].rearrange("p (a n) -> p a n", a=HC),
                asum=stack.enter_context(k["nc"].sbuf_tensor("asum", [P, 8], F32)),
                arrived=[k["sem"](f"tw_arrived{i}") for i in range(2)])


def load_ternary_weights(sp, tw, w1T, w3T, w2T):
    for raw, w in zip(tw["raw13"], (w1T, w3T)):
        sp.dma_start(raw, w.rearrange("(h p) n -> p h n", p=P)).then_inc(tw["arrived"][0], 16)
    full = (HC - 1) * P
    sp.dma_start(tw["raw2"][:, 0:HC - 1, :], w2T[0:full, :].rearrange("(a p) n -> p a n", p=P)
                 ).then_inc(tw["arrived"][1], 16)
    sp.dma_start(tw["raw2"][0:TAIL, HC - 1, :], w2T[full:HID, :]).then_inc(tw["arrived"][1], 16)


def sum_ternary_weights(act, nc, tw, unused, chain):
    parts = [raw[:, h, :] for raw in tw["raw13"] for h in range(KC)]
    half = (HC - 1) * C // 2
    flat = tw["raw2"][:, 0:HC - 1, :].rearrange("p a n -> p (a n)")
    parts += [flat[:, i * half:(i + 1) * half] for i in range(2)] + [tw["raw2"][0:TAIL, HC - 1, :]]
    for i, part in enumerate(parts):
        if i in (0, 2 * KC):
            act.wait_ge(tw["arrived"][i // (2 * KC)], 32)
        rows, n = part.shape
        chain(nc.scalar.activation(unused[0:rows, 0:n], part, ACT.Abs, accum_out=tw["asum"][0:rows, i:i + 1]))



def wkv_stage(k, x, ctxT, params, ternary_w):
    nc, sem, x_res, col, ident = k["nc"], k["sem"], k["x_res"], k["col"], k["ident"]
    BQ = B // 2
    L = S + 1
    CHUNKS = [(h, q) for h in range(KC) for q in range(2)]
    with ExitStack() as own:
        def sb(name, shape, dt=F32):
            return own.enter_context(nc.sbuf_tensor(name, shape, dt))

        def psum(name, shape, dt=F32):
            return own.enter_context(nc.psum_tensor(name, shape, dt))

        z = sb("wkv_z", [P, NT, C])
        vT = sb("vT", [P, KC, B, S])
        k65 = sb("k65", [P, KC, B, L])
        w65 = sb("w65", [P, KC, BQ, L])
        yT = z[:].rearrange("p j c -> p (j c)").rearrange("p (h b s) -> p h b s", h=KC, b=B)
        names = "o A2 E2 E2v p q"
        buf = {n: [sb(f"{n}{i}", [P, BQ, L]) for i in range(2)] for n in names.split()}
        for n in "d A E Ev Ap Aq".split():
            buf[n] = [sb(f"{n}_{i}", [P, BQ, S]) for i in range(2)]
        zT_ps = [psum(f"zT_ps{i}", [P, 512]) for i in range(4)]
        y_ps = [psum(f"y_ps{i}", [P, 512]) for i in range(2)]

        x_in = [sem(f"x_in{i}") for i in range(4)]
        par_in, v_in = sem("par_in"), [sem(f"v_in{i}") for i in range(KC)]
        consts, fills = sem("consts"), sem("wkv_fills")
        var_ready, rs_ready = k["ln_var_ready"], k["ln_rs_ready"]
        z_ready, zT_ready, k_ready = sem("wkv_z_ready"), sem("wkv_zT_ready"), sem("wkv_k_ready")
        gaps_ready, exps_ready = sem("wkv_gaps_ready"), sem("wkv_exps_ready")
        E2v_ready, Ev_ready = sem("wkv_E2v_ready"), sem("wkv_Ev_ready")
        pq_ready, Apq_ready = sem("wkv_pq_ready"), sem("wkv_Apq_ready")
        den_ready, rcp_ready = sem("wkv_den_ready"), sem("wkv_rcp_ready")
        y_ready, yt_ready, x_added = sem("wkv_y_ready"), sem("wkv_yt_ready"), sem("wkv_x_added")

        with nc.Block() as block:
            @block.sync
            def _(sp):
                sp.dma_start(k["par"][:], params).then_inc(par_in, 16)
                xr = x.rearrange("(j p) c -> p j c", p=P)
                for i in range(4):
                    sp.dma_start(x_res[:, 4 * i:4 * i + 4, :], xr[:, 4 * i:4 * i + 4, :]).then_inc(x_in[i], 16)
                for h in range(KC):
                    sp.dma_start(vT[:, h, :, :], ctxT[h * P:(h + 1) * P, :].rearrange("p (b s) -> p b s", s=S)
                                 ).then_inc(v_in[h], 16)
                load_ternary_weights(sp, k["tw"], *ternary_w)

            @block.gpsimd
            def _(pool):
                nc.gpsimd.memset(ident[:], 0.0).then_inc(consts, 1)
                nc.gpsimd.memset(k["ones"][:], 1.0).then_inc(consts, 1)
                pool.wait_ge(consts, 2)
                nc.gpsimd.affine_select(out=ident[:], in_=ident[:], compare_op=ALU.not_equal, fill=1.0, base=0,
                                        pattern=[[-1, P]], channel_multiplier=1).then_inc(consts, 1)
                nc.gpsimd.memset(k["tw"]["asum"][:], 0.0).then_inc(fills, 1)
                nc.gpsimd.memset(k65[:, :, :, 0], NEG_BIG).then_inc(fills, 1)
                nc.gpsimd.memset(w65[:], 0.0).then_inc(fills, 1)
                for n in ("A2", "E2", "E2v"):
                    for i in range(2):
                        nc.gpsimd.memset(buf[n][i][:, :, 0], 0.0).then_inc(fills, 1)
                for c, (h, q) in enumerate(CHUNKS):
                    i = c % 2
                    v = vT[:, h, BQ * q:BQ * (q + 1), :]
                    if c == 0:
                        pool.wait_ge(fills, 9)
                    if q == 0:
                        pool.wait_ge(v_in[h], 16)
                    pool.wait_ge(exps_ready, 4 * c + 2)
                    if c >= 2:
                        pool.wait_ge(pq_ready, 2 * (c - 1))
                    nc.gpsimd.tensor_tensor(buf["E2v"][i][:, :, 1:], buf["E2"][i][:, :, 1:], v, ALU.mult
                                            ).then_inc(E2v_ready, 1)
                    pool.wait_ge(exps_ready, 4 * c + 4)
                    nc.gpsimd.tensor_tensor(buf["Ev"][i][:], buf["E"][i][:], v, ALU.mult).then_inc(Ev_ready, 1)
                    pool.wait_ge(pq_ready, 2 * c + 1)
                    nc.gpsimd.tensor_tensor(buf["Ap"][i][:], buf["A"][i][:], buf["p"][i][:, :, 0:S], ALU.mult
                                            ).then_inc(Apq_ready, 1)
                    pool.wait_ge(pq_ready, 2 * c + 2)
                    nc.gpsimd.tensor_tensor(buf["Aq"][i][:], buf["A"][i][:], buf["q"][i][:, :, 0:S], ALU.mult
                                            ).then_inc(Apq_ready, 1)

            @block.vector
            def _(dve):
                chain = k["dve_chain"].on(dve)
                for j in range(NT):
                    if j % 4 == 0:
                        dve.wait_ge(x_in[j // 4], 16)
                    chain.mark(nc.vector.bn_stats(k["stat6"][:, j, :], x_res[:, j, :]))
                chain.settle()
                dve_mean_var(k, chain, var_ready)
                dve.wait_ge(rs_ready, LN_BEFORE["wkv"] + 1)
                dve.wait_ge(var_ready, LN_BEFORE["wkv"] + 1)
                rsqrt_newton(chain, nc, k["rstd"][:], k["rs0"][:], k["var"][:], k["st"][0][:])
                for j in range(NT):
                    nc.vector.tensor_scalar(z[:, j, :], x_res[:, j, :], k["mean"][:, j:j + 1],
                                            k["rstd"][:, j:j + 1], ALU.subtract, ALU.mult).then_inc(z_ready, 1)
                dve.wait_ge(par_in, 16)
                dve.wait_ge(fills, 9)
                for h in range(KC):
                    chain.mark(nc.vector.tensor_scalar(w65[:, h, :, 1:], w65[:, h, :, 1:], col("w", h), None, ALU.add))
                    chain.mark(nc.vector.memset(w65[:, h, :, 0], NEG_BIG))

                def flat(t):
                    return t.rearrange("p b l -> p (b l)")

                def gaps(c):
                    h, q = CHUNKS[c]
                    i = c % 2
                    if c >= 2:
                        dve.wait_ge(y_ready, c - 1)
                        dve.wait_ge(pq_ready, 2 * (c - 1))
                    kk = k65[:, h, BQ * q:BQ * (q + 1), :]
                    o = buf["o"][i]
                    if q == 0:
                        dve.wait_ge(k_ready, 4 * h + 4)
                    chain.settle()
                    chain(nc.vector.tensor_tensor_scan(flat(o[:]), flat(w65[:, h]), flat(kk), NEG_BIG,
                                                       ALU.add, ALU.max))
                    if c >= 2:
                        dve.wait_ge(E2v_ready, c - 1)
                        dve.wait_ge(Apq_ready, 2 * (c - 1))
                        dve.wait_ge(Ev_ready, c - 1)
                    nc.vector.tensor_tensor(buf["E2"][i][:, :, 1:], kk[:, :, 1:], o[:, :, 1:], ALU.subtract
                                            ).then_inc(gaps_ready, 1)
                    nc.vector.scalar_tensor_tensor(buf["A2"][i][:, :, 1:], o[:, :, 0:S], col("w", h), o[:, :, 1:],
                                                   ALU.add, ALU.subtract).then_inc(gaps_ready, 1)

                def output_gap(c):
                    h, q = CHUNKS[c]
                    i = c % 2
                    nc.vector.scalar_tensor_tensor(buf["d"][i][:], k65[:, h, BQ * q:BQ * (q + 1), 1:], col("u", h),
                                                   buf["o"][i][:, :, 0:S], ALU.add, ALU.subtract
                                                   ).then_inc(gaps_ready, 1)

                def scans(c):
                    t = {n: buf[n][c % 2] for n in buf}
                    dve.wait_ge(exps_ready, 4 * c + 2)
                    dve.wait_ge(E2v_ready, c + 1)
                    if c >= 2:
                        dve.wait_ge(Apq_ready, 2 * (c - 1))
                    nc.vector.tensor_tensor_scan(flat(t["p"][:]), flat(t["A2"][:]), flat(t["E2v"][:]), 0.0,
                                                 ALU.mult, ALU.add).then_inc(pq_ready, 1)
                    nc.vector.tensor_tensor_scan(flat(t["q"][:]), flat(t["A2"][:]), flat(t["E2"][:]), 0.0,
                                                 ALU.mult, ALU.add).then_inc(pq_ready, 1)

                def fraction(c):
                    t = {n: buf[n][c % 2] for n in buf}
                    dve.wait_ge(Apq_ready, 2 * c + 2)
                    dve.wait_ge(Ev_ready, c + 1)
                    nc.vector.tensor_tensor(t["Aq"][:], t["Aq"][:], t["E"][:], ALU.add).then_inc(den_ready, 1)
                    chain(nc.vector.tensor_tensor(t["Ap"][:], t["Ap"][:], t["Ev"][:], ALU.add))

                def ratio(c):
                    h, q = CHUNKS[c]
                    if c == 0:
                        dve.wait_ge(zT_ready, 2 * (NT // 4))
                    t = {n: buf[n][c % 2] for n in buf}
                    dve.wait_ge(den_ready, c + 1)
                    dve.wait_ge(rcp_ready, c + 1)
                    chain(nc.vector.tensor_tensor(t["Aq"][:], t["Aq"][:], t["d"][:], ALU.mult))
                    chain(nc.vector.scalar_tensor_tensor(t["d"][:], t["Aq"][:], -2.0, t["d"][:], ALU.add, ALU.mult))
                    nc.vector.scalar_tensor_tensor(yT[:, h, BQ * q:BQ * (q + 1), :], t["Ap"][:], -1.0, t["d"][:],
                                                   ALU.mult, ALU.mult).then_inc(y_ready, 1)

                def add_y(m):
                    dve.wait_ge(yt_ready, m + 1)
                    nc.vector.tensor_tensor(x_res[:, 2 * m:2 * m + 2, :], x_res[:, 2 * m:2 * m + 2, :],
                                            y_ps[m % 2][:].rearrange("p (j c) -> p j c", j=2), ALU.add
                                            ).then_inc(x_added, 1)
                    if m:
                        stats(m - 1)

                def stats(m):
                    dve.wait_ge(x_added, m + 1)
                    for j in (2 * m, 2 * m + 1):
                        chain.mark(nc.vector.bn_stats(k["stat6"][:, j, :], x_res[:, j, :]))

                gaps(0)
                output_gap(0)
                for c in range(len(CHUNKS)):
                    more = c + 1 < len(CHUNKS)
                    scans(c)
                    if more:
                        gaps(c + 1)
                        output_gap(c + 1)
                    else:
                        add_y(0)
                        add_y(1)
                    fraction(c)
                    if not more:
                        add_y(2)
                        add_y(3)
                    ratio(c)
                for m in range(4, NT // 2):
                    add_y(m)
                stats(NT // 2 - 1)

            @block.scalar
            def _(act):
                chain = k["act_chain"].on(act)
                nc.scalar.preload_act_table_set(LN_EXP_SET)
                act_rsqrt(act, nc, k["rs0"][:], k["var"][:], k["st"][2][:], var_ready, LN_BEFORE["wkv"] + 1,
                          chain, rs_ready)
                for n in range(2 * (NT // 4)):
                    h, g = divmod(n, NT // 4)
                    act.wait_ge(zT_ready, n + 1)
                    nc.scalar.activation(k65[:, h, 8 * g:8 * g + 8, 1:], zT_ps[n % 4][:].rearrange("p (b s) -> p b s", s=S),
                                         ACT.Copy).then_inc(k_ready, 1)

                def exps(c):
                    t = {n: buf[n][c % 2] for n in buf}
                    act.wait_ge(gaps_ready, 3 * c + 1)
                    nc.scalar.activation(t["E2"][:, :, 1:], t["E2"][:, :, 1:], ACT.Exp).then_inc(exps_ready, 1)
                    act.wait_ge(gaps_ready, 3 * c + 2)
                    nc.scalar.activation(t["A2"][:, :, 1:], t["A2"][:, :, 1:], ACT.Exp).then_inc(exps_ready, 1)

                def output_exps(c):
                    t = {n: buf[n][c % 2] for n in buf}
                    act.wait_ge(gaps_ready, 3 * c + 3)
                    chain.mark(nc.scalar.activation(t["A"][:], t["d"][:], ACT.Relu))
                    chain(nc.scalar.activation(t["E"][:], t["d"][:], ACT.Relu, scale=-1.0))
                    nc.scalar.activation(t["A"][:], t["A"][:], ACT.Exp, scale=-1.0).then_inc(exps_ready, 1)
                    nc.scalar.activation(t["E"][:], t["E"][:], ACT.Exp, scale=-1.0).then_inc(exps_ready, 1)

                def guess_rcp(c):
                    t = {n: buf[n][c % 2] for n in buf}
                    act.wait_ge(den_ready, c + 1)
                    act.wait_ge(exps_ready, 4 * c + 4)
                    chain(nc.scalar.activation(t["d"][:], t["Aq"][:], ACT.Ln))
                    nc.scalar.activation(t["d"][:], t["d"][:], ACT.Exp, scale=-1.0).then_inc(rcp_ready, 1)

                exps(0)
                output_exps(0)
                for c in range(len(CHUNKS)):
                    if c + 1 < len(CHUNKS):
                        exps(c + 1)
                    guess_rcp(c)
                    if c + 1 < len(CHUNKS):
                        output_exps(c + 1)
                act.wait_ge(fills, 9)
                sum_ternary_weights(act, nc, k["tw"], buf["o"][0][:].rearrange("p b l -> p (b l)"), chain)

            @block.tensor
            def _(pe):
                pe.wait_ge(consts, 3)
                for n in range(2 * (NT // 4)):
                    h, g = divmod(n, NT // 4)
                    pe.wait_ge(z_ready, 4 * g + 4)
                    if n >= 4:
                        pe.wait_ge(k_ready, n - 3)
                    for j in range(4):
                        last = nc.tensor.transpose(zT_ps[n % 4][:, j * P:(j + 1) * P],
                                                   z[:, 4 * g + j, h * P:(h + 1) * P], ident[:])
                    last.then_inc(zT_ready, 1)
                for m in range(NT // 2):
                    pe.wait_ge(y_ready, len(CHUNKS) - 1 + m // (NT // 4))
                    if m >= 2:
                        pe.wait_ge(x_added, m - 1)
                    for j in range(2):
                        for h in range(KC):
                            t0 = (2 * m + j) * P
                            last = nc.tensor.transpose(y_ps[m % 2][:, (2 * j + h) * P:(2 * j + h + 1) * P],
                                                       yT[:, h].rearrange("p b s -> p (b s)")[:, t0:t0 + P], ident[:])
                    last.then_inc(yt_ready, 1)



def pipeline(eng, step, rounds, width, lag, peel_last=False, peel=1):
    for i in range(peel):
        for o in range(width):
            step(i, o)
    with eng.Fori(peel, rounds - peel_last) as i:
        for o in range(width):
            step(i, o)
    if peel_last:
        for o in range(width):
            step(rounds - 1, o)
    for o in range(lag):
        step(rounds, o)


class Unit:

    def __init__(self, i, o, width, rounds, back=0):
        static = isinstance(i, int)
        self.n = width * i + o - back
        self.o = (o - back) % width
        self.live = not static or 0 <= self.n < width * rounds
        self.static = static

    def count(self, per=1, more=0):
        return self.n * per + more

    def before(self, units, per=1):
        if self.static and self.n < units:
            return None
        return (self.n - units + 1) * per


def wait_unit(eng, sem, value):
    if value is not None:
        eng.wait_ge(sem, value)



def attention_weights(k, stack):
    nc, sem = k["nc"], k["sem"]

    def pair(name, shape):
        return [stack.enter_context(nc.sbuf_tensor(f"{name}{p}", shape, F32R)) for p in range(2)]

    return dict(
        q=pair("wq", [P, KC, NH * D]), k=pair("wk", [P, KC, G * D]), v=pair("wv", [P, KC, G * D]),
        p=pair("wp", [P, NH, C]),
        sums=stack.enter_context(nc.sbuf_tensor("w_sums", [P, 3, NH], F32)),
        scales=stack.enter_context(nc.sbuf_tensor("w_scales", [P, 4 * KC], F32)),
        arrived=[sem(f"w_arrived{i}") for i in range(6)], scales_ready=sem("w_scales_ready"),
        sums_ready=sem("w_sums_ready"), scaled=sem("w_scaled"), centred=sem("w_centred"), upper=sem("w_upper"),
        lower_pool=sem("w_lower_pool"), lower_dve=sem("w_lower_dve"))


class Chunk:

    def __init__(self, pair, pick, src, centred=False, scales=()):
        self.src, self.centred, self.scales = src, centred, scales
        self.upper, self.lower = (pick(t) if len(pick(t).shape) == 2 else pick(t).rearrange("p a n -> p (a n)")
                                  for t in pair)

    def scale_of(self, head):
        return self.scales[head * len(self.scales) // NH]


def heads_of(w):
    return w.rearrange("p (h d) -> p h d", d=D)


def proj_chunks(aw, wprojT, row0):
    half = NH // 2
    return [Chunk(aw["p"], lambda t, a=a: t[:, a * half:(a + 1) * half, :],
                  wprojT[row0 + a * half * D:row0 + (a + 1) * half * D, :].rearrange("(c p) n -> p c n", p=P))
            for a in range(2)]


def self_chunks(k, aw, wqT, wkT, wvT, wprojT):
    def scale(kind, h):
        return aw["scales"][:, kind * KC + h:kind * KC + h + 1]

    def halves(w):
        return w.rearrange("(h p) n -> p h n", p=P)

    q = [Chunk(aw["q"], lambda t, h=h: t[:, h, :], wqT[h * P:(h + 1) * P, :], True, [scale(0, h)])
         for h in range(KC)]
    return q + [Chunk(aw["k"], lambda t: t[:], halves(wkT), True, [scale(1, h) for h in range(KC)]),
                Chunk(aw["v"], lambda t: t[:], halves(wvT), False, [scale(2, h) for h in range(KC)])
                ] + proj_chunks(aw, wprojT, 0)


def cross_chunks(k, aw, wqxT, wkvxT, wprojT):
    kv = wkvxT.rearrange("(h p) n -> p h n", p=P)
    q = [Chunk(aw["q"], lambda t, h=h: t[:, h, :], wqxT[h * P:(h + 1) * P, :], True,
               [aw["scales"][:, 3 * KC + h:3 * KC + h + 1]]) for h in range(KC)]
    return q + [Chunk(aw["k"], lambda t: t[:], kv[:, :, 0:G * D], True),
                Chunk(aw["v"], lambda t: t[:], kv[:, :, G * D:2 * G * D])] + proj_chunks(aw, wprojT, NH * D)


def load_weights(sp, aw, work, chunks, wait_free, first=0, last=6):
    for i in range(first, last):
        c = chunks[i]
        if i >= len(work):
            wait_free(i - len(work))
        w = work[i % len(work)][:]
        dst = w if len(c.src.shape) == 2 else w.rearrange("p (a n) -> p a n", a=c.src.shape[1])
        sp.dma_start(dst, c.src).then_inc(aw["arrived"][i], 16)


def lower_part(eng, aw, work, chunks, i, nth_upper, done):
    eng.wait_ge(aw["upper"], nth_upper + 1)
    c = chunks[i]
    eng.tensor_tensor(c.lower, work[i % len(work)][:], c.upper.bitcast(F32), ALU.subtract).then_inc(done, 1)


N_CHUNKS, N_CENTRED, N_SCALED = 6, 3, 4
CROSS_ON_DVE, CROSS_ON_POOL = (0, 1, 3), (2, 4, 5)


def self_weights_act(act, nc, aw, work, chunks):
    act.wait_ge(aw["scales_ready"], 4)
    for i, c in enumerate(chunks[0:N_CENTRED]):
        act.wait_ge(aw["arrived"][i], 16)
        for h in range(NH):
            head = heads_of(work[i][:])[:, h, :]
            last = nc.scalar.activation(head, head, ACT.Copy, scale=c.scale_of(h), accum_out=aw["sums"][:, i, h:h + 1])
        last.then_inc(aw["scaled"], 1)


def self_weights_pool(pool, nc, aw, work, chunks, col):
    for n, (scales, wscale) in enumerate((("sq", "wq_s"), ("sk", "wk_s"), ("sv", "wv_s"), ("sqx", "wqx_s"))):
        nc.gpsimd.tensor_scalar(aw["scales"][:, n * KC:(n + 1) * KC], col(scales, 0, KC), col(wscale), None,
                                ALU.mult).then_inc(aw["scales_ready"], 1)
    for i, c in enumerate(chunks):
        w = work[i % len(work)][:]
        if c.centred:
            pool.wait_ge(aw["scaled"], i + 1)
            nc.gpsimd.tensor_scalar(aw["sums"][:, i, :], aw["sums"][:, i, :], -1.0 / D, None, ALU.mult
                                    ).then_inc(aw["sums_ready"], 1)
            pool.wait_ge(aw["sums_ready"], i + 1)
            nc.gpsimd.tensor_tensor(heads_of(w), heads_of(w),
                                    aw["sums"][:, i, :].unsqueeze(2).broadcast_to([P, NH, D]), ALU.add
                                    ).then_inc(aw["centred"], 1)
            pool.wait_ge(aw["centred"], i + 1)
        else:
            pool.wait_ge(aw["arrived"][i], 16)
            if c.scales:
                for h in range(KC):
                    half = w[:, h * G * D:(h + 1) * G * D]
                    last = nc.gpsimd.tensor_scalar(half, half, c.scales[h], None, ALU.mult)
                last.then_inc(aw["scaled"], 1)
                pool.wait_ge(aw["scaled"], i + 1)
        nc.gpsimd.tensor_copy(c.upper, w).then_inc(aw["upper"], 1)
        lower_part(nc.gpsimd, aw, work, chunks, i, i, aw["lower_pool"])


class CrossHead:
    PER_ROUND = 6
    WITH_UNITS = (1, 2, 3, 5, 6, 7)

    def __init__(self, aw, work, i, o):
        o = self.WITH_UNITS.index(o)
        self.chunk, self.first = o // 2, o % 2 == 0
        self.head = 2 * i + o % 2
        self.count = self.PER_ROUND * i + o + 1
        self.w = work[self.chunk][:, bass.ds(self.head * D, D)]
        self.sum = aw["sums"][:, self.chunk, bass.ds(self.head, 1)]


def cross_head_act(act, nc, aw, work, chunks, i, o):
    c = CrossHead(aw, work, i, o)
    if c.first and isinstance(i, int) and i == 0:
        act.wait_ge(aw["arrived"][c.chunk], 32)
    scales = chunks[c.chunk].scales
    nc.scalar.activation(c.w, c.w, ACT.Copy, scale=scales[0] if scales else 1.0, accum_out=c.sum
                         ).then_inc(aw["scaled"], 1)


def cross_head_pool(pool, nc, aw, work, minus_mean, i, o):
    c = CrossHead(aw, work, i, o)
    pool.wait_ge(aw["scaled"], N_SCALED + c.count)
    nc.gpsimd.tensor_tensor(c.sum, c.sum, minus_mean, ALU.mult).then_inc(aw["sums_ready"], 1)
    pool.wait_ge(aw["sums_ready"], N_CENTRED + c.count)
    nc.gpsimd.tensor_tensor(c.w, c.w, c.sum.broadcast_to([P, D]), ALU.add).then_inc(aw["centred"], 1)


def cross_weights_act(act, nc, aw, work, chunks):
    for i, c in enumerate(chunks):
        if not c.centred:
            act.wait_ge(aw["arrived"][i], 32)
        nc.scalar.activation(c.upper, work[i % len(work)][:], ACT.Copy).then_inc(aw["upper"], 1)


def cross_weights_dve(dve, nc, aw, work, chunks):
    for i in CROSS_ON_DVE:
        lower_part(nc.vector, aw, work, chunks, i, N_CHUNKS + i, aw["lower_dve"])



def ternary_ffn_stage(k, aw, self_w):
    nc, sem, x_res, ident = k["nc"], k["sem"], k["x_res"], k["ident"]
    BANK = 512
    HH = HID // 2
    WIDTH = 4
    ROUNDS = NT // WIDTH
    with ExitStack() as own:
        def sb(name, shape, dt=F32):
            return own.enter_context(nc.sbuf_tensor(name, shape, dt))

        def psum(name, shape, dt=F32):
            return own.enter_context(nc.psum_tensor(name, shape, dt))

        raw13, raw2, asum = (k["tw"][n] for n in ("raw13", "raw2", "asum"))
        w13q = [sb(f"w{n}q", [P, KC, HID], BF16) for n in (1, 3)]
        w2q = sb("w2q", [P, HC, C], BF16)
        ws = sb("ws", [P, 4])
        iws = sb("iws", [P, 4])
        z = sb("tf_z", [P, NT, C])
        work = [sb(f"tf_work{i}", [P, KC * G * D]) for i in range(3)]
        amax = sb("tf_amax", [P, NT])
        qs = sb("tf_qs", [P, NT])
        tsc = sb("tf_tsc", [P, NT, 2])
        cur = [sb(f"tf_cur{i}", [P, 2]) for i in range(4)]
        xq = [sb(f"tf_xq{i}", [P, C], BF16) for i in range(2)]
        xqT = [sb(f"tf_xqT{i}", [P, C], BF16) for i in range(2)]
        gate = sb("tf_gate", [P, HID])
        hm = sb("tf_hm", [P, HID])
        hr = sb("tf_hr", [P, HID])
        hq = [sb(f"tf_hq{i}", [P, HID], BF16) for i in range(2)]
        hqT = [sb(f"tf_hqT{i}", [P, HC * P], BF16) for i in range(2)]
        small = sb("tf_small", [P, 4])
        gam = [sb(f"tf_gam{i}", [P, 1]) for i in range(4)]
        identb = sb("identb", [P, P], BF16)
        xT_ps = psum("tf_xT_ps", [P, 2 * BANK], BF16)
        h1_ps = [psum(f"h1_ps{i}", [P, BANK]) for i in range(2)]
        h3_ps = [psum(f"h3_ps{i}", [P, BANK]) for i in range(2)]
        hT_ps = psum("hT_ps", [P, 2 * BANK], BF16)
        y_ps = psum("tf_y_ps", [P, BANK])

        idb_ready, wsum_ready, w_ready = sem("idb_ready"), sem("wsum_ready"), sem("tf_w_ready")
        var_ready, rs_ready = k["ln_var_ready"], k["ln_rs_ready"]
        unit_done = sem("tf_unit_done")
        xq_ready, xT_ready, xqT_ready = sem("tf_xq_ready"), sem("tf_xT_ready"), sem("tf_xqT_ready")
        h_ready, gate_ready, hm_ready = sem("tf_h_ready"), sem("tf_gate_ready"), sem("tf_hm_ready")
        hq_ready, hT_ready, hqT_ready = sem("tf_hq_ready"), sem("tf_hT_ready"), sem("tf_hqT_ready")
        y_ready, x_added = sem("tf_y_ready"), sem("tf_x_added")

        with nc.Block() as block:
            @block.sync
            def _(sp):
                load_weights(sp, aw, work, self_w, lambda i: sp.wait_ge(aw["lower_pool"], i + 1))

            @block.gpsimd
            def _(pool):
                nc.gpsimd.tensor_copy(identb[:], ident[:]).then_inc(idb_ready, 1)
                self_weights_pool(pool, nc, aw, work, self_w, k["col"])

            @block.vector
            def _(dve):
                chain = k["dve_chain"].on(dve)
                dve_mean_var(k, chain, var_ready)
                dve.wait_ge(wsum_ready, 1)
                chain(nc.vector.tensor_reduce(ws[:, 0:3], y_ps[:, 0:6].rearrange("p (a b) -> p a b", b=2), AX.X,
                                              ALU.add))
                chain(nc.vector.tensor_tensor(ws[:, 2:3], y_ps[:, 6:7], ws[:, 2:3], ALU.add))
                chain(nc.vector.tensor_scalar(ws[:, 0:3], ws[:, 0:3], 1.0 / (HID * C), QUANT_EPS, ALU.mult, ALU.max))
                chain(nc.vector.reciprocal(iws[:, 0:3], ws[:, 0:3]))
                dve.wait_ge(rs_ready, LN_BEFORE["ternary"] + 1)
                dve.wait_ge(var_ready, LN_BEFORE["ternary"] + 1)
                rsqrt_newton(chain, nc, k["rstd"][:], k["rs0"][:], k["var"][:], k["st"][0][:])
                for j in range(NT):
                    chain.mark(nc.vector.tensor_scalar(z[:, j, :], x_res[:, j, :], k["mean"][:, j:j + 1],
                                                       k["rstd"][:, j:j + 1], ALU.subtract, ALU.mult))
                chain.settle()
                def ternary(raw, n, dst):
                    chain(nc.vector.tensor_scalar(raw, raw, iws[0:raw.shape[0], n:n + 1], ROUND32, ALU.mult, ALU.add))
                    chain(nc.vector.tensor_scalar(raw, raw, -ROUND32, 1.0, ALU.add, ALU.min))
                    nc.vector.tensor_scalar(dst, raw, -1.0, None, ALU.max).then_inc(w_ready, 1)

                for n in range(2):
                    ternary(raw13[n], n, w13q[n][:])
                ternary(raw2[:, 0:HC - 1, :], 2, w2q[:, 0:HC - 1, :])
                ternary(raw2[0:TAIL, HC - 1, :], 2, w2q[0:TAIL, HC - 1, :])
                chain(nc.vector.tensor_reduce(amax[:], z[:], AX.X, ALU.max, apply_absolute_value=True))
                chain(nc.vector.tensor_scalar(amax[:], amax[:], QUANT_EPS, 1.0 / 127.0, ALU.max, ALU.mult))
                chain.mark(nc.vector.tensor_scalar(tsc[:, :, 0], amax[:], ws[:, 0:1], None, ALU.mult))
                chain.mark(nc.vector.tensor_scalar(tsc[:, :, 1], amax[:], ws[:, 1:2], None, ALU.mult))
                chain(nc.vector.reciprocal(qs[:], amax[:]))
                for j in range(NT):
                    chain.mark(nc.vector.tensor_scalar(z[:, j, :], z[:, j, :], qs[:, j:j + 1], ROUND32,
                                                       ALU.mult, ALU.add))
                chain.settle()
                steps = Chain(dve, unit_done)

                def step(i, o):
                    u, mid, late = (Unit(i, o, WIDTH, ROUNDS, b) for b in (0, 2, 4))
                    if mid.live:
                        steps.at(mid.count(6))
                        for c in range(2):
                            dve.wait_ge(gate_ready, mid.count(2, c + 1))
                            nc.vector.tensor_tensor(hm[:, c * HH:(c + 1) * HH], gate[:, c * HH:(c + 1) * HH],
                                                    h3_ps[c][:, 0:HH], ALU.mult).then_inc(hm_ready, 1)
                        dve.wait_ge(hm_ready, mid.count(2, 2))
                        steps.mark(nc.vector.tensor_reduce(small[:, 0:1], hm[:], AX.X, ALU.max,
                                                           apply_absolute_value=True))
                    if u.live:
                        wait_unit(dve, xT_ready, u.before(2))
                        wait_unit(dve, gate_ready, u.before(4, 2))
                        nc.vector.tensor_scalar(xq[u.o % 2][:], z[:, bass.ds(u.n, 1), :].rearrange("p a c -> p (a c)"),
                                                -ROUND32, None, ALU.add).then_inc(xq_ready, 1)
                        nc.vector.tensor_copy(cur[u.o][:], tsc[:, bass.ds(u.n, 1), :].rearrange("p a c -> p (a c)")
                                              ).then_inc(xq_ready, 1)
                    if mid.live:
                        steps.settle()
                        dve.wait_ge(xq_ready, mid.count(2, 2))
                        steps(nc.vector.tensor_scalar(small[:, 0:1], small[:, 0:1], cur[mid.o][:, 1:2], QUANT_EPS,
                                                      ALU.mult, ALU.max))
                        steps.mark(nc.vector.reciprocal(small[:, 1:2], small[:, 0:1]))
                        wait_unit(dve, x_added, mid.before(4))
                        steps(nc.vector.tensor_scalar(gam[mid.o][:], small[:, 0:1], ws[:, 2:3], 1.0 / 127.0,
                                                      ALU.mult, ALU.mult))
                        steps.mark(nc.vector.tensor_scalar(small[:, 2:3], small[:, 1:2], cur[mid.o][:, 1:2], 127.0,
                                                           ALU.mult, ALU.mult))
                    if late.live:
                        dve.wait_ge(y_ready, late.count(1, 1))
                        xt = x_res[:, bass.ds(late.n, 1), :].rearrange("p a c -> p (a c)")
                        nc.vector.scalar_tensor_tensor(xt, y_ps[:, 0:C], gam[late.o][:], xt, ALU.mult, ALU.add
                                                       ).then_inc(x_added, 1)
                    if mid.live:
                        steps.settle()
                        steps(nc.vector.tensor_scalar(hr[:], hm[:], small[:, 2:3], ROUND32, ALU.mult, ALU.add))
                        wait_unit(dve, hT_ready, mid.before(2))
                        nc.vector.tensor_scalar(hq[mid.o % 2][:], hr[:], -ROUND32, None, ALU.add).then_inc(hq_ready, 1)
                        dve.wait_ge(hq_ready, mid.count(1, 1))

                pipeline(dve, step, ROUNDS, WIDTH, 4, peel=2)

            @block.scalar
            def _(act):
                chain = k["act_chain"].on(act)
                nc.scalar.preload_act_table_set(LN_EXP_SET)
                act_rsqrt(act, nc, k["rs0"][:], k["var"][:], k["st"][2][:], var_ready, LN_BEFORE["ternary"] + 1,
                          chain, rs_ready)
                self_weights_act(act, nc, aw, work, self_w)
                nc.scalar.preload_act_table(ACT.Silu)

                def step(i, o):
                    u, mid, late = (Unit(i, o, WIDTH, ROUNDS, b) for b in (0, 1, 3))
                    if mid.live:
                        for c in range(2):
                            act.wait_ge(h_ready, mid.count(2, c + 1))
                            act.wait_ge(xq_ready, mid.count(2, 2))
                            wait_unit(act, hm_ready, mid.before(1, 2))
                            nc.scalar.activation(gate[:, c * HH:(c + 1) * HH], h1_ps[c][:, 0:HH], ACT.Silu,
                                                 scale=cur[mid.o][:, 0:1]).then_inc(gate_ready, 1)
                    if late.live:
                        par = late.o % 2
                        act.wait_ge(hT_ready, late.count(1, 1))
                        wait_unit(act, y_ready, late.before(2))
                        full = (HC - 1) * P
                        nc.scalar.activation(hqT[par][:, 0:full], hT_ps[:, 0:full], ACT.Copy).then_inc(hqT_ready, 1)
                        nc.scalar.activation(hqT[par][0:TAIL, full:full + P], hT_ps[0:TAIL, full:full + P], ACT.Copy
                                             ).then_inc(hqT_ready, 1)
                    if u.live:
                        act.wait_ge(xT_ready, u.count(1, 1))
                        wait_unit(act, h_ready, u.before(2, 2))
                        nc.scalar.activation(xqT[u.o % 2][:], xT_ps[:, 0:C], ACT.Copy).then_inc(xqT_ready, 1)

                pipeline(act, step, ROUNDS, WIDTH, 3, peel=2)

            @block.tensor
            def _(pe):
                nc.tensor.matmul(y_ps[:, 0:8], k["ones"][:], asum[:], start=True, stop=True).then_inc(wsum_ready, 1)
                pe.wait_ge(idb_ready, 1)

                def step(i, o):
                    u, mid, late = (Unit(i, o, WIDTH, ROUNDS, b) for b in (0, 1, 3))
                    if mid.live:
                        if mid.static and mid.n == 0:
                            pe.wait_ge(w_ready, 4)
                        pe.wait_ge(xqT_ready, mid.count(1, 1))
                        for c in range(2):
                            if not (mid.static and mid.n == 0):
                                pe.wait_ge(hm_ready, mid.count(2, c - 1))
                            for ps, w in ((h1_ps, w13q[0]), (h3_ps, w13q[1])):
                                for h in range(KC):
                                    last = nc.tensor.matmul(ps[c][:, 0:HH], xqT[mid.o % 2][:, h * P:(h + 1) * P],
                                                            w[:, h, c * HH:(c + 1) * HH], start=(h == 0),
                                                            stop=(h == KC - 1))
                            last.then_inc(h_ready, 1)
                    if late.live:
                        par = late.o % 2
                        pe.wait_ge(hq_ready, late.count(1, 1))
                        wait_unit(pe, hqT_ready, late.before(1, 2))
                        for a in range(HC):
                            m = min(P, HID - a * P)
                            last = nc.tensor.transpose(hT_ps[0:m, a * P:a * P + P], hq[par][:, a * P:a * P + m],
                                                       identb[:])
                        last.then_inc(hT_ready, 1)
                    if u.live:
                        par = u.o % 2
                        pe.wait_ge(xq_ready, u.count(2, 1))
                        wait_unit(pe, xqT_ready, u.before(1))
                        for h in range(KC):
                            last = nc.tensor.transpose(xT_ps[:, h * P:(h + 1) * P], xq[par][:, h * P:(h + 1) * P],
                                                       identb[:])
                        last.then_inc(xT_ready, 1)
                    if late.live:
                        par = late.o % 2
                        pe.wait_ge(hqT_ready, late.count(2, 2))
                        wait_unit(pe, x_added, late.before(1))
                        for a in range(HC):
                            m = min(P, HID - a * P)
                            last = nc.tensor.matmul(y_ps[:, 0:C], hqT[par][0:m, a * P:a * P + P], w2q[0:m, a, :],
                                                    start=(a == 0), stop=(a == HC - 1))
                        last.then_inc(y_ready, 1)

                pipeline(pe, step, ROUNDS, WIDTH, 3)



def fp8_rounding(chain, nc, y, m, out):
    chain(nc.vector.tensor_scalar(y, y, FP8_MAX, -FP8_MAX, ALU.min, ALU.max))
    chain(nc.vector.tensor_scalar(m.bitcast(U16), y.bitcast(U16), 0x7F80, None, ALU.bitwise_and))
    chain(nc.vector.tensor_scalar(m, m, 2.0 ** -6, 1.5 * 2.0 ** 4, ALU.max, ALU.mult))
    chain(nc.vector.tensor_tensor(y, y, m, ALU.add))
    chain.mark(nc.vector.tensor_tensor(out, y, m, ALU.subtract))


def ln_quant_stage(k, xq8, work):
    nc, sem, x_res, ident, col = k["nc"], k["sem"], k["x_res"], k["ident"], k["col"]
    GT = 4
    NG = NT // GT
    W = GT * P
    with ExitStack() as own:
        def sb(name, shape, dt=F32):
            return own.enter_context(nc.sbuf_tensor(name, shape, dt))

        def z(j):
            per = work[0].shape[1] // C
            return work[j // per][:, j % per * C:(j % per + 1) * C]

        lnT = [sb(f"lnT{i}", [P, KC, W]) for i in range(2)]
        y = [sb(f"lq_y{i}", [P, 4 * KC, W], BF16) for i in range(2)]
        m = sb("lq_m", [P, 4 * KC, W], BF16)
        inv = sb("lq_inv", [P, 4 * KC])
        zT_ps = [own.enter_context(nc.psum_tensor(f"lq_zT_ps{i}", [P, 512], F32)) for i in range(4)]
        var_ready, rs_ready = k["ln_var_ready"], k["ln_rs_ready"]
        inv_ready = sem("lq_inv_ready")
        z_ready, zT_ready, y_ready, xq_ready = sem("lq_z_ready"), sem("lq_zT_ready"), sem("lq_y_ready"), sem("lq_xq_ready")
        lnT_ready = sem("lq_lnT_ready")

        with nc.Block() as block:
            @block.vector
            def _(dve):
                chain = k["dve_chain"].on(dve)
                nc.vector.reciprocal(inv[:], col("sq", 0, 4 * KC)).then_inc(inv_ready, 1)
                for j in range(NT):
                    chain.mark(nc.vector.bn_stats(k["stat6"][:, j, :], x_res[:, j, :]))
                chain.settle()
                dve_mean_var(k, chain, var_ready)
                dve.wait_ge(rs_ready, LN_BEFORE["quant"] + 1)
                dve.wait_ge(var_ready, LN_BEFORE["quant"] + 1)
                rsqrt_newton(chain, nc, k["rstd"][:], k["rs0"][:], k["var"][:], k["st"][0][:])
                chain(nc.vector.tensor_tensor(k["st"][0][:], k["rstd"][:], k["rstd"][:], ALU.mult))
                chain(nc.vector.tensor_tensor(k["st"][0][:], k["st"][0][:], k["var0"][:], ALU.mult))
                nc.vector.tensor_scalar(k["var"][:], k["st"][0][:], LN_EPS, None, ALU.add).then_inc(var_ready, 1)
                dve.wait_ge(rs_ready, LN_BEFORE["quant"] + 2)
                dve.wait_ge(var_ready, LN_BEFORE["quant"] + 2)
                rsqrt_newton(chain, nc, k["st"][1][:], k["rs0"][:], k["var"][:], k["st"][0][:])
                chain(nc.vector.tensor_tensor(k["rstd"][:], k["rstd"][:], k["st"][1][:], ALU.mult))
                for j in range(NT):
                    nc.vector.tensor_scalar(z(j), x_res[:, j, :], k["mean"][:, j:j + 1],
                                            k["rstd"][:, j:j + 1], ALU.subtract, ALU.mult).then_inc(z_ready, 1)
                for g in range(NG):
                    dve.wait_ge(y_ready, 8 * g + 8)
                    fp8_rounding(chain, nc, y[g % 2][:], m[:], xq8[:, :, g * W:(g + 1) * W])
                    chain.settle()
                    nc.vector.memset(k["st"][1][:, 0:1], 0.0).then_inc(xq_ready, 1)

            @block.tensor
            def _(pe):
                for n in range(NG * KC):
                    g, h = divmod(n, KC)
                    pe.wait_ge(z_ready, GT * g + GT)
                    if n >= 4:
                        pe.wait_ge(lnT_ready, n - 3)
                    for j in range(GT):
                        last = nc.tensor.transpose(zT_ps[n % 4][:, j * P:(j + 1) * P],
                                                   z(GT * g + j)[:, h * P:(h + 1) * P], ident[:])
                    last.then_inc(zT_ready, 1)

            @block.scalar
            def _(act):
                chain = k["act_chain"].on(act)
                nc.scalar.preload_act_table_set(LN_EXP_SET)
                for r in range(2):
                    act_rsqrt(act, nc, k["rs0"][:], k["var"][:], k["st"][2][:], var_ready,
                              LN_BEFORE["quant"] + r + 1, chain, rs_ready)
                act.wait_ge(inv_ready, 1)
                for g in range(NG):
                    for h in range(KC):
                        n = g * KC + h
                        act.wait_ge(zT_ready, n + 1)
                        nc.scalar.activation(lnT[g % 2][:, h, :], zT_ps[n % 4][:], ACT.Identity, scale=col("ln_w", h),
                                             bias=col("ln_b", h)).then_inc(lnT_ready, 1)
                    act.wait_ge(lnT_ready, KC * (g + 1))
                    if g >= 2:
                        act.wait_ge(xq_ready, g - 1)
                    for q in range(4):
                        for h in range(KC):
                            a = q * KC + h
                            nc.scalar.activation(y[g % 2][:, a, :], lnT[g % 2][:, h, :], ACT.Copy,
                                                 scale=inv[:, a:a + 1]).then_inc(y_ready, 1)



def attention_stage(k, kind, xq8, aw, work, chunks, ctxT):
    nc, sem, x_res, ident, col = k["nc"], k["sem"], k["x_res"], k["ident"], k["col"]
    own_kv = kind == "self"
    name = kind[0]
    GU = 2
    HU = GU * HPG
    UT = G // GU
    WIDTH = 2 * UT
    ROUNDS = NT // 2
    QW, KW = HU * D, GU * D
    NQ = 3 if own_kv else 1
    Q0 = 0 if own_kv else 3
    scale = float(D) ** -0.5
    pre = "" if own_kv else "x"
    with ExitStack() as own:
        def sb(nm, shape, dt=F32):
            return own.enter_context(nc.sbuf_tensor(f"{name}_{nm}", shape, dt))

        def psum(nm, shape, dt=F32):
            return own.enter_context(nc.psum_tensor(f"{name}_{nm}", shape, dt))

        def sg(nm):
            return sem(f"{name}_{nm}")

        wq, wk, wv, wp = (aw[n] for n in "qkvp")
        if not own_kv:
            ctx_t = [sb(f"ctx{i}", [P, KC, P]) for i in range(2)]
            ctx_p = [[sb(f"ctxp{i}{p}", [P, KC, P], F32R) for p in range(2)] for i in range(2)]
        xqf = [sb(f"xqf{i}", [P, NQ * KC, P], F32R) for i in range(2)]
        lnp = sb("lnp", [P, 2])
        ism = sb("ism", [P, NH])
        pscale = sb("pscale", [P, 1])
        minus_mean = sb("minus_mean", [P, 1])
        sq = sb("sq", [P, QW + KW])
        v6, r6, t6, l6 = (sb(nm, [P, HU + GU]) for nm in ("v6", "r6", "t6", "l6"))
        g6 = sb("g6", [P, HU + GU])
        qn, kn = sb("qn", [P, QW]), sb("kn", [P, KW])
        v_s = [sb(f"v{i}", [P, KW]) for i in range(4)]
        qT, kT = sb("qT", [P, QW]), sb("kT", [P, KW])
        nmax, psum_s, rsum = sb("nmax", [P, 4]), sb("psums", [P, 4]), sb("rsum", [P, 4])
        pe_s, pn = sb("p", [P, 4 * S]), sb("pn", [P, 4 * S])
        pT = sb("pT", [P, GU, HPG, 2, S])
        yb, eb, mb, tb = (sb(nm, [P, QW], BF16) for nm in ("yb", "eb", "mb", "tb"))
        cat = [sb(f"cat{i}", [P, QW], F32R) for i in range(2)]
        q_ps = [psum(f"q_ps{i}", [P, QW]) for i in range(2)]
        kv_ps = [psum(f"kv_ps{i}", [P, 2 * KW]) for i in range(2)]
        qT_ps = psum("qT_ps", [P, QW])
        kT_sc_ps = psum("kT_sc_ps", [P, 512])
        kT_ps, sc_ps = kT_sc_ps[:, 0:KW], kT_sc_ps[:, KW:KW + 4 * S]
        po_ps = psum("po_ps", [P, 512])
        pj_ps = psum("pj_ps", [P, 512])

        prep = k["dve_chain"]
        own_consts = prep.n + 3
        if not own_kv:
            ctx_in, ctx_upper, ctx_ready = [sg(f"ctx_in{i}") for i in range(2)], sg("ctx_upper"), sg("ctx_ready")
        cleared = sg("cleared")
        xqf_ready = sg("xqf_ready")
        q_done, kv_done, tq_done, t_done = sg("q_done"), sg("kv_done"), sg("tq_done"), sg("t_done")
        sqq_ready, sqk_ready, v_ready = sg("sqq_ready"), sg("sqk_ready"), sg("v_ready")
        var_ready, rs_ready = sg("var_ready"), sg("rs_ready")
        qn_ready, kn_ready = sg("qn_ready"), sg("kn_ready")
        qT_ready, kT_ready = sg("qT_ready"), sg("kT_ready")
        sc_done, max_ready, exp_ready = sg("sc_done"), sg("max_ready"), sg("exp_ready")
        rsum_ready, pn_ready = sg("rsum_ready"), sg("pn_ready")
        pt_done, pT_ready, pv_done = sg("pt_done"), sg("pT_ready"), sg("pv_done")
        r_ready, cadd_ready = sg("r_ready"), sg("cadd_ready")
        y_ready, cat_ready, pj_done, x_added = sg("y_ready"), sg("cat_ready"), sg("pj_done"), sg("x_added")
        norm_steps, cat_steps, act_steps = sg("norm_steps"), sg("cat_steps"), sg("act_steps")

        def units(i, o, *backs):
            return [Unit(i, o, WIDTH, ROUNDS, b) for b in backs]

        def tile_of(i, o, back=0):
            return 2 * i + (o - back) // UT

        def q_bank(u):
            return q_ps[u.o % 2]

        def kv_bank(u):
            return kv_ps[u.o % 2]

        with nc.Block() as block:
            @block.sync
            def _(sp):
                if own_kv:
                    load_weights(sp, aw, work, chunks, None, last=3)
                else:
                    cv = ctxT.rearrange("(h p) t -> p h t", p=P)
                    for t in range(2):
                        sp.dma_start(ctx_t[t][:], cv[:, :, t * P:(t + 1) * P]).then_inc(ctx_in[t], 16)
                    load_weights(sp, aw, work, chunks, lambda i: sp.wait_ge(aw["lower_dve"], CROSS_ON_DVE.index(i) + 1)
                                 if i in CROSS_ON_DVE else
                                 sp.wait_ge(aw["lower_pool"], N_CHUNKS + CROSS_ON_POOL.index(i) + 1), first=3)
                    with sp.Fori(1, ROUNDS) as i:
                        for t in range(2):
                            sp.wait_ge(ctx_ready, 2 * i - 1 + t)
                            sp.dma_start(ctx_t[t][:], cv[:, :, bass.ds((2 * i + t) * P, P)]).then_inc(ctx_in[t], 16)

            @block.gpsimd
            def _(pool):
                nc.gpsimd.memset(minus_mean[:], -1.0 / D).then_inc(cleared, 1)
                nc.gpsimd.memset(pT[:], 0.0).then_inc(cleared, 1)
                pool.wait_ge(cleared, 2)

                def convert(t, par, fill):
                    if not own_kv:
                        pool.wait_ge(ctx_in[par], 16 * fill)
                    nc.gpsimd.tensor_copy(xqf[par][:], xq8[:, Q0 * KC:(Q0 + NQ) * KC, bass.ds(t * P, P)]
                                          ).then_inc(xqf_ready, 1)
                    if not own_kv:
                        nc.gpsimd.tensor_copy(ctx_p[par][0][:], ctx_t[par][:]).then_inc(ctx_upper, 1)
                        pool.wait_ge(ctx_upper, t + 1)
                        nc.gpsimd.tensor_tensor(ctx_p[par][1][:], ctx_t[par][:], ctx_p[par][0][:].bitcast(F32),
                                                ALU.subtract).then_inc(ctx_ready, 1)

                convert(0, 0, 1)
                if not own_kv:
                    for i in CROSS_ON_POOL:
                        lower_part(nc.gpsimd, aw, work, chunks, i, N_CHUNKS + i, aw["lower_pool"])

                def step(i, o):
                    u, soft, out8 = units(i, o, 0, 1, 3)
                    if out8.live:
                        pool.wait_ge(cadd_ready, out8.count(1, 1))
                        wait_unit(pool, pj_done, out8.before(2))
                        nc.gpsimd.tensor_tensor(cat[out8.o % 2][:], tb[:], mb[:], ALU.subtract).then_inc(cat_ready, 1)
                    if soft.live:
                        pool.wait_ge(rsum_ready, soft.count(1, 1))
                        pool.wait_ge(exp_ready, soft.count(4, 4))
                        wait_unit(pool, pt_done, soft.before(1))
                        nc.gpsimd.tensor_tensor(
                            pn[:].rearrange("p (a t) -> p a t", a=4), pe_s[:].rearrange("p (a t) -> p a t", a=4),
                            rsum[:].unsqueeze(2).broadcast_to([P, 4, S]), ALU.mult).then_inc(pn_ready, 1)
                    if u.live and o % UT == 0:
                        nxt = tile_of(i, o) + 1
                        if not isinstance(nxt, int) or nxt < NT:
                            wait_unit(pool, kv_done, u.before(1))
                            par = (o // UT + 1) % 2
                            convert(nxt, par, i + 1 if par else i + 2)
                    if own_kv and u.live and o in CrossHead.WITH_UNITS:
                        cross_head_pool(pool, nc, aw, work, minus_mean[:], i, o)

                pipeline(pool, step, ROUNDS, WIDTH, 3, peel_last=True)

            @block.vector
            def _(dve):
                prep.on(dve)
                prep.mark(nc.vector.tensor_scalar(lnp[:], col(f"q{pre}ln_w", 0, 2), scale, None, ALU.mult))
                prep.mark(nc.vector.reciprocal(ism[:], col("smooth", 0 if own_kv else NH, NH)))
                prep.mark(nc.vector.tensor_tensor(pscale[:], col("proj_in"), col("proj_w"), ALU.mult))
                if not own_kv:
                    cross_weights_dve(dve, nc, aw, work, chunks)
                norm, catc = Chain(dve, norm_steps), Chain(dve, cat_steps)

                def step(i, o):
                    u, sm, pv, f8, pj = units(i, o, 0, 1, 2, 3, 4)

                    def norm_guess():
                        norm.at(u.count(3))
                        dve.wait_ge(sqq_ready, u.count(1, 1))
                        dve.wait_ge(sqk_ready, u.count(1, 1))
                        norm(nc.vector.tensor_reduce(v6[:], sq[:].rearrange("p (h d) -> p h d", d=D), AX.X, ALU.add))
                        nc.vector.tensor_scalar(v6[:], v6[:], 1.0 / D, LN_EPS, ALU.mult, ALU.add
                                                ).then_inc(var_ready, 1)

                    def maxima():
                        dve.wait_ge(sc_done, sm.count(1, 1))
                        wait_unit(dve, exp_ready, sm.before(1, 4))
                        nc.vector.tensor_reduce(nmax[:], sc_ps.rearrange("p (a t) -> p a t", a=4), AX.X,
                                                ALU.max, negate=True).then_inc(max_ready, 1)

                    def newton(part):
                        if part == 0:
                            dve.wait_ge(rs_ready, u.count(1, 1))
                            dve.wait_ge(var_ready, u.count(1, 1))
                            norm.mark(nc.vector.scalar_tensor_tensor(t6[:], g6[:], -0.5, g6[:], ALU.mult, ALU.mult))
                        elif part == 1:
                            norm.settle()
                            norm.mark(nc.vector.tensor_tensor(t6[:], t6[:], v6[:], ALU.mult))
                        else:
                            norm.settle()
                            nc.vector.scalar_tensor_tensor(r6[:], t6[:], 1.5, g6[:], ALU.add, ALU.mult
                                                           ).then_inc(r_ready, 1)

                    def round8(part):
                        if part == 0:
                            catc.at(f8.count(3))
                            dve.wait_ge(y_ready, f8.count(1, 1))
                            catc.mark(nc.vector.tensor_scalar(yb[:], yb[:], FP8_MAX, -FP8_MAX, ALU.min, ALU.max))
                        elif part == 1:
                            catc.settle()
                            catc.mark(nc.vector.tensor_scalar(eb[:].bitcast(U16), yb[:].bitcast(U16), 0x7F80, None,
                                                              ALU.bitwise_and))
                        elif part == 2:
                            catc.settle()
                            wait_unit(dve, cat_ready, f8.before(1))
                            catc.mark(nc.vector.tensor_scalar(mb[:], eb[:], 2.0 ** -6, 1.5 * 2.0 ** 4, ALU.max,
                                                              ALU.mult))
                        elif part == 3:
                            catc.settle()
                            nc.vector.tensor_tensor(tb[:], yb[:], mb[:], ALU.add).then_inc(cadd_ready, 1)

                    def normalised():
                        dve.wait_ge(r_ready, u.count(1, 1))
                        wait_unit(dve, t_done, u.before(1))
                        nc.vector.tensor_tensor(qn[:].rearrange("p (h d) -> p h d", d=D),
                                                q_bank(u)[:].rearrange("p (h d) -> p h d", d=D),
                                                r6[:, 0:HU].unsqueeze(2).broadcast_to([P, HU, D]), ALU.mult
                                                ).then_inc(qn_ready, 1)
                        dve.wait_ge(v_ready, u.count(1, 1))
                        nc.vector.tensor_tensor(kn[:].rearrange("p (h d) -> p h d", d=D),
                                                kv_bank(u)[:, 0:KW].rearrange("p (h d) -> p h d", d=D),
                                                r6[:, HU:HU + GU].unsqueeze(2).broadcast_to([P, GU, D]), ALU.mult
                                                ).then_inc(kn_ready, 1)

                    if u.live:
                        norm_guess()
                    for part in range(3):
                        if f8.live:
                            round8(part)
                        if u.live:
                            newton(part)
                    if pj.live and pj.o % UT == UT - 1:
                        dve.wait_ge(pj_done, pj.count(1, 1))
                        xt = x_res[:, bass.ds(tile_of(i, o, 4), 1), :].rearrange("p a c -> p (a c)")
                        nc.vector.scalar_tensor_tensor(xt, pj_ps[:, 0:C], pscale[:], xt, ALU.mult, ALU.add
                                                       ).then_inc(x_added, 1)
                        if not own_kv:
                            dve.wait_ge(x_added, tile_of(i, o, 4) + 1)
                            nc.vector.bn_stats(k["stat6"][:, bass.ds(tile_of(i, o, 4), 1), :].rearrange(
                                "p a c -> p (a c)"), xt)
                    if sm.live:
                        maxima()
                    if f8.live:
                        round8(3)
                    if u.live:
                        normalised()
                    if sm.live:
                        dve.wait_ge(exp_ready, sm.count(4, 4))
                        wait_unit(dve, pn_ready, sm.before(1))
                        nc.vector.reciprocal(rsum[:], psum_s[:]).then_inc(rsum_ready, 1)
                    if pv.live:
                        dve.wait_ge(pv_done, pv.count(1, 1))
                        wait_unit(dve, cadd_ready, pv.before(1))
                        first_head = (pv.o % UT) * HU
                        nc.vector.tensor_tensor(yb[:].rearrange("p (h t) -> p h t", h=HU),
                                                po_ps[:].rearrange("p (h t) -> p h t", h=HU),
                                                ism[:, first_head:first_head + HU].unsqueeze(2).broadcast_to([P, HU, P]),
                                                ALU.mult).then_inc(y_ready, 1)

                pipeline(dve, step, ROUNDS, WIDTH, 4)

            @block.scalar
            def _(act):
                nc.scalar.preload_act_table_set(LN_EXP_SET)
                if not own_kv:
                    cross_weights_act(act, nc, aw, work, chunks)
                act.wait_ge(prep.sem, own_consts)
                act.wait_ge(cleared, 2)
                chain = Chain(act, act_steps)

                def step(i, o):
                    u, sm, pv = units(i, o, 0, 1, 2)
                    if u.live:
                        act.wait_ge(q_done, u.count(1, 1))
                        wait_unit(act, var_ready, u.before(1))
                        nc.scalar.activation(sq[:, 0:QW], q_bank(u)[:], ACT.Square).then_inc(sqq_ready, 1)
                        act.wait_ge(kv_done, u.count(1, 1))
                        nc.scalar.activation(sq[:, QW:QW + KW], kv_bank(u)[:, 0:KW], ACT.Square).then_inc(sqk_ready, 1)
                        wait_unit(act, pv_done, u.before(4))
                        nc.scalar.activation(v_s[u.o % 4][:], kv_bank(u)[:, KW:2 * KW], ACT.Copy).then_inc(v_ready, 1)
                    if sm.live:
                        act.wait_ge(tq_done, sm.count(1, 1))
                        nc.scalar.activation(qT[:], qT_ps[:], ACT.Identity, scale=lnp[:, 0:1], bias=lnp[:, 1:2]
                                             ).then_inc(qT_ready, 1)
                        act.wait_ge(t_done, sm.count(1, 1))
                        nc.scalar.activation(kT[:], kT_ps, ACT.Identity, scale=col(f"k{pre}ln_w"),
                                             bias=col(f"k{pre}ln_b")).then_inc(kT_ready, 1)
                    if u.live:
                        chain.at(u.count(1))
                        act.wait_ge(var_ready, u.count(1, 1))
                        chain(nc.scalar.activation(l6[:], v6[:], ACT.Ln))
                        wait_unit(act, r_ready, u.before(1))
                        nc.scalar.activation(g6[:], l6[:], ACT.Exp, scale=-0.5).then_inc(rs_ready, 1)
                    if pv.live:
                        act.wait_ge(pt_done, pv.count(1, 1))
                        for b in range(2):
                            rows = slice(b * S, (b + 1) * S)
                            nc.scalar.activation(pT[rows, :, :, b, :], po_ps[rows, 0:GU * P].rearrange(
                                "p (g h s) -> p g h s", g=GU, h=HPG), ACT.Copy).then_inc(pT_ready, 1)
                    if own_kv and u.live and o in CrossHead.WITH_UNITS:
                        cross_head_act(act, nc, aw, work, chunks, i, o)
                    if sm.live:
                        act.wait_ge(max_ready, sm.count(1, 1))
                        wait_unit(act, pn_ready, sm.before(1))
                        wait_unit(act, rsum_ready, sm.before(1))
                        for a in range(4):
                            nc.scalar.activation(pe_s[:, a * S:(a + 1) * S], sc_ps[:, a * S:(a + 1) * S], ACT.Exp,
                                                 bias=nmax[:, a:a + 1], accum_out=psum_s[:, a:a + 1]
                                                 ).then_inc(exp_ready, 1)

                pipeline(act, step, ROUNDS, WIDTH, 2)

            @block.tensor
            def _(pe):
                if not own_kv:
                    pe.wait_ge(aw["lower_dve"], len(CROSS_ON_DVE))
                    pe.wait_ge(aw["lower_pool"], N_CHUNKS + 1)

                def split_product(out_ap, x_col, w_pair, c0, c1):
                    n = 0
                    for h in range(KC):
                        for part in range(2):
                            last = nc.tensor.matmul(out_ap, x_col(h), w_pair[part][:, h, c0:c1], start=(n == 0),
                                                    stop=(n == 2 * KC - 1))
                            n += 1
                    return last

                def step(i, o):
                    u, kv_u, t, pv, pj = units(i, o, 0, 1, 2, 3, 5)
                    if kv_u.live:
                        gp, tp = kv_u.o % UT, (kv_u.o // UT) % 2
                        wait_unit(pe, kn_ready, kv_u.before(2))
                        kv = kv_bank(kv_u)
                        if own_kv:
                            split_product(kv[:, 0:KW], lambda h: xqf[tp][:, KC + h, :], wk, gp * KW, (gp + 1) * KW)
                            last = split_product(kv[:, KW:2 * KW], lambda h: xqf[tp][:, 2 * KC + h, :], wv,
                                                 gp * KW, (gp + 1) * KW)
                        else:
                            if gp == 0:
                                pe.wait_ge(ctx_ready, tile_of(i, o, 1) + 1)
                            cols = slice(gp * KW, (gp + 1) * KW)
                            for c, w in ((0, wk), (KW, wv)):
                                n = 0
                                for h in range(KC):
                                    for xp, wpart in ((0, 0), (0, 1), (1, 0)):
                                        last = nc.tensor.matmul(kv[:, c:c + KW], ctx_p[tp][xp][:, h, :],
                                                                w[wpart][:, h, cols], start=(n == 0),
                                                                stop=(n == 3 * KC - 1))
                                        n += 1
                        last.then_inc(kv_done, 1)
                    if t.live:
                        pe.wait_ge(qn_ready, t.count(1, 1))
                        wait_unit(pe, qT_ready, t.before(1))
                        for a in range(HU):
                            g, h = divmod(a, HPG)
                            qcols = qT_ps[:].rearrange("p (g b h s) -> p g b h s", g=GU, b=2, h=HPG)[:, g, :, h, :]
                            last = nc.tensor.transpose(qcols, qn[:, a * P:(a + 1) * P], ident[:])
                        last.then_inc(tq_done, 1)
                        pe.wait_ge(kn_ready, t.count(1, 1))
                        wait_unit(pe, kT_ready, t.before(1))
                        wait_unit(pe, exp_ready, t.before(1, 4))
                        for a in range(GU):
                            last = nc.tensor.transpose(kT_ps[:, a * P:(a + 1) * P], kn[:, a * P:(a + 1) * P], ident[:])
                        last.then_inc(t_done, 1)
                    if pj.live:
                        gpj = pj.o % UT
                        if not own_kv and pj.static and pj.n == 0:
                            pe.wait_ge(aw["lower_pool"], N_CHUNKS + len(CROSS_ON_POOL))
                        pe.wait_ge(cat_ready, pj.count(1, 1))
                        if gpj == 0 and not (pj.static and pj.n < UT):
                            pe.wait_ge(x_added, tile_of(i, o, 5))
                        for a in range(HU):
                            for part in range(2):
                                last = nc.tensor.matmul(pj_ps[:, 0:C], cat[pj.o % 2][:, a * P:(a + 1) * P],
                                                        wp[part][:, gpj * HU + a, :],
                                                        start=(gpj == 0 and a == 0 and part == 0),
                                                        stop=(gpj == UT - 1 and a == HU - 1 and part == 1))
                        last.then_inc(pj_done, 1)
                    if pv.live:
                        pe.wait_ge(pn_ready, pv.count(1, 1))
                        wait_unit(pe, y_ready, pv.before(1))
                        for g in range(GU):
                            last = nc.tensor.transpose(po_ps[:, g * P:(g + 1) * P], pn[:, g * P:(g + 1) * P], ident[:])
                        last.then_inc(pt_done, 1)
                    if u.live:
                        gp, tp = u.o % UT, (u.o // UT) % 2
                        if gp == 0:
                            pe.wait_ge(xqf_ready, tile_of(i, o) + 1)
                        wait_unit(pe, qn_ready, u.before(2))
                        split_product(q_bank(u)[:], lambda h: xqf[tp][:, h, :], wq, gp * QW, (gp + 1) * QW
                                      ).then_inc(q_done, 1)
                    if t.live:
                        pe.wait_ge(qT_ready, t.count(1, 1))
                        pe.wait_ge(kT_ready, t.count(1, 1))
                        for g in range(GU):
                            for b in range(2):
                                a = g * 2 + b
                                last = nc.tensor.matmul(sc_ps[:, a * S:(a + 1) * S], qT[:, a * P:(a + 1) * P],
                                                        kT[:, g * P + b * S:g * P + (b + 1) * S], start=True, stop=True)
                        last.then_inc(sc_done, 1)
                    if pv.live:
                        pe.wait_ge(pT_ready, pv.count(2, 2))
                        for g in range(GU):
                            last = nc.tensor.matmul(po_ps[:, g * HPG * P:(g + 1) * HPG * P],
                                                    v_s[pv.o % 4][:, g * D:(g + 1) * D],
                                                    pT[:, g].rearrange("p h b s -> p (h b s)"), start=True, stop=True)
                        last.then_inc(pv_done, 1)

                pipeline(pe, step, ROUNDS, WIDTH, 5)



def routed_ffn_stage(k, routerT, fw1T, fw2T, fb2, out):
    nc, sem, x_res, ident, col = k["nc"], k["sem"], k["x_res"], k["ident"], k["col"]
    GT = 4
    NG = NT // GT
    W = GT * P
    FC = FF // P
    N2 = 2 * NT
    with ExitStack() as own:
        def sb(name, shape, dt=F32):
            return own.enter_context(nc.sbuf_tensor(name, shape, dt))

        def psum(name, shape, dt=F32):
            return own.enter_context(nc.psum_tensor(name, shape, dt))

        z = sb("rf_z", [P, NT, C])
        zT = [sb(f"rf_zT{i}", [P, KC, W]) for i in range(2)]
        zTp = [sb(f"rf_zTp{p}", [P, KC, TOK], F32R) for p in range(2)]
        w1p = [sb(f"rf_w1p{p}", [P, KC * FF], F32R) for p in range(2)]
        w2p = [sb(f"rf_w2p{p}", [P, FC * C], F32R) for p in range(2)]
        rw = sb("rf_rw", [P, KC, E])
        lgT = [sb(f"rf_lgT{i}", [P, W]) for i in range(2)]
        raw = [sb(f"rf_raw{i}", [P, KC * FF]) for i in range(2)]
        lgT_ready, lgTs_ready = sem("rf_lgT_ready"), sem("rf_lgTs_ready")
        b2 = sb("rf_b2", [P, C])
        tri = sb("rf_tri", [P, P])
        iota8 = sb("rf_iota8", [P, NT, E])
        first = sb("rf_first", [P, E, N2])
        pr, tmp = sb("rf_pr", [P, NT, E]), sb("rf_tmp", [P, NT, E])
        oh = sb("rf_oh", [P, N2, E])
        top = sb("rf_top", [P, N2])
        low = sb("rf_low", [P, NT])
        tot, acc = sb("rf_tot", [P, E, N2]), sb("rf_acc", [P, E, N2])
        cnt = sb("rf_cnt", [P, N2, E])
        pos = sb("rf_pos", [P, N2])
        gate = sb("rf_gate", [P, NT])
        h_s = [sb(f"rf_h{i}", [P, W]) for i in range(3)]
        hT = [[sb(f"rf_hT{i}{p}", [P, FC, W], F32R) for p in range(2)] for i in range(2)]
        t_s = sb("rf_t", [P, C])
        zT_ps = [psum(f"rf_zT_ps{i}", [P, 512]) for i in range(2)]
        h_ps = [psum(f"rf_h_ps{i}", [P, 512]) for i in range(3)]
        y_ps = [psum(f"rf_y_ps{i}", [P, 512]) for i in range(2)]
        lg_ps = psum("rf_lg_ps", [P, 512])

        w_in, b2_in, rw_in = [sem(f"rf_w_in{i}") for i in range(2)], sem("rf_b2_in"), sem("rf_rw_in")
        wup_ready, wlow_ready = sem("rf_wup_ready"), sem("rf_wlow_ready")
        zlow_ready, gelu_ready = sem("rf_zlow_ready"), sem("rf_gelu_ready")
        consts = sem("rf_consts")
        var_ready, rs_ready = k["ln_var_ready"], k["ln_rs_ready"]
        z_ready, zTp_ready, zT_ready = sem("rf_z_ready"), sem("rf_zTp_ready"), sem("rf_zT_ready")
        lg_ready, sub_ready, exp_ready = sem("rf_lg_ready"), sem("rf_sub_ready"), sem("rf_exp_ready")
        oh_ready, cnt_ready = sem("rf_oh_ready"), sem("rf_cnt_ready")
        h_ready, hT_ready, y_ready, x_added = sem("rf_h_ready"), sem("rf_hT_ready"), sem("rf_y_ready"), sem("rf_x_added")
        out_done = sem("out_done")

        with nc.Block() as block:
            @block.sync
            def _(sp):
                sp.dma_start(rw[:], routerT.rearrange("(h p) n -> p h n", p=P)).then_inc(rw_in, 16)
                for i, w in enumerate((fw1T, fw2T)):
                    src = w.rearrange("(h p) n -> p h n", p=P)
                    sp.dma_start(raw[i][:].rearrange("p (h n) -> p h n", h=src.shape[1]), src).then_inc(w_in[i], 16)
                sp.dma_start(b2[:], fb2.broadcast_to([P, C])).then_inc(b2_in, 16)
                outr = out.rearrange("(j p) c -> p j c", p=P)
                for j in range(0, NT, 2):
                    sp.wait_ge(x_added, j + 2)
                    sp.dma_start(outr[:, j:j + 2, :], x_res[:, j:j + 2, :]).then_inc(out_done, 16)
                sp.wait_ge(out_done, 16 * (NT // 2))

            @block.gpsimd
            def _(pool):
                nc.gpsimd.memset(tri[:], 1.0).then_inc(consts, 1)
                nc.gpsimd.memset(first[:], 1.0).then_inc(consts, 1)
                for e in range(E):
                    nc.gpsimd.memset(iota8[:, :, e], float(e - E)).then_inc(consts, 1)
                pool.wait_ge(consts, 2 + E)
                nc.gpsimd.affine_select(out=tri[:], in_=tri[:], compare_op=ALU.is_ge, fill=0.0, base=0,
                                        pattern=[[1, P]], channel_multiplier=-1).then_inc(consts, 1)
                nc.gpsimd.memset(first[:, :, 0], 0.0).then_inc(consts, 1)
                for i, parts in enumerate((w1p, w2p)):
                    pool.wait_ge(wup_ready, i + 1)
                    nc.gpsimd.tensor_tensor(parts[1][:], raw[i][:], parts[0][:].bitcast(F32), ALU.subtract
                                            ).then_inc(wlow_ready, 1)
                for n in range(NG * FC):
                    g, f = divmod(n, FC)
                    pool.wait_ge(gelu_ready, 2 * n + 2)
                    if g >= 2:
                        pool.wait_ge(y_ready, GT * (g - 1))
                    nc.gpsimd.tensor_tensor(hT[g % 2][1][:, f, :], h_s[n % 3][:], hT[g % 2][0][:, f, :].bitcast(F32),
                                            ALU.subtract).then_inc(hT_ready, 1)

            @block.vector
            def _(dve):
                chain = k["dve_chain"].on(dve)
                dve_mean_var(k, chain, var_ready)
                dve.wait_ge(rs_ready, LN_BEFORE["routed"] + 1)
                dve.wait_ge(var_ready, LN_BEFORE["routed"] + 1)
                rsqrt_newton(chain, nc, k["rstd"][:], k["rs0"][:], k["var"][:], k["st"][0][:])
                for j in range(NT):
                    nc.vector.tensor_scalar(z[:, j, :], x_res[:, j, :], k["mean"][:, j:j + 1],
                                            k["rstd"][:, j:j + 1], ALU.subtract, ALU.mult).then_inc(z_ready, 1)

                for n in range(NG * KC):
                    g, h = divmod(n, KC)
                    dve.wait_ge(zT_ready, 2 * n + 2)
                    cols = slice(g * W, (g + 1) * W)
                    nc.vector.tensor_tensor(zTp[1][:, h, cols], zT[g % 2][:, h, :], zTp[0][:, h, cols].bitcast(F32),
                                            ALU.subtract).then_inc(zlow_ready, 1)

                def wide(v):
                    return v.unsqueeze(2).broadcast_to([P, NT, E])

                dve.wait_ge(lg_ready, NG)
                lg = lg_ps[:, 0:NT * E].rearrange("p (j e) -> p j e", e=E)
                chain(nc.vector.tensor_reduce(low[:], lg, AX.X, ALU.max))
                nc.vector.tensor_tensor(tmp[:], lg, wide(low[:]), ALU.subtract).then_inc(sub_ready, 1)
                dve.wait_ge(exp_ready, 1)
                chain(nc.vector.tensor_reduce(low[:], pr[:], AX.X, ALU.add))
                chain(nc.vector.reciprocal(low[:], low[:]))
                chain(nc.vector.tensor_tensor(pr[:], pr[:], wide(low[:]), ALU.mult))
                dve.wait_ge(consts, 4 + E)
                for c in range(2):
                    best = top[:, c * NT:(c + 1) * NT]
                    one = oh[:, c * NT:(c + 1) * NT, :]
                    chain(nc.vector.tensor_reduce(best, pr[:], AX.X, ALU.max))
                    chain(nc.vector.tensor_tensor(tmp[:], pr[:], wide(best), ALU.is_equal))
                    chain(nc.vector.tensor_tensor(tmp[:], tmp[:], iota8[:], ALU.mult))
                    chain(nc.vector.tensor_reduce(low[:], tmp[:], AX.X, ALU.min))
                    nc.vector.tensor_tensor(one, iota8[:], wide(low[:]), ALU.is_equal).then_inc(oh_ready, 1)
                    dve.wait_ge(oh_ready, c + 1)
                    if c == 0:
                        chain(nc.vector.scalar_tensor_tensor(pr[:], one, -2.0, pr[:], ALU.mult, ALU.add))
                dve.wait_ge(cnt_ready, 2)
                inside = zT_ps[0][:, 0:N2 * E].rearrange("p (n e) -> p n e", e=E)
                totals = zT_ps[1][:, 0:N2 * E].rearrange("p (n e) -> p e n", e=E)
                chain(nc.vector.tensor_copy(tot[:], totals))
                chain(nc.vector.tensor_tensor_scan(acc[:].rearrange("p e n -> p (e n)"),
                                                   first[:].rearrange("p e n -> p (e n)"),
                                                   tot[:].rearrange("p e n -> p (e n)"), 0.0, ALU.mult, ALU.add))
                chain(nc.vector.tensor_tensor(acc[:], acc[:], tot[:], ALU.subtract))
                chain(nc.vector.tensor_tensor(cnt[:], inside, acc[:].rearrange("p e n -> p n e"), ALU.add))
                chain(nc.vector.tensor_tensor(cnt[:], cnt[:], oh[:], ALU.mult))
                chain(nc.vector.tensor_reduce(pos[:], cnt[:], AX.X, ALU.add))
                chain(nc.vector.tensor_scalar(pos[:], pos[:], float(CAP), None, ALU.is_le))
                chain(nc.vector.tensor_tensor(pos[:], pos[:], top[:], ALU.mult))
                chain(nc.vector.tensor_tensor(gate[:], pos[:, 0:NT], pos[:, NT:N2], ALU.add))
                dve.wait_ge(b2_in, 16)
                for j in range(NT):
                    dve.wait_ge(y_ready, j + 1)
                    if j:
                        dve.wait_ge(x_added, j)
                    chain(nc.vector.tensor_tensor(t_s[:], y_ps[j % 2][:, 0:C], b2[:], ALU.add))
                    nc.vector.scalar_tensor_tensor(x_res[:, j, :], t_s[:], gate[:, j:j + 1], x_res[:, j, :],
                                                   ALU.mult, ALU.add).then_inc(x_added, 1)

            @block.scalar
            def _(act):
                chain = k["act_chain"].on(act)
                nc.scalar.preload_act_table_set(LN_EXP_SET)
                act_rsqrt(act, nc, k["rs0"][:], k["var"][:], k["st"][2][:], var_ready, LN_BEFORE["routed"] + 1,
                          chain, rs_ready)
                def weight_upper(i):
                    act.wait_ge(w_in[i], 16)
                    nc.scalar.activation((w1p, w2p)[i][0][:], raw[i][:], ACT.Copy).then_inc(wup_ready, 1)

                def logits_out(g):
                    act.wait_ge(lgT_ready, g + 1)
                    if g >= 2:
                        act.wait_ge(lg_ready, g - 1)
                    nc.scalar.activation(lgT[g % 2][0:E, :], y_ps[g % 2][0:E, :], ACT.Copy).then_inc(lgTs_ready, 1)

                weight_upper(0)
                for n in range(NG * KC):
                    g, h = divmod(n, KC)
                    act.wait_ge(zTp_ready, n + 1)
                    if g >= 2:
                        act.wait_ge(lgT_ready, g - 1)
                        act.wait_ge(zlow_ready, KC * (g - 1))
                    nc.scalar.activation(zT[g % 2][:, h, :], zT_ps[n % 2][:], ACT.Copy).then_inc(zT_ready, 1)
                    act.wait_ge(zT_ready, 2 * n + 1)
                    nc.scalar.activation(zTp[0][:, h, g * W:(g + 1) * W], zT[g % 2][:, h, :], ACT.Copy
                                         ).then_inc(zT_ready, 1)
                    if h == KC - 1 and g:
                        logits_out(g - 1)
                logits_out(NG - 1)
                weight_upper(1)
                act.wait_ge(sub_ready, 1)
                nc.scalar.activation(pr[:], tmp[:], ACT.Exp).then_inc(exp_ready, 1)
                for n in range(NG * FC):
                    g, f = divmod(n, FC)
                    act.wait_ge(h_ready, n + 1)
                    if n >= 3:
                        act.wait_ge(hT_ready, n - 2)
                    nc.scalar.activation(h_s[n % 3][:], h_ps[n % 3][:], ACT.Gelu, bias=col("b1", f)
                                         ).then_inc(gelu_ready, 1)
                    if g >= 2:
                        act.wait_ge(y_ready, GT * (g - 1))
                    act.wait_ge(gelu_ready, 2 * n + 1)
                    nc.scalar.activation(hT[g % 2][0][:, f, :], h_s[n % 3][:], ACT.Copy).then_inc(gelu_ready, 1)

            @block.tensor
            def _(pe):
                def transposes(g):
                    for h in range(KC):
                        n = g * KC + h
                        pe.wait_ge(z_ready, GT * (g + 1))
                        if n >= 2:
                            pe.wait_ge(zT_ready, 2 * n - 3)
                        for j in range(GT):
                            last = nc.tensor.transpose(zT_ps[n % 2][:, j * P:(j + 1) * P],
                                                       z[:, GT * g + j, h * P:(h + 1) * P], ident[:])
                        last.then_inc(zTp_ready, 1)

                def logits(g):
                    pe.wait_ge(zT_ready, 2 * KC * (g + 1) - 1)
                    if g >= 2:
                        pe.wait_ge(lgTs_ready, g - 1)
                    for h in range(KC):
                        last = nc.tensor.matmul(y_ps[g % 2][0:E, :], rw[:, h, :], zT[g % 2][:, h, :],
                                                start=(h == 0), stop=(h == KC - 1))
                    last.then_inc(lgT_ready, 1)

                def logits_back(g):
                    pe.wait_ge(lgTs_ready, g + 1)
                    for j in range(GT):
                        n = GT * g + j
                        last = nc.tensor.transpose(lg_ps[:, n * E:(n + 1) * E], lgT[g % 2][0:E, j * P:(j + 1) * P],
                                                   ident[0:E, 0:E])
                    last.then_inc(lg_ready, 1)

                PARTS = ((0, 0), (0, 1), (1, 0))

                def first_product(g, chunks=range(FC)):
                    pe.wait_ge(zlow_ready, KC * (g + 1))
                    for f in chunks:
                        n = g * FC + f
                        if n >= 3:
                            pe.wait_ge(gelu_ready, 2 * n - 5)
                        for h in range(KC):
                            for a, b in PARTS:
                                c0 = h * FF + f * P
                                last = nc.tensor.matmul(h_ps[n % 3][:], w1p[a][:, c0:c0 + P],
                                                        zTp[b][:, h, g * W:(g + 1) * W],
                                                        start=(h == 0 and (a, b) == PARTS[0]),
                                                        stop=(h == KC - 1 and (a, b) == PARTS[-1]))
                        last.then_inc(h_ready, 1)

                def counts():
                    pe.wait_ge(consts, 4 + E)
                    pe.wait_ge(oh_ready, 2)
                    ohf = oh[:].rearrange("p n e -> p (n e)")
                    nc.tensor.matmul(zT_ps[0][:, 0:N2 * E], tri[:], ohf, start=True, stop=True).then_inc(cnt_ready, 1)
                    nc.tensor.matmul(zT_ps[1][:, 0:N2 * E], k["ones"][:], ohf, start=True, stop=True
                                     ).then_inc(cnt_ready, 1)

                def second_product(g):
                    pe.wait_ge(hT_ready, FC * (g + 1))
                    for j in range(GT):
                        n = GT * g + j
                        if n >= 2:
                            pe.wait_ge(x_added, n - 1)
                        for f in range(FC):
                            for a, b in PARTS:
                                last = nc.tensor.matmul(y_ps[n % 2][:, 0:C], hT[g % 2][a][:, f, j * P:(j + 1) * P],
                                                        w2p[b][:, f * C:(f + 1) * C],
                                                        start=(f == 0 and (a, b) == PARTS[0]),
                                                        stop=(f == FC - 1 and (a, b) == PARTS[-1]))
                        last.then_inc(y_ready, 1)

                transposes(0)
                pe.wait_ge(rw_in, 16)
                for g in range(NG):
                    if g + 1 < NG:
                        transposes(g + 1)
                    logits(g)
                    if g:
                        logits_back(g - 1)
                        if g == 1:
                            pe.wait_ge(wlow_ready, 1)
                        first_product(0, [g - 1])
                logits_back(NG - 1)
                first_product(0, range(NG - 1, FC))
                for g in range(NG):
                    if g + 1 < NG:
                        first_product(g + 1)
                    if g == 0:
                        counts()
                        pe.wait_ge(wlow_ready, 2)
                    second_product(g)



def kernel(**inputs):
    import numpy as np
    import concourse.bacc as bacc
    from concourse.bass_utils import run_bass_kernel_spmd

    def get(name):
        return np.asarray(inputs[name])

    def columns(v, n):
        return v.reshape(n, P).T

    def everywhere(v):
        return np.broadcast_to(v.reshape(1, 1), (P, 1))

    packed = {
        "w": columns(get("L0_xattn_w"), KC), "u": columns(get("L0_xattn_u"), KC),
        "ln_w": columns(get("L1_xattn_ln_w"), KC), "ln_b": columns(get("L1_xattn_ln_b"), KC),
        "sq": columns(get("L1_xattn_q_in_scale"), KC), "sk": columns(get("L1_xattn_k_in_scale"), KC),
        "sv": columns(get("L1_xattn_v_in_scale"), KC), "sqx": columns(get("L1_xattn_qx_in_scale"), KC),
        "smooth": columns(get("L1_xattn_proj_smooth"), 2 * NH), "b1": columns(get("L1_ffn_b1"), FF // P),
        "wq_s": everywhere(get("L1_xattn_wq_scale")), "wk_s": everywhere(get("L1_xattn_wk_scale")),
        "wv_s": everywhere(get("L1_xattn_wv_scale")), "wqx_s": everywhere(get("L1_xattn_wqx_scale")),
        "proj_in": everywhere(get("L1_xattn_proj_in_scale")), "proj_w": everywhere(get("L1_xattn_proj_w_scale")),
    }
    for name in ("qln_w", "qln_b", "kln_w", "kln_b", "qxln_w", "qxln_b", "kxln_w", "kxln_b"):
        packed[name] = columns(get(f"L1_xattn_{name}"), 1)
    arrays = {
        "x": get("x").reshape(TOK, C),
        "ctxT": get("ctx_2048").reshape(TOK, C).T,
        "params": np.concatenate([packed[name] for name in PARAM_COLS], axis=1),
        "w1T": get("L0_ffn_w1").T, "w3T": get("L0_ffn_w3").T, "w2T": get("L0_ffn_w2").T,
        "wqT": get("L1_xattn_wq").T, "wkT": get("L1_xattn_wk").T, "wvT": get("L1_xattn_wv").T,
        "wqxT": get("L1_xattn_wqx").T, "wkvxT": get("L1_xattn_w_kv_x").T, "wprojT": get("L1_xattn_wproj").T,
        "routerT": get("L1_ffn_router_w").T, "fw1T": get("L1_ffn_w1").T, "fw2T": get("L1_ffn_w2").T,
        "fb2": get("L1_ffn_b2").reshape(1, C),
    }
    nc = bacc.Bacc("TRN2", target_bir_lowering=False, num_devices=1)
    args, feed = [], {}
    for name, a in arrays.items():
        a = np.ascontiguousarray(a)
        feed[f"in_{name}"] = a
        args.append(nc.dram_tensor(f"in_{name}", a.shape, mybir.dt.from_np(a.dtype), kind="ExternalInput").ap())
    args.append(nc.dram_tensor("out_x", (TOK, C), F32, kind="ExternalOutput").ap())
    build_program(nc, *args)
    r = run_bass_kernel_spmd(nc, [feed], core_ids=[0])
    return r.results[0]["out_x"].reshape(B, S, C)
```
